# Optimizing a Trainium2 kernel written in Bass

```python
import numpy as np
import jax
import jax.numpy as jnp

def _softmax(x, axis=-1):
    return jax.nn.softmax(x, axis=axis)

def _gelu(x):
    return jax.nn.gelu(x, approximate=True)

def _silu(x):
    return jax.nn.silu(x)

def _sigmoid(x):
    return jax.nn.sigmoid(x)

def _layernorm(x, axis=-1, eps=1e-05):
    m = jnp.mean(x, axis=axis, keepdims=True)
    v = jnp.var(x, axis=axis, keepdims=True)
    return (x - m) / jnp.sqrt(v + eps)

def _scatter_add(tgt, idx, src, axis=0):
    return tgt.at[idx].add(src)

def _segment_sum(src, seg, n):
    return jax.ops.segment_sum(src, seg, n)
kernel_name = 'mk_decoder_postln_d2_seqx_r4_229e72'

def setup_inputs(seed: int=0):
    np.random.seed(seed)
    _w = jnp.asarray

    def _rec_inputs():
        import jax
        import jax.numpy as jnp
        _rk = jax.random.key(seed)
        x = -0.0003929 + 0.9999 * jax.random.normal(jax.random.fold_in(_rk, 1), (4, 512, 256), jnp.float32)
        _lenS = 512 - jax.random.randint(jax.random.fold_in(_rk, 7), (4,), 0, max(1, 512 // 4) + 1, jnp.int32)
        _lenS2 = 1601 - jax.random.randint(jax.random.fold_in(_rk, 8), (4,), 0, max(1, 1601 // 4) + 1, jnp.int32)
        _ctx_1024P = jax.random.normal(jax.random.fold_in(_rk, 11), (4, 16, 256), jnp.float32)
        _ctx_1024c = jax.random.dirichlet(jax.random.fold_in(_rk, 511), 0.3 * jnp.ones((16,), jnp.float32), (4, 1601))
        _ctx_1024t = jnp.einsum('bsk,bkd->bsd', _ctx_1024c, _ctx_1024P)
        _ctx_1024t = _ctx_1024t * jax.lax.rsqrt(jnp.mean(jnp.square(_ctx_1024t)) + 1e-12) * 0.953939
        ctx_1024 = 2.81802e-05 + 1.00001 * (_ctx_1024t + 0.3 * jax.random.normal(jax.random.fold_in(_rk, 611), (4, 1601, 256), jnp.float32))
        fside_1xSxS2_0 = 0.000675642 + 1.00031 * jax.random.normal(jax.random.fold_in(_rk, 12), (1, 512, 1601), jnp.float32)
        _validS = jnp.arange(512)[None, :] < _lenS[:, None]
        _validS2 = jnp.arange(1601)[None, :] < _lenS2[:, None]
        _causal = jnp.tril(jnp.ones((512, 512), dtype=bool))
        mask_BxS2_if1 = jnp.where(jnp.ones((4, 1601), dtype=bool), 1, 0).astype(jnp.int32)
        return (x, ctx_1024, fside_1xSxS2_0, mask_BxS2_if1)
    x, ctx_1024, fside_1xSxS2_0, mask_BxS2_if1 = _rec_inputs()

    def _L0_attn_setup():
        import jax, jax.numpy as jnp
        import numpy as np
        B, S, D_IN, D_H = (8, 512, 256, 256)
        LR = 0.01
        key = jax.random.key(seed)
        ks = jax.random.split(key, 6)
        return {'in_seq': jax.random.normal(ks[0], (B, S, D_IN), jnp.float32), 'theta_K': jax.random.normal(ks[1], (D_H, D_IN), jnp.float32) * 0.02, 'theta_V': jax.random.normal(ks[2], (D_H, D_IN), jnp.float32) * 0.02, 'theta_Q': jax.random.normal(ks[3], (D_H, D_IN), jnp.float32) * 0.02, 'W0': jax.random.normal(ks[4], (D_H, D_H), jnp.float32) * 0.02, 'b0': jnp.zeros((D_H,), jnp.float32)}
    _L0_attn_all = _L0_attn_setup()
    _L0_attn_in = {k: v for k, v in _L0_attn_all.items() if k in ('theta_K', 'theta_V', 'theta_Q', 'W0', 'b0')}
    del _L0_attn_all

    def _L0_xattn_setup():
        import jax, jax.numpy as jnp
        import numpy as np
        import math
        D = 256
        B, S = (8, 512)

        def _proj(x, W1, b1, W2, b2):
            h = jnp.einsum('bsd,od->bso', x, W1) + b1
            return jnp.einsum('bsd,od->bso', h, W2) + b2
        key = jax.random.key(seed)
        ks = jax.random.split(key, 8)
        q = jax.random.normal(ks[0], (B, S, D), dtype=jnp.float32)
        k = jax.random.normal(ks[1], (B, S, D), dtype=jnp.float32)
        v1 = jax.random.normal(ks[2], (B, S, D), dtype=jnp.float32)
        mask = jax.random.normal(ks[3], (1, S, S), dtype=jnp.float32)
        lim = 1.0 / math.sqrt(D)
        W1 = jax.random.uniform(ks[4], (D, D), jnp.float32, -lim, lim)
        b1 = jax.random.uniform(ks[5], (D,), jnp.float32, -lim, lim)
        W2 = jax.random.uniform(ks[6], (D, D), jnp.float32, -lim, lim)
        b2 = jax.random.uniform(ks[7], (D,), jnp.float32, -lim, lim)
        return {'q': q, 'k': k, 'v1': v1, 'mask': mask, 'W1': W1, 'b1': b1, 'W2': W2, 'b2': b2}
    _L0_xattn_all = _L0_xattn_setup()
    _L0_xattn_in = {k: v for k, v in _L0_xattn_all.items() if k in ('W1', 'b1', 'W2', 'b2')}
    del _L0_xattn_all

    def _L0_ffn_setup():
        import jax, jax.numpy as jnp
        import numpy as np
        E, K = (8, 2)
        B, S, H, F = (2, 512, 256, 1024)
        EPS = 1e-12

        def _expert_ffn(xf, Wi_e, bi_e, Wg_e, bg_e, Wo_e, bo_e, g_e, b_e):
            h = jax.nn.gelu(xf @ Wi_e + bi_e, approximate=False) * jax.nn.sigmoid(xf @ Wg_e + bg_e)
            r = xf + (h @ Wo_e + bo_e)
            mu = jnp.mean(r, axis=-1, keepdims=True)
            var = jnp.mean(jnp.square(r - mu), axis=-1, keepdims=True)
            return (r - mu) * jax.lax.rsqrt(var + EPS) * g_e + b_e
        key = jax.random.key(seed)
        ks = jax.random.split(key, 8)
        s = 0.02
        return {'x': jax.random.normal(ks[0], (B, S, H), jnp.float32), 'Wr': jax.random.normal(ks[1], (H, E), jnp.float32) * s, 'br': jnp.zeros((E,), jnp.float32), 'Wi': jax.random.normal(ks[2], (E, H, F), jnp.float32) * s, 'bi': jnp.zeros((E, F), jnp.float32), 'Wg': jax.random.normal(ks[3], (E, H, F), jnp.float32) * s, 'bg': jnp.zeros((E, F), jnp.float32), 'Wo': jax.random.normal(ks[4], (E, F, H), jnp.float32) * s, 'bo': jnp.zeros((E, H), jnp.float32), 'gamma': jnp.ones((E, H), jnp.float32), 'beta': jnp.zeros((E, H), jnp.float32)}
    _L0_ffn_all = _L0_ffn_setup()
    _L0_ffn_in = {k: v for k, v in _L0_ffn_all.items() if k in ('Wr', 'br', 'Wi', 'bi', 'Wg', 'bg', 'Wo', 'bo', 'gamma', 'beta')}
    del _L0_ffn_all

    def _L1_attn_setup():
        import jax, jax.numpy as jnp
        import numpy as np
        B, T, D_IN, D_OUT, NH = (4, 512, 256, 256, 16)
        HD = D_OUT // NH
        SCALE = 1.0 / float(np.sqrt(HD))
        key = jax.random.key(seed)
        k1, k2, k3 = jax.random.split(key, 3)
        x = jax.random.normal(k1, (B, T, D_IN), dtype=jnp.float32)
        w_qkv = jax.random.normal(k2, (3 * D_OUT, D_IN), dtype=jnp.float32) / np.sqrt(D_IN)
        w_out = jax.random.normal(k3, (D_OUT, D_OUT), dtype=jnp.float32) / np.sqrt(D_OUT)
        return {'x': x, 'w_qkv': w_qkv, 'w_out': w_out}
    _L1_attn_all = _L1_attn_setup()
    _L1_attn_in = {k: v for k, v in _L1_attn_all.items() if k in ('w_qkv', 'w_out')}
    del _L1_attn_all

    def _L1_xattn_setup():
        import jax, jax.numpy as jnp
        import numpy as np
        B, S, E, H = (2, 512, 256, 16)
        D = E // H
        SCALE = 1.0 / np.sqrt(D)

        def rope_tables(seq_len, dim, dtype=jnp.float32):
            inv_freq = 1.0 / 10000.0 ** (jnp.arange(0, dim, 2, dtype=dtype) / dim)
            t = jnp.arange(seq_len, dtype=dtype)
            freqs = t[:, None] * inv_freq[None, :]
            emb = jnp.concatenate([freqs, freqs], axis=-1)
            return (jnp.cos(emb)[None, None], jnp.sin(emb)[None, None])

        def apply_rope(x, cos, sin):
            x2 = jnp.stack([-x[..., 1::2], x[..., 0::2]], axis=-1).reshape(x.shape)
            return x * cos + x2 * sin
        key = jax.random.key(seed)
        ks = jax.random.split(key, 12)
        std = 1.0 / np.sqrt(E)
        inp = {'query': jax.random.normal(ks[0], (B, S, E), jnp.float32), 'key': jax.random.normal(ks[1], (B, S, E), jnp.float32), 'value': jax.random.normal(ks[2], (B, S, E), jnp.float32), 'mask': jnp.ones((B, S), jnp.int32), 'Wq': jax.random.normal(ks[3], (E, E), jnp.float32) * std, 'bq': jax.random.normal(ks[4], (E,), jnp.float32) * std, 'Wk': jax.random.normal(ks[5], (E, E), jnp.float32) * std, 'bk': jax.random.normal(ks[6], (E,), jnp.float32) * std, 'Wv': jax.random.normal(ks[7], (E, E), jnp.float32) * std, 'bv': jax.random.normal(ks[8], (E,), jnp.float32) * std, 'Wo': jax.random.normal(ks[9], (E, E), jnp.float32) * std, 'bo': jax.random.normal(ks[10], (E,), jnp.float32) * std}
        return inp
    _L1_xattn_all = _L1_xattn_setup()
    _L1_xattn_in = {k: v for k, v in _L1_xattn_all.items() if k in ('Wq', 'bq', 'Wk', 'bk', 'Wv', 'bv', 'Wo', 'bo')}
    del _L1_xattn_all

    def _L1_ffn_setup():
        import jax, jax.numpy as jnp
        import numpy as np
        B, S, H, F, G = (8, 512, 256, 1024, 128)
        EPS = 1e-05

        def _dequant(q, scales, g):
            K, N = q.shape
            w = (q.astype(jnp.float32) - 128.0).reshape(K // g, g, N) * scales[:, None, :]
            return w.reshape(K, N)
        key = jax.random.key(seed)
        ks = jax.random.split(key, 8)
        x = jax.random.normal(ks[0], (B, S, H), dtype=jnp.float32)
        ln_gamma = jnp.ones((H,), jnp.float32)
        ln_beta = jnp.zeros((H,), jnp.float32)
        fc1_q = jax.random.randint(ks[1], (H, F), 0, 64, dtype=jnp.int32)
        fc2_q = jax.random.randint(ks[2], (F, H), 0, 64, dtype=jnp.int32)
        fc1_scales = jax.random.uniform(ks[3], (H // G, F), jnp.float32) * 0.02 + 0.001
        fc2_scales = jax.random.uniform(ks[4], (F // G, H), jnp.float32) * 0.02 + 0.001
        fc1_bias = jax.random.normal(ks[5], (F,), jnp.float32) * 0.02
        fc2_bias = jax.random.normal(ks[6], (H,), jnp.float32) * 0.02
        return {'x': x, 'ln_gamma': ln_gamma, 'ln_beta': ln_beta, 'fc1_q': fc1_q, 'fc1_scales': fc1_scales, 'fc1_bias': fc1_bias, 'fc2_q': fc2_q, 'fc2_scales': fc2_scales, 'fc2_bias': fc2_bias}
    _L1_ffn_all = _L1_ffn_setup()
    _L1_ffn_in = {k: v for k, v in _L1_ffn_all.items() if k in ('ln_gamma', 'ln_beta', 'fc1_q', 'fc1_scales', 'fc1_bias', 'fc2_q', 'fc2_scales', 'fc2_bias')}
    del _L1_ffn_all
    return {'x': x, 'ctx_1024': ctx_1024, 'fside_1xSxS2_0': fside_1xSxS2_0, 'mask_BxS2_if1': mask_BxS2_if1, 'L0_attn_theta_K': _L0_attn_in['theta_K'], 'L0_attn_theta_V': _L0_attn_in['theta_V'], 'L0_attn_theta_Q': _L0_attn_in['theta_Q'], 'L0_attn_W0': _L0_attn_in['W0'], 'L0_attn_b0': _L0_attn_in['b0'], 'L0_xattn_W1': _L0_xattn_in['W1'], 'L0_xattn_b1': _L0_xattn_in['b1'], 'L0_xattn_W2': _L0_xattn_in['W2'], 'L0_xattn_b2': _L0_xattn_in['b2'], 'L0_ffn_Wr': _L0_ffn_in['Wr'], 'L0_ffn_br': _L0_ffn_in['br'], 'L0_ffn_Wi': _L0_ffn_in['Wi'], 'L0_ffn_bi': _L0_ffn_in['bi'], 'L0_ffn_Wg': _L0_ffn_in['Wg'], 'L0_ffn_bg': _L0_ffn_in['bg'], 'L0_ffn_Wo': _L0_ffn_in['Wo'], 'L0_ffn_bo': _L0_ffn_in['bo'], 'L0_ffn_gamma': _L0_ffn_in['gamma'], 'L0_ffn_beta': _L0_ffn_in['beta'], 'L1_attn_w_qkv': _L1_attn_in['w_qkv'], 'L1_attn_w_out': _L1_attn_in['w_out'], 'L1_xattn_Wq': _L1_xattn_in['Wq'], 'L1_xattn_bq': _L1_xattn_in['bq'], 'L1_xattn_Wk': _L1_xattn_in['Wk'], 'L1_xattn_bk': _L1_xattn_in['bk'], 'L1_xattn_Wv': _L1_xattn_in['Wv'], 'L1_xattn_bv': _L1_xattn_in['bv'], 'L1_xattn_Wo': _L1_xattn_in['Wo'], 'L1_xattn_bo': _L1_xattn_in['bo'], 'L1_ffn_ln_gamma': _L1_ffn_in['ln_gamma'], 'L1_ffn_ln_beta': _L1_ffn_in['ln_beta'], 'L1_ffn_fc1_q': _L1_ffn_in['fc1_q'], 'L1_ffn_fc1_scales': _L1_ffn_in['fc1_scales'], 'L1_ffn_fc1_bias': _L1_ffn_in['fc1_bias'], 'L1_ffn_fc2_q': _L1_ffn_in['fc2_q'], 'L1_ffn_fc2_scales': _L1_ffn_in['fc2_scales'], 'L1_ffn_fc2_bias': _L1_ffn_in['fc2_bias']}

def reference(x, ctx_1024, fside_1xSxS2_0, mask_BxS2_if1, L0_attn_theta_K, L0_attn_theta_V, L0_attn_theta_Q, L0_attn_W0, L0_attn_b0, L0_xattn_W1, L0_xattn_b1, L0_xattn_W2, L0_xattn_b2, L0_ffn_Wr, L0_ffn_br, L0_ffn_Wi, L0_ffn_bi, L0_ffn_Wg, L0_ffn_bg, L0_ffn_Wo, L0_ffn_bo, L0_ffn_gamma, L0_ffn_beta, L1_attn_w_qkv, L1_attn_w_out, L1_xattn_Wq, L1_xattn_bq, L1_xattn_Wk, L1_xattn_bk, L1_xattn_Wv, L1_xattn_bv, L1_xattn_Wo, L1_xattn_bo, L1_ffn_ln_gamma, L1_ffn_ln_beta, L1_ffn_fc1_q, L1_ffn_fc1_scales, L1_ffn_fc1_bias, L1_ffn_fc2_q, L1_ffn_fc2_scales, L1_ffn_fc2_bias):
    import jax
    import jax.numpy as jnp

    def _L0_attn_ref(in_seq, theta_K, theta_V, theta_Q, W0, b0):
        import jax, jax.numpy as jnp
        import numpy as np
        B, S, D_IN, D_H = (8, 512, 256, 256)
        LR = 0.01
        'TTT layer: per-token inner SGD step on MSE(W@k+b, v), then predict W@q+b.'
        d_h = W0.shape[0]
        K = jnp.einsum('bsd,ed->bse', in_seq, theta_K)
        V = jnp.einsum('bsd,ed->bse', in_seq, theta_V)
        Q = jnp.einsum('bsd,ed->bse', in_seq, theta_Q)

        def step(carry, kvq):
            W, b = carry
            k, v, q = kvq
            pred = W @ k + b
            g = 2.0 / d_h * (pred - v)
            W = W - LR * jnp.outer(g, k)
            b = b - LR * g
            out = W @ q + b
            return ((W, b), out)

        def run_seq(k_s, v_s, q_s):
            _, ys = jax.lax.scan(step, (W0, b0), (k_s, v_s, q_s))
            return ys
        return jax.vmap(run_seq)(K, V, Q)

    def _L0_xattn_ref(q, k, v1, mask, W1, b1, W2, b2):
        import jax, jax.numpy as jnp
        import numpy as np
        import math
        D = 256
        B, S = (8, 512)

        def _proj(x, W1, b1, W2, b2):
            h = jnp.einsum('bsd,od->bso', x, W1) + b1
            return jnp.einsum('bsd,od->bso', h, W2) + b2
        qp = _proj(q, W1, b1, W2, b2)
        kp = _proj(k, W1, b1, W2, b2)
        scale = 1.0 / math.sqrt(qp.shape[-1])
        qk = jnp.einsum('bqd,bkd->bqk', qp, kp) * scale
        qk = qk + mask
        attn = jax.nn.softmax(qk, axis=-1)
        return jnp.einsum('bqk,bkd->bqd', attn, v1)

    def _L0_ffn_ref(x, Wr, br, Wi, bi, Wg, bg, Wo, bo, gamma, beta):
        import jax, jax.numpy as jnp
        import numpy as np
        E, K = (8, 2)
        B, S, H, F = (2, 512, 256, 1024)
        EPS = 1e-12

        def _expert_ffn(xf, Wi_e, bi_e, Wg_e, bg_e, Wo_e, bo_e, g_e, b_e):
            h = jax.nn.gelu(xf @ Wi_e + bi_e, approximate=False) * jax.nn.sigmoid(xf @ Wg_e + bg_e)
            r = xf + (h @ Wo_e + bo_e)
            mu = jnp.mean(r, axis=-1, keepdims=True)
            var = jnp.mean(jnp.square(r - mu), axis=-1, keepdims=True)
            return (r - mu) * jax.lax.rsqrt(var + EPS) * g_e + b_e
        b, s, h = x.shape
        T = b * s
        xf = x.reshape(T, h)
        probs = jax.nn.softmax(xf @ Wr + br, axis=-1)
        topw, topi = jax.lax.top_k(probs, K)
        topw = topw / jnp.sum(topw, axis=-1, keepdims=True)
        c = jnp.zeros((T, E), x.dtype).at[jnp.arange(T)[:, None], topi].set(topw)
        y = jax.vmap(_expert_ffn, in_axes=(None, 0, 0, 0, 0, 0, 0, 0, 0))(xf, Wi, bi, Wg, bg, Wo, bo, gamma, beta)
        out = jnp.einsum('te,eth->th', c, y)
        return out.reshape(b, s, h)

    def _L1_attn_ref(x, w_qkv, w_out):
        import jax, jax.numpy as jnp
        import numpy as np
        B, T, D_IN, D_OUT, NH = (4, 512, 256, 256, 16)
        HD = D_OUT // NH
        SCALE = 1.0 / float(np.sqrt(HD))
        b, t, _ = x.shape
        qkv = jnp.einsum('btd,ed->bte', x, w_qkv)
        qkv = qkv.reshape(b, t, 3, NH, HD)
        q, k, v = jnp.moveaxis(qkv, 2, 0)
        scores = jnp.einsum('bqhd,bkhd->bhqk', q, k) * SCALE
        causal_bias = (1.0 - jnp.tril(jnp.ones((t, t), dtype=x.dtype))) * -10000.0
        scores = scores + causal_bias
        attn = jax.nn.softmax(scores, axis=-1)
        out = jnp.einsum('bhqk,bkhd->bqhd', attn, v)
        out = out.reshape(b, t, D_OUT)
        return jnp.einsum('btd,ed->bte', out, w_out)

    def _L1_xattn_ref(query, key, value, mask, Wq, bq, Wk, bk, Wv, bv, Wo, bo):
        import jax, jax.numpy as jnp
        import numpy as np
        B, S, E, H = (2, 512, 256, 16)
        D = E // H
        SCALE = 1.0 / np.sqrt(D)

        def rope_tables(seq_len, dim, dtype=jnp.float32):
            inv_freq = 1.0 / 10000.0 ** (jnp.arange(0, dim, 2, dtype=dtype) / dim)
            t = jnp.arange(seq_len, dtype=dtype)
            freqs = t[:, None] * inv_freq[None, :]
            emb = jnp.concatenate([freqs, freqs], axis=-1)
            return (jnp.cos(emb)[None, None], jnp.sin(emb)[None, None])

        def apply_rope(x, cos, sin):
            x2 = jnp.stack([-x[..., 1::2], x[..., 0::2]], axis=-1).reshape(x.shape)
            return x * cos + x2 * sin
        b, sq, _ = query.shape
        sk = key.shape[1]
        Q = (query @ Wq.T + bq).reshape(b, sq, H, D).transpose(0, 2, 1, 3)
        K = (key @ Wk.T + bk).reshape(b, sk, H, D).transpose(0, 2, 1, 3)
        V = (value @ Wv.T + bv).reshape(b, sk, H, D).transpose(0, 2, 1, 3)
        cos_q, sin_q = rope_tables(sq, D)
        cos_k, sin_k = rope_tables(sk, D)
        Q = apply_rope(Q, cos_q, sin_q)
        K = apply_rope(K, cos_k, sin_k)
        scores = jnp.einsum('bhqd,bhkd->bhqk', Q, K) * SCALE
        neg_inf = jnp.finfo(scores.dtype).min
        scores = jnp.where(mask[:, None, None, :] == 0, neg_inf, scores)
        attn = jax.nn.softmax(scores, axis=-1)
        out = jnp.einsum('bhqk,bhkd->bhqd', attn, V)
        out = out.transpose(0, 2, 1, 3).reshape(b, sq, E)
        return out @ Wo.T + bo

    def _L1_ffn_ref(x, ln_gamma, ln_beta, fc1_q, fc1_scales, fc1_bias, fc2_q, fc2_scales, fc2_bias):
        import jax, jax.numpy as jnp
        import numpy as np
        B, S, H, F, G = (8, 512, 256, 1024, 128)
        EPS = 1e-05

        def _dequant(q, scales, g):
            K, N = q.shape
            w = (q.astype(jnp.float32) - 128.0).reshape(K // g, g, N) * scales[:, None, :]
            return w.reshape(K, N)
        residual = x
        mu = jnp.mean(x, axis=-1, keepdims=True)
        var = jnp.mean(jnp.square(x - mu), axis=-1, keepdims=True)
        h = (x - mu) * jax.lax.rsqrt(var + EPS) * ln_gamma + ln_beta
        hf = h.reshape(-1, H)
        w1 = _dequant(fc1_q, fc1_scales, G)
        y = hf @ w1 + fc1_bias
        y = jax.nn.silu(y)
        w2 = _dequant(fc2_q, fc2_scales, G)
        z = y @ w2 + fc2_bias
        return residual + 0.5 * z.reshape(residual.shape)
    x = _layernorm(x + _L0_attn_ref(x, L0_attn_theta_K, L0_attn_theta_V, L0_attn_theta_Q, L0_attn_W0, L0_attn_b0), axis=-1)
    x = _layernorm(x + _L0_xattn_ref(x, ctx_1024, ctx_1024, fside_1xSxS2_0, L0_xattn_W1, L0_xattn_b1, L0_xattn_W2, L0_xattn_b2), axis=-1)
    x = _layernorm(x + _L0_ffn_ref(x, L0_ffn_Wr, L0_ffn_br, L0_ffn_Wi, L0_ffn_bi, L0_ffn_Wg, L0_ffn_bg, L0_ffn_Wo, L0_ffn_bo, L0_ffn_gamma, L0_ffn_beta), axis=-1)
    x = _layernorm(x + _L1_attn_ref(x, L1_attn_w_qkv, L1_attn_w_out), axis=-1)
    x = _layernorm(x + _L1_xattn_ref(x, ctx_1024, ctx_1024, mask_BxS2_if1, L1_xattn_Wq, L1_xattn_bq, L1_xattn_Wk, L1_xattn_bk, L1_xattn_Wv, L1_xattn_bv, L1_xattn_Wo, L1_xattn_bo), axis=-1)
    x = _layernorm(x + _L1_ffn_ref(x, L1_ffn_ln_gamma, L1_ffn_ln_beta, L1_ffn_fc1_q, L1_ffn_fc1_scales, L1_ffn_fc1_bias, L1_ffn_fc2_q, L1_ffn_fc2_scales, L1_ffn_fc2_bias), axis=-1)
    return x

_drawn_inputs = setup_inputs


def setup_inputs(seed=0):
    import zlib

    import numpy as np

    out = dict(_drawn_inputs(seed))
    spreads = {'L0_attn_b0': (0.0, 0.1),
     'L0_ffn_br': (0.0, 0.1),
     'L0_ffn_bi': (0.0, 0.8),
     'L0_ffn_bg': (0.0, 0.8),
     'L0_ffn_bo': (0.0, 0.297),
     'L0_ffn_gamma': (1.0, 0.2),
     'L0_ffn_beta': (0.0, 0.1),
     'L1_ffn_ln_gamma': (1.0, 0.2),
     'L1_ffn_ln_beta': (0.0, 0.1)}
    factors = {'L0_attn_theta_K': 8.0,
     'L0_attn_theta_V': 8.0,
     'L0_xattn_b1': 8.0,
     'L0_xattn_W2': 2.919,
     'L0_xattn_b2': 8.0,
     'L0_ffn_Wi': 2.726,
     'L0_ffn_Wg': 8.0,
     'L0_ffn_Wo': 3.019,
     'L1_xattn_bq': 6.485,
     'L1_xattn_bk': 5.673,
     'L1_ffn_fc1_bias': 26.922,
     'L1_ffn_fc2_bias': 64.0}
    for name, (base, spread) in spreads.items():
        noise = np.random.default_rng([zlib.crc32(name.encode()), seed]).standard_normal(out[name].shape)
        drawn = base * np.exp(spread * noise) if base else spread * noise
        out[name] = jnp.asarray(drawn.astype(out[name].dtype))
    for name, factor in factors.items():
        out[name] = (out[name] * factor).astype(out[name].dtype)
    return out
```

```python
from contextlib import ExitStack

import numpy as np

import concourse.bass as bass
from concourse import mybir

P = 128
B, S, D = 4, 512, 256
T = B * S
NT = T // P
KD = D // P
TPB = S // P
S2 = 1601
NK2 = (S2 + P - 1) // P
F = 1024
NF = F // P
E = 8
H, DH = 16, 16
LN_EPS = 1e-5

F32 = mybir.dt.float32
F16 = mybir.dt.float16
BF16 = mybir.dt.bfloat16
I32 = mybir.dt.int32
ALU = mybir.AluOpType
ACT = mybir.ActivationFunctionType
AX_X = mybir.AxisListType.X
ds = bass.ds

PHASES = "ABCDEF"


class Norm:

    def __init__(self, ctx, nc, name, X, eps):
        self.nc, self.X, self.eps = nc, X, eps
        sb = lambda n, s: ctx.enter_context(nc.sbuf_tensor(f"{name}_{n}", s, F32))
        sem = lambda n: ctx.enter_context(nc.semaphore(f"{name}_{n}"))
        self.stats_buf = sb("stats", [P, NT, 6])
        self.mv = sb("mv", [P, NT, 2])
        self.var_eps = sb("var_eps", [P, NT])
        self.rstd = sb("rstd", [P, NT])
        self.neg_half = sb("neg_half", [P, NT])
        self.half_ready = sem("half_ready")
        self.stats_ready = sem("stats_ready")
        self.mv_ready = sem("mv_ready")
        self.ve_ready = sem("ve_ready")
        self.rstd_ready = sem("rstd_ready")
        self.normed = sem("normed")

    def setup(self, pool):
        self.nc.gpsimd.memset(self.neg_half[:], -0.5).then_inc(self.half_ready, 1)
        pool.wait_ge(self.half_ready, 1)

    def statistics(self, dve, c, sum_ready, first=0):
        for t in range(c * TPB, (c + 1) * TPB):
            dve.wait_ge(sum_ready, first + t + 1)
            self.nc.vector.bn_stats(self.stats_buf[:, t, :], self.X[:, t, :]).then_inc(self.stats_ready, 1)
        for t in range(c * TPB, (c + 1) * TPB):
            dve.wait_ge(self.stats_ready, t + 1)
            self.nc.vector.bn_aggr(self.mv[:, t, :], self.stats_buf[:, t, :]).then_inc(self.mv_ready, 1)

    def inverse_deviation(self, pool, c):
        g = slice(c * TPB, (c + 1) * TPB)
        pool.wait_ge(self.mv_ready, (c + 1) * TPB)
        self.nc.gpsimd.tensor_scalar(self.var_eps[:, g], self.mv[:, g, 1], self.eps, 1.0,
                                     ALU.add, ALU.mult).then_inc(self.ve_ready, 1)
        pool.wait_ge(self.ve_ready, c + 1)
        self.nc.gpsimd.tensor_tensor(self.rstd[:, g], self.var_eps[:, g], self.neg_half[:, g],
                                     ALU.pow).then_inc(self.rstd_ready, 1)

    def normalize(self, dve, c, out=None):
        out = self.X if out is None else out
        dve.wait_ge(self.rstd_ready, c + 1)
        for t in range(c * TPB, (c + 1) * TPB):
            self.nc.vector.tensor_scalar(out[:, t, :], self.X[:, t, :], self.mv[:, t, 0:1], self.rstd[:, t:t + 1],
                                         ALU.subtract, ALU.mult).then_inc(self.normed, 1)


def turn_group(nc, pe, src, ident, banks, c, normed, copied, turned):
    pe.wait_ge(normed, (c + 1) * TPB)
    if c >= 1:
        pe.wait_ge(copied, KD * c)
    for h in range(KD):
        for t in range(TPB):
            last = nc.tensor.transpose(banks[h][:, t * P:(t + 1) * P], src[:, c * TPB + t, h * P:(h + 1) * P], ident)
        last.then_inc(turned, 1)


def copy_turned(nc, act, dst, banks, c, turned, copied):
    for h in range(KD):
        act.wait_ge(turned, KD * c + h + 1)
        nc.scalar.activation(dst[:, h, c * S:(c + 1) * S], banks[h][:], ACT.Copy).then_inc(copied, 1)


LEVELS = 7
ETA = 0.01 * 2.0 / D


def phase_ttt(nc, ctx, dram, X, XT, ident):
    sb = lambda n, s, dt=F32: ctx.enter_context(nc.sbuf_tensor(f"A_{n}", s, dt))
    sem = lambda n: ctx.enter_context(nc.semaphore(f"A_{n}"))
    thKT, thQT, thVT = (sb(n, [P, KD, D]) for n in ("thKT", "thQT", "thVT"))
    thK, thQ, W0T = (sb(n, [P, KD, D]) for n in ("thK", "thQ", "W0T"))
    b0 = sb("b0", [P, D])
    masks = sb("masks", [P, LEVELS + 2, P])
    M1, M2 = sb("M1", [P, KD, D]), sb("M2", [P, KD, D])
    KT, QT = sb("KT", [P, KD, T]), sb("QT", [P, KD, T])
    ROW = TPB * S
    GN = sb("GN", [P, B * ROW + S])
    GQ = sb("GQ", [P, B * ROW])
    XI, YI = sb("XI", [P, B, S]), sb("YI", [P, B, S])
    CT = sb("CT", [P, 4, S])
    P1 = sb("P1", [P, 2, S])
    R = sb("R", [P, 2, D])
    U = KT[:, :, :].rearrange("p k t -> p (k t)").rearrange("p (n d) -> p n d", d=D)
    banks = [ctx.enter_context(nc.psum_tensor(f"A_bank{i}", [P, S], F32)) for i in range(8)]

    norm = Norm(ctx, nc, "A_norm", X, LN_EPS)
    loaded = sem("loaded")
    product, act_copied, dve_copied = sem("product"), sem("act_copied"), sem("dve_copied")
    mask_ready, start_tmp, start_ready = sem("mask_ready"), sem("start_tmp"), sem("start_ready")
    cx_ready, cx_copied = sem("cx_ready"), sem("cx_copied")
    xcx_ready, inv_ready = sem("xcx_ready"), sem("inv_ready")
    acc_ready, rhs_ready, u_ready, u_copied = sem("acc_ready"), sem("rhs_ready"), sem("u_ready"), sem("u_copied")
    out_ready, sum_ready, xb_ready = sem("out_ready"), sem("sum_ready"), sem("xb_ready")
    turned, copied = sem("turned"), sem("copied")

    plain = [("M2", h) for h in range(KD)] + [("M1", h) for h in range(KD)]
    plain += [(w, (h, b)) for b in range(B) for h in range(KD) for w in ("KT", "QT")]
    plain += [(w, (b, j)) for b in range(B) for j in range(TPB) for w in ("GK", "GQ")]
    by_act = {"M2", "KT", "GK"}
    order = []
    for kind, _ in plain:
        mine = kind in by_act
        order.append((mine, 1 + sum(1 for m, _ in order if m == mine)))

    def wait_copied(eng, n):
        mine, count = order[n]
        eng.wait_ge(act_copied if mine else dve_copied, count)

    last_proj = max(n for n, (k, _) in enumerate(plain) if k in ("KT", "QT"))
    pairs = [(0, 1), (2, 3)]
    steps = [(m, b) for pair in pairs for m in range(1, LEVELS) for b in pair]
    step_no = {s: n for n, s in enumerate(steps)}
    blocks = [(b, i) for i in range(TPB) for b in range(B)]

    def diagonal(b):
        v = GN[:, b * ROW:b * ROW + TPB * (S + P)].rearrange("p (j c) -> p j c", c=S + P)
        return v[:, :, 0:P]

    def four(m):
        return masks[:, m:m + 1, :].broadcast_to([P, TPB, P])

    def view(t):
        return t.rearrange("p (j c) -> p j c", c=P)

    with nc.Block() as block:
        @block.sync
        def _(sp):
            for t, n in ((thQ, "L0_attn_theta_Q"), (thK, "L0_attn_theta_K"), (W0T, "W0T"), (thVT, "thVT"), (thKT, "thKT"), (thQT, "thQT")):
                sp.dma_start(t[:], dram[n].rearrange("(k p) d -> p k d", p=P)).then_inc(loaded, 16)
            sp.dma_start(b0[:], dram["L0_attn_b0"].partition_broadcast(P)).then_inc(loaded, 16)
            sp.dma_start(masks[:], dram["ttt_masks"]).then_inc(loaded, 16)

        @block.tensor
        def _(pe):
            mm = nc.tensor.matmul
            pe.wait_ge(loaded, 128)
            for n, (kind, w) in enumerate(plain):
                bank = banks[n % 8]
                if n >= 8:
                    wait_copied(pe, n - 8)
                if kind in ("GK", "GQ") and w == (0, 0) and kind == "GK":
                    wait_copied(pe, last_proj)
                    wait_copied(pe, last_proj - 1)
                for k in range(KD):
                    if kind in ("M1", "M2"):
                        lhsT, rhs, o = (thK if kind == "M1" else thQ)[:, k, w * P:(w + 1) * P], W0T[:, k, :], bank[:, 0:D]
                    elif kind in ("KT", "QT"):
                        h, b = w
                        lhsT, rhs, o = (thKT if kind == "KT" else thQT)[:, k, h * P:(h + 1) * P], XT[:, k, b * S:(b + 1) * S], bank[:]
                    else:
                        b, j = w
                        at = b * S + j * P
                        lhsT = KT[:, k, at:at + P]
                        rhs = (KT if kind == "GK" else QT)[:, k, at:(b + 1) * S]
                        o = bank[:, j * P:S]
                    last = mm(o, lhsT, rhs, start=(k == 0), stop=(k == KD - 1))
                last.then_inc(product, 1)
            for n in range(len(plain) - 8, len(plain)):
                wait_copied(pe, n)
            for n, (m, b) in enumerate(steps):
                s = b % 2
                cx, xcx, ycx = banks[3 * s], banks[3 * s + 1], banks[3 * s + 2]
                pe.wait_ge(mask_ready, n + 1)
                if m == 1:
                    pe.wait_ge(start_ready, 2 * (b + 1))
                else:
                    pe.wait_ge(inv_ready, 2 * (step_no[(m - 1, b)] + 1))
                if b >= 2 and m == 1:
                    pe.wait_ge(inv_ready, 2 * (step_no[(LEVELS - 1, b - 2)] + 1))
                for j in range(TPB):
                    c = slice(j * P, (j + 1) * P)
                    last = mm(cx[:, c], CT[:, n % 4, c], XI[:, b, c], start=True, stop=True)
                last.then_inc(cx_ready, 1)
                pe.wait_ge(cx_copied, n + 1)
                for j in range(TPB):
                    c = slice(j * P, (j + 1) * P)
                    mm(xcx[:, c], YI[:, b, c], P1[:, s, c], start=True, stop=True)
                for j in range(TPB):
                    c = slice(j * P, (j + 1) * P)
                    last = mm(ycx[:, c], P1[:, s, c], YI[:, b, c], start=True, stop=True)
                last.then_inc(xcx_ready, 1)
            pe.wait_ge(inv_ready, 2 * len(steps))
            for n, (b, i) in enumerate(blocks):
                tok = slice(b * S + i * P, b * S + (i + 1) * P)
                acc, u_ps, out_ps = banks[n % 2], banks[2 + n % 2], banks[4 + n % 2]
                if n >= 2:
                    pe.wait_ge(rhs_ready, n - 1)
                for k in range(KD):
                    last = mm(acc[:, 0:D], XT[:, k, tok], M1[:, k, :], start=(k == 0), stop=(i == 0 and k == KD - 1))
                if i > 0:
                    pe.wait_ge(u_copied, (i - 1) * B + b + 1)
                for j in range(i):
                    last = mm(acc[:, 0:D], GN[:, b * ROW + j * S + i * P:b * ROW + j * S + (i + 1) * P],
                              U[:, b * TPB + j, :], start=False, stop=(j == i - 1))
                last.then_inc(acc_ready, 1)
                if n >= 2:
                    pe.wait_ge(sum_ready, n - 1)
                for k in range(KD):
                    mm(out_ps[:, 0:D], XT[:, k, tok], M2[:, k, :], start=(k == 0), stop=False)
                for j in range(i):
                    mm(out_ps[:, 0:D], GQ[:, b * ROW + j * S + i * P:b * ROW + j * S + (i + 1) * P],
                       U[:, b * TPB + j, :], start=False, stop=False)
                pe.wait_ge(rhs_ready, n + 1)
                if n >= 2:
                    pe.wait_ge(u_copied, n - 1)
                mm(u_ps[:, 0:D], YI[:, b, i * P:(i + 1) * P], R[:, n % 2, :], start=True, stop=True).then_inc(u_ready, 1)
                pe.wait_ge(u_copied, n + 1)
                mm(out_ps[:, 0:D], GQ[:, b * ROW + i * (S + P):b * ROW + i * (S + P) + P],
                   U[:, b * TPB + i, :], start=False, stop=True).then_inc(out_ready, 1)
            pe.wait_ge(sum_ready, NT)
            for c in range(B):
                turn_group(nc, pe, X, ident[:], banks, c, norm.normed, copied, turned)

        @block.scalar
        def _(act):
            for n, (kind, w) in enumerate(plain):
                if kind not in by_act:
                    continue
                act.wait_ge(product, n + 1)
                bank = banks[n % 8]
                if kind == "M2":
                    o = nc.scalar.activation(M2[:, w, :], bank[:, 0:D], ACT.Copy)
                elif kind == "KT":
                    h, b = w
                    o = nc.scalar.activation(KT[:, h, b * S:(b + 1) * S], bank[:], ACT.Copy)
                else:
                    b, j = w
                    o = nc.scalar.activation(GN[:, b * ROW + j * (S + P):b * ROW + (j + 1) * S], bank[:, j * P:S],
                                             ACT.Copy, bias=-ETA, scale=-ETA)
                o.then_inc(act_copied, 1)
            for n, (m, b) in enumerate(steps):
                act.wait_ge(cx_ready, n + 1)
                if n >= 2:
                    act.wait_ge(xcx_ready, n - 1)
                nc.scalar.activation(P1[:, b % 2, :], banks[3 * (b % 2)][:], ACT.Copy).then_inc(cx_copied, 1)
            for n, (b, i) in enumerate(blocks):
                act.wait_ge(u_ready, n + 1)
                nc.scalar.activation(U[:, b * TPB + i, :], banks[2 + n % 2][:, 0:D], ACT.Copy).then_inc(u_copied, 1)
            for c in range(B):
                copy_turned(nc, act, XT, banks, c, turned, copied)

        @block.gpsimd
        def _(pool):
            norm.setup(pool)
            pool.wait_ge(loaded, 128)
            tt = nc.gpsimd.tensor_tensor

            def start(b, tmp):
                for q, (m, dst) in enumerate(((LEVELS, XI), (0, YI))):
                    tt(view(dst[:, b, :]), diagonal(b), four(m), ALU.mult).then_inc(start_tmp, 1)
                    pool.wait_ge(start_tmp, 2 * b + q + 1)
                    tt(view(dst[:, b, :]), view(dst[:, b, :]), ident[:].rearrange("p (a c) -> p a c", a=1).broadcast_to([P, TPB, P]),
                       ALU.add).then_inc(start_ready, 1)

            for n, (m, b) in enumerate(steps):
                if m == 1:
                    wait_copied(pool, plain.index(("GK", (b, TPB - 1))))
                    start(b, None)
                if n >= 4:
                    pool.wait_ge(cx_ready, n - 3)
                tt(view(CT[:, n % 4, :]), diagonal(b), four(m), ALU.mult).then_inc(mask_ready, 1)
            for c in range(B):
                norm.inverse_deviation(pool, c)

        @block.vector
        def _(dve):
            dve.wait_ge(loaded, 128)
            for t in range(NT):
                nc.vector.tensor_tensor(X[:, t, :], X[:, t, :], b0[:], ALU.add).then_inc(xb_ready, 1)
            for n, (kind, w) in enumerate(plain):
                if kind in by_act:
                    continue
                dve.wait_ge(product, n + 1)
                bank = banks[n % 8]
                if kind == "M1":
                    o = nc.vector.tensor_tensor(M1[:, w, :], bank[:, 0:D], thVT[:, w, :], ALU.subtract)
                elif kind == "QT":
                    h, b = w
                    o = nc.vector.tensor_copy(QT[:, h, b * S:(b + 1) * S], bank[:])
                else:
                    b, j = w
                    at = b * ROW + j * (S + P)
                    o = nc.vector.scalar_tensor_tensor(GQ[:, at:at + P], bank[:, j * P:(j + 1) * P], 1.0,
                                                       masks[:, LEVELS + 1, :], ALU.add, ALU.mult)
                    if j < TPB - 1:
                        o = nc.vector.tensor_scalar(GQ[:, at + P:b * ROW + (j + 1) * S], bank[:, (j + 1) * P:S],
                                                    1.0, -ETA, ALU.add, ALU.mult)
                o.then_inc(dve_copied, 1)
            for n, (m, b) in enumerate(steps):
                dve.wait_ge(xcx_ready, n + 1)
                s = b % 2
                nc.vector.tensor_tensor(XI[:, b, :], XI[:, b, :], banks[3 * s + 1][:], ALU.add).then_inc(inv_ready, 1)
                nc.vector.tensor_tensor(YI[:, b, :], YI[:, b, :], banks[3 * s + 2][:], ALU.add).then_inc(inv_ready, 1)
            dve.wait_ge(xb_ready, NT)

            def add_out(n):
                b, i = blocks[n]
                dve.wait_ge(out_ready, n + 1)
                x = X[:, b * TPB + i, :]
                nc.vector.tensor_tensor(x, banks[4 + n % 2][:, 0:D], x, ALU.add).then_inc(sum_ready, 1)

            for n in range(NT):
                dve.wait_ge(acc_ready, n + 1)
                if n >= 2:
                    dve.wait_ge(u_ready, n - 1)
                nc.vector.tensor_tensor(R[:, n % 2, :], banks[n % 2][:, 0:D], b0[:], ALU.add).then_inc(rhs_ready, 1)
                add_out(n)
            dve.wait_ge(sum_ready, NT)
            for c in range(B):
                norm.statistics(dve, c, sum_ready)
            for c in range(B):
                norm.normalize(dve, c)


def key_rows(kt):
    return min(P, S2 - kt * P)


def phase_cross0(nc, ctx, dram, X, XT, ident):
    sb = lambda n, s, dt=F32: ctx.enter_context(nc.sbuf_tensor(f"B_{n}", s, dt))
    sem = lambda n: ctx.enter_context(nc.semaphore(f"B_{n}"))
    W1, W2T = sb("W1", [P, KD, D]), sb("W2T", [P, KD, D])
    b1, b2, b12 = sb("b1", [P, KD]), sb("b2", [P, KD]), sb("b12", [P, KD])
    W12T, W12 = sb("W12T", [P, KD, D]), sb("W12", [P, KD, D])
    ctxT = sb("ctxT", [P, 2, KD, S2])
    ctxN = sb("ctxN", [P, 2, NK2, D])
    bias = sb("bias", [P, TPB, S2])
    qpT, q2T = sb("qpT", [P, KD, S]), sb("q2T", [P, KD, S])
    probs = sb("probs", [P, 2, S2])
    PT = sb("PT", [P, 2, NK2, P])
    top, neg_top, total, inv_total = (sb(n, [P, 2]) for n in ("top", "neg_top", "total", "inv_total"))
    fence = sb("fence", [P, 1])
    scores_ps = ctx.enter_context(nc.psum_tensor("B_scores", [P, 4 * S], F32))
    ring = [ctx.enter_context(nc.psum_tensor(f"B_ring{i}", [P, S], F32)) for i in range(2)]
    av_ps = ctx.enter_context(nc.psum_tensor("B_av", [P, D], F32))

    norm = Norm(ctx, nc, "B_norm", X, LN_EPS)
    loaded, bias_loaded = sem("loaded"), sem("bias_loaded")
    ctx_loaded = [sem(f"ctx_loaded{i}") for i in range(2)]
    w_product, w_copied = sem("w_product"), sem("w_copied")
    ring_ready, act_copied, dve_copied = sem("ring_ready"), sem("act_copied"), sem("dve_copied")
    scores_ready, scores_read, max_ready, probs_ready = sem("scores_ready"), sem("scores_read"), sem("max_ready"), sem("probs_ready")
    av_ready, inv_ready, sum_ready = sem("av_ready"), sem("inv_ready"), sem("sum_ready")
    turned, copied = sem("turned"), sem("copied")

    RING, BY_ACT, BY_DVE = 4 + 4 * TPB, 4 + 2 * TPB, 2 * TPB
    groups = [range(g * 4, min(g * 4 + 4, NK2)) for g in range(4)]

    with nc.Block() as block:
        @block.sync
        def _(sp):
            sp.dma_start(W1[:], dram["L0_xattn_W1"].rearrange("(k p) d -> p k d", p=P)).then_inc(loaded, 16)
            sp.dma_start(W2T[:], dram["xW2T"].rearrange("(k p) d -> p k d", p=P)).then_inc(loaded, 16)
            sp.dma_start(b1[:], dram["L0_xattn_b1"]).then_inc(loaded, 16)
            sp.dma_start(b2[:], dram["L0_xattn_b2"]).then_inc(loaded, 16)
            with sp.Fori(0, B // 2) as bb:
                for u in range(2):
                    b = bb * 2 + u
                    sp.wait_ge(av_ready, bb * 2 * TPB)
                    sp.dma_start(ctxT[:, u], dram["ctxT"][ds(b, 1)].rearrange("b (k p) s -> p (b k) s", p=P)).then_inc(ctx_loaded[u], 16)
                    sp.dma_start(ctxN[:, u, 0:NK2 - 1, :], dram["ctx"][ds(b, 1), 0:(NK2 - 1) * P].rearrange("b (k p) d -> p (b k) d", p=P)).then_inc(ctx_loaded[u], 16)
                    sp.dma_start(ctxN[0:key_rows(NK2 - 1), u, NK2 - 1, :], dram["ctx"][ds(b, 1), (NK2 - 1) * P:S2].rearrange("b p d -> (b p) d")).then_inc(ctx_loaded[u], 16)

        @block.tensor
        def _(pe):
            mm = nc.tensor.matmul
            pe.wait_ge(loaded, 64)
            for n in range(6):
                kind, h = n // 2, n % 2
                if n >= 2:
                    pe.wait_ge(w_copied, n - 1)
                for k in range(KD):
                    lhsT = (W1 if kind == 0 else W2T)[:, k, h * P:(h + 1) * P]
                    rhs = (W2T[:, k, :], W1[:, k, :], b1[:, k:k + 1])[kind]
                    last = mm(ring[h][:, 0:1] if kind == 2 else ring[h][:, 0:D], lhsT, rhs, start=(k == 0), stop=(k == KD - 1))
                last.then_inc(w_product, 1)
            pe.wait_ge(w_copied, 6)

            def scores(b, u, t):
                n = b * TPB + t
                pe.wait_ge(scores_read, n)
                for c in range(4):
                    w = min(S, S2 - c * S)
                    for k in range(KD):
                        last = mm(scores_ps[:, c * S:c * S + w], q2T[:, k, t * P:(t + 1) * P], ctxT[:, u, k, c * S:c * S + w],
                                  start=(k == 0), stop=(k == KD - 1))
                last.then_inc(scores_ready, 1)

            with pe.Fori(0, B // 2) as bb:
                for u in range(2):
                    b = bb * 2 + u
                    pe.wait_ge(dve_copied, b * BY_DVE)
                    pe.wait_ge(act_copied, b * BY_ACT)
                    for m in range(KD):
                        for k in range(KD):
                            last = mm(ring[m][:], W12T[:, k, m * P:(m + 1) * P], XT[:, k, ds(b * S, S)], start=(k == 0), stop=(k == KD - 1))
                        last.then_inc(ring_ready, 1)
                    pe.wait_ge(act_copied, b * BY_ACT + 2)
                    for m in range(KD):
                        for k in range(KD):
                            last = mm(ring[m][:], W12[:, k, m * P:(m + 1) * P], qpT[:, k, :], start=(k == 0), stop=(k == KD - 1))
                        last.then_inc(ring_ready, 1)
                    pe.wait_ge(act_copied, b * BY_ACT + 4)
                    pe.wait_ge(ctx_loaded[u], bb * 48 + 48)
                    scores(b, u, 0)
                    for t in range(TPB):
                        n = b * TPB + t
                        if t + 1 < TPB:
                            scores(b, u, t + 1)
                        pe.wait_ge(probs_ready, n + 1)
                        for g in range(4):
                            if g % 2 == 0:
                                pe.wait_ge(dve_copied, b * BY_DVE + 2 * t + g // 2)
                            else:
                                pe.wait_ge(act_copied, b * BY_ACT + 4 + 2 * t + g // 2)
                            for q, kt in enumerate(groups[g]):
                                r = key_rows(kt)
                                last = nc.tensor.transpose(ring[g % 2][0:r, q * P:(q + 1) * P], probs[:, t % 2, kt * P:kt * P + r], ident[:])
                            last.then_inc(ring_ready, 1)
                        pe.wait_ge(dve_copied, b * BY_DVE + 2 * t + 2)
                        pe.wait_ge(act_copied, b * BY_ACT + 4 + 2 * t + 2)
                        pe.wait_ge(sum_ready, n)
                        for kt in range(NK2):
                            r = key_rows(kt)
                            last = mm(av_ps[:], PT[0:r, t % 2, kt, :], ctxN[0:r, u, kt, :], start=(kt == 0), stop=(kt == NK2 - 1))
                        last.then_inc(av_ready, 1)
            for c in range(B):
                turn_group(nc, pe, X, ident[:], ring, c, norm.normed, copied, turned)

        def copy_group(eng_copy, t, g):
            k0, k1 = groups[g][0], groups[g][-1] + 1
            r = key_rows(k1 - 1) if k1 - k0 == 1 else P
            return eng_copy(PT[0:r, t % 2, k0:k1, :], ring[g % 2][0:r, 0:(k1 - k0) * P].rearrange("p (k c) -> p k c", c=P))

        @block.scalar
        def _(act):
            act.dma_start(bias[:], dram["fside"].rearrange("(t p) s -> p t s", p=P)).then_inc(bias_loaded, 16)
            act.wait_ge(loaded, 64)
            for n in range(6):
                kind, h = n // 2, n % 2
                act.wait_ge(w_product, n + 1)
                if kind == 2:
                    o = nc.scalar.activation(b12[:, h:h + 1], ring[h][:, 0:1], ACT.Identity, bias=b2[:, h:h + 1])
                else:
                    o = nc.scalar.activation((W12T if kind == 0 else W12)[:, h, :], ring[h][:, 0:D], ACT.Copy)
                o.then_inc(w_copied, 1)
            act.wait_ge(w_copied, 6)

            def exponentials(b, t):
                n = b * TPB + t
                act.wait_ge(max_ready, n + 1)
                nc.scalar.activation(probs[:, t % 2, :], probs[:, t % 2, :], ACT.Exp, bias=neg_top[:, t % 2:t % 2 + 1],
                                     accum_out=total[:, t % 2:t % 2 + 1]).then_inc(probs_ready, 1)

            with act.Fori(0, B // 2) as bb:
                for u in range(2):
                    b = bb * 2 + u
                    for m in range(KD):
                        act.wait_ge(ring_ready, b * RING + m + 1)
                        nc.scalar.activation(qpT[:, m, :], ring[m][:], ACT.Identity, bias=b12[:, m:m + 1]).then_inc(act_copied, 1)
                    for m in range(KD):
                        act.wait_ge(ring_ready, b * RING + m + 3)
                        nc.scalar.activation(q2T[:, m, :], ring[m][:], ACT.Copy, scale=float(D) ** -0.5).then_inc(act_copied, 1)
                    exponentials(b, 0)
                    for t in range(TPB):
                        for g in (1, 3):
                            act.wait_ge(ring_ready, b * RING + 4 + 4 * t + g + 1)
                            copy_group(nc.scalar.copy, t, g).then_inc(act_copied, 1)
                        if t + 1 < TPB:
                            exponentials(b, t + 1)
            for c in range(B):
                copy_turned(nc, act, XT, ring, c, turned, copied)

        @block.gpsimd
        def _(pool):
            norm.setup(pool)
            for c in range(B):
                norm.inverse_deviation(pool, c)

        @block.vector
        def _(dve):
            dve.wait_ge(bias_loaded, 16)

            def maximum(b, t):
                n = b * TPB + t
                dve.wait_ge(scores_ready, n + 1)
                nc.vector.memset(fence[:], 0.0)
                nc.vector.tensor_tensor_reduce(out=probs[:, t % 2, :], in0=scores_ps[:, 0:S2], in1=bias[:, t, :], scale=1.0,
                                               scalar=-3.0e38, op0=ALU.add, op1=ALU.max,
                                               accum_out=top[:, t % 2:t % 2 + 1]).then_inc(scores_read, 1)
                dve.wait_ge(scores_read, n + 1)
                nc.vector.tensor_scalar(neg_top[:, t % 2:t % 2 + 1], top[:, t % 2:t % 2 + 1], -1.0, None, ALU.mult).then_inc(max_ready, 1)

            with dve.Fori(0, B // 2) as bb:
                for u in range(2):
                    b = bb * 2 + u
                    maximum(b, 0)
                    for t in range(TPB):
                        n = b * TPB + t
                        for g in (0, 2):
                            dve.wait_ge(ring_ready, b * RING + 4 + 4 * t + g + 1)
                            copy_group(nc.vector.tensor_copy, t, g).then_inc(dve_copied, 1)
                        if t + 1 < TPB:
                            maximum(b, t + 1)
                        dve.wait_ge(probs_ready, n + 1)
                        nc.vector.reciprocal(inv_total[:, t % 2:t % 2 + 1], total[:, t % 2:t % 2 + 1]).then_inc(inv_ready, 1)
                        dve.wait_ge(inv_ready, n + 1)
                        dve.wait_ge(av_ready, n + 1)
                        x = X[:, ds(n, 1), :].rearrange("p a d -> p (a d)")
                        nc.vector.scalar_tensor_tensor(x, av_ps[:], inv_total[:, t % 2:t % 2 + 1], x, ALU.mult, ALU.add).then_inc(sum_ready, 1)
            for c in range(B):
                norm.statistics(dve, c, sum_ready)
            for c in range(B):
                norm.normalize(dve, c)


def phase_moe(nc, ctx, dram, X, XT, ident):
    sb = lambda n, s, dt=F32: ctx.enter_context(nc.sbuf_tensor(f"C_{n}", s, dt))
    ps = lambda n, s: ctx.enter_context(nc.psum_tensor(f"C_{n}", s, F32))
    sem = lambda n: ctx.enter_context(nc.semaphore(f"C_{n}"))
    Wr, br, lanes = sb("Wr", [P, KD, E]), sb("br", [P, E]), sb("lanes", [P, E])
    logits, best = sb("logits", [P, NT, E]), sb("best", [P, NT])
    top8, index8, index_f = sb("top8", [P, NT, 8]), sb("index8", [P, NT, 8], mybir.dt.uint32), sb("index_f", [P, NT, 2])
    pair_sum, first, second = sb("pair_sum", [P, NT]), sb("first", [P, NT, E]), sb("second", [P, NT, E])
    comb = sb("comb", [P, NT, E])
    bi, bg, half_bg = sb("bi", [P, E, NF]), sb("bg", [P, E, NF]), sb("half_bg", [P, E, NF])
    Wi, Wg, Wo = (sb(n, [P, 2, KD * F]) for n in ("Wi", "Wg", "Wo"))
    tail = sb("tail", [P, 2, 3, D])
    gelu, gate = sb("gelu", [P, 2, S]), sb("gate", [P, 2, S])
    hT = sb("hT", [P, NF, S])
    R = sb("R", [P, TPB, D])
    N = sb("N", [P, 2, D])
    OUT = sb("OUT", [P, NT, D])
    stats, mv, ve, rstd = sb("stats", [P, TPB, 6]), sb("mv", [P, TPB, 2]), sb("ve", [P, TPB]), sb("rstd", [P, TPB])
    neg_half, eps, fence = sb("neg_half", [P, 1]), sb("eps", [P, 1]), sb("fence", [P, 1])
    router_ps = ps("router", [P, NT * E])
    yi_ps, yg_ps, y2_ps = ([ps(f"{n}{i}", [P, w]) for i in range(2)] for n, w in (("yi", S), ("yg", S), ("y2", D)))

    norm = Norm(ctx, nc, "C_norm", OUT, LN_EPS)
    loaded = sem("loaded")
    w_loaded = [sem(f"w_loaded{u}") for u in range(2)]
    routed, r_step, exp_ready, comb_ready = sem("routed"), sem("r_step"), sem("exp_ready"), sem("comb_ready")
    bias_scaled, out_started = sem("bias_scaled"), sem("out_started")
    yi_ready, yg_ready, gelu_ready, gate_ready = sem("yi_ready"), sem("yg_ready"), sem("gelu_ready"), sem("gate_ready")
    act_ready = sem("act_ready")
    base_ready, y2_ready, r_ready = sem("base_ready"), sem("y2_ready"), sem("r_ready")
    stats_ready, mv_ready, ve_ready, rstd_ready = sem("stats_ready"), sem("mv_ready"), sem("ve_ready"), sem("rstd_ready")
    n_ready, g_ready, b_ready, mixed = sem("n_ready"), sem("g_ready"), sem("b_ready"), sem("mixed")
    half_ready = sem("half_ready")
    turned, copied = sem("turned"), sem("copied")
    turn_ps = yi_ps

    with nc.Block() as block:
        @block.sync
        def _(sp):
            for t, n in ((Wr, "L0_ffn_Wr"), (br, "L0_ffn_br"), (lanes, "lanes"), (bi, "L0_ffn_bi"), (bg, "L0_ffn_bg")):
                sp.dma_start(t[:], dram[n]).then_inc(loaded, 16)

            def load(e, u):
                one = ds(e, 1)
                sp.dma_start(Wi[:, u, :].rearrange("p (k f) -> p k f", k=KD), dram["L0_ffn_Wi"][one].rearrange("e (k p) f -> p (e k) f", p=P)).then_inc(w_loaded[u], 16)
                sp.dma_start(Wg[:, u, :].rearrange("p (k f) -> p k f", k=KD), dram["L0_ffn_Wg"][one].rearrange("e (k p) f -> p (e k) f", p=P)).then_inc(w_loaded[u], 16)
                sp.dma_start(Wo[:, u, :].rearrange("p (k f) -> p k f", k=NF), dram["L0_ffn_Wo"][one].rearrange("e (k p) f -> p (e k) f", p=P)).then_inc(w_loaded[u], 16)
                sp.dma_start(tail[:, u], dram["expert_tail"][:, one].rearrange("q e r d -> q (e r) d")).then_inc(w_loaded[u], 16)

            for u in range(2):
                load(u, u)
            with sp.Fori(0, E // 2 - 1) as ee:
                for u in range(2):
                    sp.wait_ge(mixed, (ee * 2 + u + 1) * NT)
                    load(ee * 2 + 2 + u, u)

        @block.tensor
        def _(pe):
            mm = nc.tensor.matmul
            pe.wait_ge(loaded, 80)
            for t in range(NT):
                for k in range(KD):
                    last = mm(router_ps[:, t * E:(t + 1) * E], XT[:, k, t * P:(t + 1) * P], Wr[:, k, :], start=(k == 0), stop=(k == KD - 1))
            last.then_inc(routed, 1)
            with pe.Fori(0, E // 2) as ee:
                for u in range(2):
                    with pe.Fori(0, B) as c:
                        pe.wait_ge(w_loaded[u], ee * 64 + 64)
                        it = (ee * 2 + u) * B + c
                        for j in range(NF):
                            n = it * NF + j
                            if j >= 2:
                                pe.wait_ge(gate_ready, n - 1)
                            for w, banks, ready in ((Wi, yi_ps, yi_ready), (Wg, yg_ps, yg_ready)):
                                for k in range(KD):
                                    last = mm(banks[j % 2][:], w[:, u, k * F + j * P:k * F + (j + 1) * P], XT[:, k, ds(c * S, S)],
                                              start=(k == 0), stop=(k == KD - 1))
                                last.then_inc(ready, 1)
                        for t in range(TPB):
                            n = it * TPB + t
                            pe.wait_ge(r_ready, n - 1) if t >= 2 else None
                            for j in range(NF):
                                if t == 0:
                                    pe.wait_ge(act_ready, it * NF + j + 1)
                                last = mm(y2_ps[t % 2][:], hT[:, j, t * P:(t + 1) * P], Wo[:, u, j * D:(j + 1) * D],
                                          start=(j == 0), stop=(j == NF - 1))
                            last.then_inc(y2_ready, 1)
                        pe.wait_ge(r_ready, (it + 1) * TPB)
            for c in range(B):
                turn_group(nc, pe, X, ident[:], turn_ps, c, norm.normed, copied, turned)

        @block.scalar
        def _(act):
            act.wait_ge(r_step, 2)
            nc.scalar.activation(logits[:], logits[:], ACT.Exp).then_inc(exp_ready, 1)
            act.wait_ge(bias_scaled, 1)
            with act.Fori(0, E) as e:
                with act.Fori(0, B) as c:
                    for j in range(NF):
                        n = (e * B + c) * NF + j
                        act.wait_ge(yi_ready, n + 1)
                        if j >= 2:
                            act.wait_ge(act_ready, n - 1)
                        b = bi[:, ds(e, 1), j:j + 1].rearrange("p a b -> p (a b)")
                        nc.scalar.activation(gelu[:, j % 2, :], yi_ps[j % 2][:], ACT.Gelu, bias=b).then_inc(gelu_ready, 1)
                        act.wait_ge(yg_ready, n + 1)
                        b = half_bg[:, ds(e, 1), j:j + 1].rearrange("p a b -> p (a b)")
                        nc.scalar.activation(gate[:, j % 2, :], yg_ps[j % 2][:], ACT.Tanh, bias=b, scale=0.5).then_inc(gate_ready, 1)
            for c in range(B):
                copy_turned(nc, act, XT, turn_ps, c, turned, copied)

        @block.gpsimd
        def _(pool):
            norm.setup(pool)
            nc.gpsimd.memset(neg_half[:], -0.5).then_inc(half_ready, 1)
            nc.gpsimd.memset(eps[:], 1e-12).then_inc(half_ready, 1)
            pool.wait_ge(half_ready, 2)
            for c in range(B):
                nc.gpsimd.tensor_copy(OUT[:, c * TPB:(c + 1) * TPB, :], X[:, c * TPB:(c + 1) * TPB, :]).then_inc(out_started, 1)
            with pool.Fori(0, E // 2) as ee:
                for u in range(2):
                    with pool.Fori(0, B) as c:
                        pool.wait_ge(w_loaded[u], ee * 64 + 64)
                        it = (ee * 2 + u) * B + c
                        pool.wait_ge(n_ready, it * TPB)
                        for t in range(TPB):
                            nc.gpsimd.tensor_tensor(R[:, t, :], X[:, ds(c * TPB + t, 1), :].rearrange("p a d -> p (a d)"),
                                                    tail[:, u, 0, :], ALU.add).then_inc(base_ready, 1)
                        for t in range(TPB):
                            n = it * TPB + t
                            pool.wait_ge(mv_ready, n + 1)
                            nc.gpsimd.tensor_tensor(ve[:, t:t + 1], mv[:, t, 1:2], eps[:], ALU.add).then_inc(ve_ready, 1)
                            pool.wait_ge(ve_ready, n + 1)
                            nc.gpsimd.tensor_tensor(rstd[:, t:t + 1], ve[:, t:t + 1], neg_half[:], ALU.pow).then_inc(rstd_ready, 1)
            for c in range(B):
                norm.inverse_deviation(pool, c)

        @block.vector
        def _(dve):
            v = nc.vector
            dve.wait_ge(loaded, 80)
            v.tensor_scalar(half_bg[:], bg[:], 0.5, None, ALU.mult).then_inc(bias_scaled, 1)
            dve.wait_ge(routed, 1)
            v.tensor_tensor(logits[:], router_ps[:].rearrange("p (t e) -> p t e", e=E),
                            br[:].rearrange("p (a e) -> p a e", a=1).broadcast_to([P, NT, E]), ALU.add).then_inc(r_step, 1)
            dve.wait_ge(r_step, 1)
            v.tensor_reduce(best[:], logits[:], AX_X, ALU.max).then_inc(comb_ready, 1)
            dve.wait_ge(comb_ready, 1)
            v.tensor_tensor(logits[:], logits[:], best[:].rearrange("p (t a) -> p t a", a=1).broadcast_to([P, NT, E]), ALU.subtract).then_inc(r_step, 1)
            dve.wait_ge(exp_ready, 1)
            for t in range(NT):
                v.max(top8[:, t, :], logits[:, t, :]).then_inc(comb_ready, 1)
            dve.wait_ge(comb_ready, 1 + NT)
            for t in range(NT):
                v.max_index(index8[:, t, :], top8[:, t, :], logits[:, t, :]).then_inc(comb_ready, 1)
            v.tensor_tensor(pair_sum[:], top8[:, :, 0], top8[:, :, 1], ALU.add).then_inc(comb_ready, 1)
            dve.wait_ge(comb_ready, 2 + 2 * NT)
            v.tensor_copy(index_f[:], index8[:, :, 0:2]).then_inc(comb_ready, 1)
            v.reciprocal(pair_sum[:], pair_sum[:]).then_inc(comb_ready, 1)
            dve.wait_ge(comb_ready, 4 + 2 * NT)
            for t in range(NT):
                for q, dst in ((0, first), (1, second)):
                    v.tensor_scalar(dst[:, t, :], lanes[:], index_f[:, t, q:q + 1], top8[:, t, q:q + 1], ALU.is_equal, ALU.mult).then_inc(comb_ready, 1)
            dve.wait_ge(comb_ready, 4 + 4 * NT)
            v.tensor_tensor(first[:], first[:], second[:], ALU.add).then_inc(comb_ready, 1)
            dve.wait_ge(comb_ready, 5 + 4 * NT)
            v.tensor_tensor(comb[:], first[:], pair_sum[:].rearrange("p (t a) -> p t a", a=1).broadcast_to([P, NT, E]), ALU.mult).then_inc(comb_ready, 1)
            dve.wait_ge(comb_ready, 6 + 4 * NT)
            dve.wait_ge(out_started, B)

            with dve.Fori(0, E // 2) as ee:
                for u in range(2):
                    e = ee * 2 + u
                    with dve.Fori(0, B) as c:
                        it = e * B + c
                        for j in range(NF):
                            n = it * NF + j
                            dve.wait_ge(gelu_ready, n + 1)
                            dve.wait_ge(gate_ready, n + 1)
                            v.scalar_tensor_tensor(hT[:, j, :], gate[:, j % 2, :], 1.0, gelu[:, j % 2, :], ALU.add, ALU.mult).then_inc(act_ready, 1)

                        def finish(t):
                            n = it * TPB + t
                            dve.wait_ge(rstd_ready, n + 1)
                            v.tensor_scalar(N[:, t % 2, :], R[:, t, :], mv[:, t, 0:1], rstd[:, t:t + 1], ALU.subtract, ALU.mult).then_inc(n_ready, 1)
                            dve.wait_ge(n_ready, n + 1)
                            v.tensor_tensor(N[:, t % 2, :], N[:, t % 2, :], tail[:, u, 1, :], ALU.mult).then_inc(g_ready, 1)
                            dve.wait_ge(g_ready, n + 1)
                            v.tensor_tensor(N[:, t % 2, :], N[:, t % 2, :], tail[:, u, 2, :], ALU.add).then_inc(b_ready, 1)
                            dve.wait_ge(b_ready, n + 1)
                            o = OUT[:, ds(c * TPB + t, 1), :].rearrange("p a d -> p (a d)")
                            w = comb[:, ds(c * TPB + t, 1), ds(e, 1)].rearrange("p a b -> p (a b)")
                            v.scalar_tensor_tensor(o, N[:, t % 2, :], w, o, ALU.mult, ALU.add).then_inc(mixed, 1)

                        for t in range(TPB):
                            n = it * TPB + t
                            dve.wait_ge(base_ready, n + 1)
                            dve.wait_ge(y2_ready, n + 1)
                            v.scalar_tensor_tensor(R[:, t, :], y2_ps[t % 2][:], 0.5, R[:, t, :], ALU.mult, ALU.add).then_inc(r_ready, 1)
                            dve.wait_ge(r_ready, n + 1)
                            v.bn_stats(stats[:, t, :], R[:, t, :]).then_inc(stats_ready, 1)
                            dve.wait_ge(stats_ready, n + 1)
                            v.memset(fence[:], 0.0)
                            v.bn_aggr(mv[:, t, :], stats[:, t, :]).then_inc(mv_ready, 1)
                            if t > 0:
                                finish(t - 1)
                        finish(TPB - 1)
            dve.wait_ge(mixed, E * NT)
            for c in range(B):
                norm.statistics(dve, c, mixed, (E - 1) * NT)
            for c in range(B):
                norm.normalize(dve, c, X)


PARTS = 3
Q_PARTS = (0, 0, 1, 1, 0, 2)
K_PARTS = (0, 1, 0, 1, 2, 0)
STACK = len(Q_PARTS) * DH
NEG = 2.0 ** 100
UNITS = B * H
SLOTS = 4
VW = DH + 1


class Heads:

    def __init__(self, ctx, nc, name, n_keys, extra, causal, qd, kd, V, ATT, ident16, tri):
        self.nc, self.n_keys, self.causal = nc, n_keys, causal
        self.qd, self.kd, self.V, self.ATT, self.tri = qd, kd, V, ATT, tri
        self.ident_bf, self.ident_half = ident16
        self.R = STACK + extra
        self.tiles = [(kt, min(P, n_keys - kt * P)) for kt in range((n_keys + P - 1) // P)]
        self.groups = [self.tiles[i:i + 2] for i in range(0, len(self.tiles), 2)]
        n_chunks = (n_keys + S - 1) // S
        w = -(-n_keys // n_chunks)
        self.chunks = [(qt, c, min(w, n_keys - c)) for qt in range(TPB) for c in range(0, n_keys, w)]
        self.per_q = n_chunks
        sb = lambda n, s, dt=F32: ctx.enter_context(nc.sbuf_tensor(f"{name}_{n}", s, dt))
        ps = lambda n, s, dt=F32: ctx.enter_context(nc.psum_tensor(f"{name}_{n}", s, dt))
        sem = lambda n: ctx.enter_context(nc.semaphore(f"{name}_{n}"))
        self.KS = sb("KS", [self.R + 2, SLOTS, n_keys], BF16)
        self.QS = sb("QS", [self.R + 2, SLOTS, S], BF16)
        self.probs = sb("probs", [P, 4, 2 * S])
        self.maxima = sb("maxima", [P, TPB, n_chunks])
        self.neg, self.rest = sb("neg", [P, TPB]), sb("rest", [P, TPB])
        self.neg_parts = sb("neg_parts", [P, 2, TPB], BF16)
        self.neg_rows = sb("neg_rows", [2 * TPB, 2, P], BF16)
        self.inv = sb("inv", [P, TPB])
        self.score_ps = [ps(f"score{i}", [P, 2 * S]) for i in range(2)]
        self.max_ps = [ps(f"max{i}", [P, S]) for i in range(2)]
        self.row_ps = ps("row", [2 * TPB, P], BF16)
        self.av_ps = ps("av", [P, TPB * VW])
        self.loaded = [sem(f"loaded{i}") for i in range(SLOTS)]
        self.rows_loaded = [sem(f"rows_loaded{i}") for i in range(SLOTS)]
        self.chunk_ready, self.chunk_read = sem("chunk_ready"), sem("chunk_read")
        self.neg_f, self.neg_a, self.neg_r, self.neg_ready = sem("neg_f"), sem("neg_a"), sem("neg_r"), sem("neg_ready")
        self.rows_turned, self.rows_copied = sem("rows_turned"), sem("rows_copied")
        self.scores_ready, self.probs_ready, self.probs_free = sem("scores_ready"), sem("probs_ready"), sem("probs_free")
        self.inv_ready, self.unit_read = sem("inv_ready"), sem("unit_read")

    def walk(self, eng, step):
        with eng.Fori(0, UNITS // SLOTS - 1) as i:
            for u in range(SLOTS):
                step(i * SLOTS + u, u, True, True, i)
        for u in range(SLOTS):
            s = UNITS - SLOTS + u
            step(s, u, s + 1 < UNITS, s + 2 < UNITS, UNITS // SLOTS - 1)

    def sync(self, sp):
        def load(unit, slot):
            sp.dma_start(self.KS[:, slot, :], self.kd[ds(unit, 1)].rearrange("u r s -> (u r) s")).then_inc(self.loaded[slot], 16)
            sp.dma_start(self.QS[0:self.R, slot, :], self.qd[ds(unit, 1)].rearrange("u r s -> (u r) s")).then_inc(self.loaded[slot], 16)

        def rows(unit, slot, two):
            sp.wait_ge(self.rows_copied, unit + 1)
            sp.dma_start(self.QS[self.R:self.R + 2, slot, :].rearrange("a (t q) -> a t q", q=P),
                         self.neg_rows[:, two, :]).then_inc(self.rows_loaded[slot], 16)

        for u in range(SLOTS):
            load(u, u)
        rows(0, 0, 0)

        def step(s, u, has_next, has_max, i):
            if has_next:
                rows(s + 1, (u + 1) % SLOTS, (u + 1) % 2)
            if isinstance(s, int):
                return
            sp.wait_ge(self.probs_free, 4 + (s + 1) * len(self.groups))
            load(s + SLOTS, u)

        self.walk(sp, step)

    def max_chunk(self, pe, unit, slot, m):
        nc = self.nc
        qt, c, w = self.chunks[m]
        n = unit * len(self.chunks) + m
        if not isinstance(unit, int) or n >= 2:
            pe.wait_ge(self.chunk_read, n - 1)
        out = self.max_ps[m % 2]
        last = nc.tensor.matmul(out[:, 0:w], self.QS[0:self.R, slot, qt * P:(qt + 1) * P], self.KS[0:self.R, slot, c:c + w],
                                start=True, stop=True)
        if self.causal:
            last = nc.tensor.matmul(out[:, qt * P:(qt + 1) * P], self.ident_half[:], self.tri[:, 0, :], start=False, stop=True,
                                    skip_group_check=True)
        last.then_inc(self.chunk_ready, 1)

    def wait_loaded(self, pe, slot, round_):
        pe.wait_ge(self.loaded[slot], round_ * 32 + 32)

    def turn_rows(self, pe, unit):
        pe.wait_ge(self.neg_ready, unit + 1)
        if not isinstance(unit, int) or unit >= 1:
            pe.wait_ge(self.rows_copied, unit)
        self.nc.tensor.transpose(self.row_ps[:], self.neg_parts[:].rearrange("p a t -> p (a t)"), self.ident_bf[:]).then_inc(self.rows_turned, 1)

    def tensor(self, pe):
        nc = self.nc
        NG, NCH = len(self.groups), len(self.chunks)
        assert (SLOTS * NG) % 4 == 0
        pe.sem_inc(self.probs_free, 4)
        for unit in range(2):
            self.wait_loaded(pe, unit, 0)
            for m in range(NCH):
                self.max_chunk(pe, unit, unit, m)
            if unit == 0:
                self.turn_rows(pe, 0)

        def scores(s, u, g):
            n = s * NG + g
            pe.wait_ge(self.probs_ready, n - 1 if g else n)
            bank = self.score_ps[(u * NG + g) % 2]
            for q, (kt, r) in enumerate(self.groups[g]):
                o = bank[0:r, q * S:(q + 1) * S]
                last = nc.tensor.matmul(o, self.KS[:, u, kt * P:kt * P + r], self.QS[:, u, :], start=True, stop=True)
                if self.causal:
                    last = nc.tensor.matmul(bank[:, q * S + kt * P:q * S + (kt + 1) * P], self.ident_half[:], self.tri[:, 1, :],
                                            start=False, stop=True, skip_group_check=True)
            last.then_inc(self.scores_ready, 1)

        def values(s, u, g):
            n = s * NG + g
            pe.wait_ge(self.probs_ready, n + 1)
            if g == 0:
                pe.wait_ge(self.unit_read, s)
            for q, (kt, r) in enumerate(self.groups[g]):
                for qt in range(TPB):
                    last = nc.tensor.matmul(self.av_ps[:, qt * VW:(qt + 1) * VW],
                                            self.probs[0:r, (u * NG + g) % 4, q * S + qt * P:q * S + (qt + 1) * P],
                                            self.V[0:r, kt, ds(s * VW, VW)],
                                            start=(kt == 0 and qt == 0), stop=(kt == len(self.tiles) - 1), skip_group_check=True)
            last.then_inc(self.probs_free, 1)

        def step(s, u, has_next, has_max, i):
            pe.wait_ge(self.rows_loaded[u], i * 16 + 16)
            scores(s, u, 0)
            if NG > 1:
                scores(s, u, 1)
            if has_next:
                self.turn_rows(pe, s + 1)
            m = 0
            if has_max:
                slot = (u + 2) % SLOTS
                self.wait_loaded(pe, slot, i + (1 if u >= 2 else 0))
            for g in range(NG):
                quota = (NCH * (g + 2)) // (NG + 1) if has_max else 0
                while m < quota:
                    self.max_chunk(pe, s + 2, (u + 2) % SLOTS, m)
                    m += 1
                values(s, u, g)
                if g + 2 < NG:
                    scores(s, u, g + 2)

        self.walk(pe, step)

    def scalar(self, act):
        nc = self.nc
        NG = len(self.groups)

        def step(s, u, has_next, has_max, i):
            for g, group in enumerate(self.groups):
                n = s * NG + g
                act.wait_ge(self.scores_ready, n + 1)
                act.wait_ge(self.probs_free, n + 1)
                r, w = group[-1][1], len(group) * S
                nc.scalar.activation(self.probs[0:r, (u * NG + g) % 4, 0:w], self.score_ps[(u * NG + g) % 2][0:r, 0:w],
                                     ACT.Exp).then_inc(self.probs_ready, 1)

        self.walk(act, step)

    def maximum(self, dve, unit, m0, m1):
        nc = self.nc
        for m in range(m0, m1):
            qt, c, w = self.chunks[m]
            dve.wait_ge(self.chunk_ready, unit * len(self.chunks) + m + 1)
            nc.vector.tensor_reduce(self.maxima[:, qt, m % self.per_q:m % self.per_q + 1], self.max_ps[m % 2][:, 0:w], AX_X,
                                    ALU.max).then_inc(self.chunk_read, 1)

    def negate(self, dve, unit):
        nc = self.nc
        v = nc.vector
        dve.wait_ge(self.chunk_read, (unit + 1) * len(self.chunks))
        v.tensor_reduce(self.neg[:], self.maxima[:], AX_X, ALU.max, negate=True).then_inc(self.neg_f, 1)
        dve.wait_ge(self.neg_f, unit + 1)
        if not isinstance(unit, int) or unit >= 1:
            dve.wait_ge(self.rows_turned, unit)
        v.tensor_copy(self.neg_parts[:, 0, :], self.neg[:]).then_inc(self.neg_a, 1)
        dve.wait_ge(self.neg_a, unit + 1)
        v.tensor_tensor(self.neg_parts[:, 1, :], self.neg[:], self.neg_parts[:, 0, :], ALU.subtract).then_inc(self.neg_ready, 1)

    def copy_rows(self, dve, unit, two):
        dve.wait_ge(self.rows_turned, unit + 1)
        self.nc.vector.tensor_copy(self.neg_rows[:, two, :], self.row_ps[:]).then_inc(self.rows_copied, 1)

    def vector(self, dve):
        nc = self.nc
        NCH = len(self.chunks)
        self.maximum(dve, 0, 0, NCH)
        self.negate(dve, 0)
        self.copy_rows(dve, 0, 0)
        self.maximum(dve, 1, 0, NCH)
        self.negate(dve, 1)

        def step(s, u, has_next, has_max, i):
            if has_next:
                dve.wait_ge(self.rows_loaded[(u - 1) % SLOTS], i * 16 + (16 if u >= 1 else 0))
                self.copy_rows(dve, s + 1, (u + 1) % 2)
            if has_max:
                self.maximum(dve, s + 2, 0, NCH)
                self.negate(dve, s + 2)
            dve.wait_ge(self.probs_free, 4 + (s + 1) * len(self.groups))
            av = self.av_ps[:].rearrange("p (t v) -> p t v", v=VW)
            nc.vector.reciprocal(self.inv[:], av[:, :, DH]).then_inc(self.inv_ready, 1)
            dve.wait_ge(self.inv_ready, s + 1)
            nc.vector.tensor_tensor(self.ATT[:, :, ds(s * DH, DH)], av[:, :, 0:DH],
                                    self.inv[:].rearrange("p (t a) -> p t a", a=1).broadcast_to([P, TPB, DH]), ALU.mult).then_inc(self.unit_read, 1)

        self.walk(dve, step)


class Split:

    def __init__(self, ctx, nc, name):
        self.nc = nc
        sb = lambda n, dt: ctx.enter_context(nc.sbuf_tensor(f"{name}_{n}", [P, 2, S], dt))
        sems = lambda n: [ctx.enter_context(nc.semaphore(f"{name}_{n}{i}")) for i in range(2)]
        self.t = sb("t", F32)
        self.parts = [sb(f"part{i}", BF16) for i in range(PARTS)]
        self.t_ready, self.a_ready, self.r_ready, self.b_ready, self.c_ready, self.stored = (
            sems(n) for n in ("t_ready", "a_ready", "r_ready", "b_ready", "c_ready", "stored"))

    def before_t(self, dve, slot, turn):
        dve.wait_ge(self.c_ready[slot], turn)

    def scalar(self, act, slot, turn, w):
        nc, (a, b, _) = self.nc, self.parts
        act.wait_ge(self.stored[slot], turn * 16 * len(Q_PARTS))
        act.wait_ge(self.t_ready[slot], turn + 1)
        nc.scalar.copy(a[:, slot, 0:w], self.t[:, slot, 0:w]).then_inc(self.a_ready[slot], 1)
        act.wait_ge(self.r_ready[slot], turn + 1)
        nc.scalar.copy(b[:, slot, 0:w], self.t[:, slot, 0:w]).then_inc(self.b_ready[slot], 1)

    def pool(self, pool, slot, turn, w):
        nc, (a, b, c) = self.nc, self.parts
        t = self.t[:, slot, 0:w]
        pool.wait_ge(self.a_ready[slot], turn + 1)
        nc.gpsimd.tensor_tensor(t, t, a[:, slot, 0:w], ALU.subtract).then_inc(self.r_ready[slot], 1)
        pool.wait_ge(self.b_ready[slot], turn + 1)
        nc.gpsimd.tensor_tensor(c[:, slot, 0:w], t, b[:, slot, 0:w], ALU.subtract).then_inc(self.c_ready[slot], 1)

    def sync(self, sp, slot, turn, w, dst, order, unit0, c0):
        sp.wait_ge(self.c_ready[slot], turn + 1)
        for block, part in enumerate(order):
            sp.dma_start(dst[ds(unit0, P // DH), block * DH:(block + 1) * DH, ds(c0, w)],
                         self.parts[part][:, slot, 0:w]).then_inc(self.stored[slot], 16)


def project_out(nc, ctx, name, X, XT, ATT, ident, WoT, bo):
    sem = lambda n: ctx.enter_context(nc.semaphore(f"{name}_{n}"))
    ps = [ctx.enter_context(nc.psum_tensor(f"{name}_out{i}", [P, S], F32)) for i in range(8)]
    turn_ps, out_ps, back_ps = ps[0:2], ps[2:6], ps[6:8]
    norm = Norm(ctx, nc, f"{name}_norm", X, LN_EPS)
    loaded, turned, copied = sem("loaded"), sem("turned"), sem("copied")
    out_ready, base_ready, sum_ready, turned2, copied2 = sem("out_ready"), sem("base_ready"), sem("sum_ready"), sem("turned2"), sem("copied2")
    WoT_sb = ctx.enter_context(nc.sbuf_tensor(f"{name}_WoT", [P, KD, D], F32))
    bo_sb = ctx.enter_context(nc.sbuf_tensor(f"{name}_bo", [P, D], F32)) if bo is not None else None
    need = 16 if bo is None else 32
    with nc.Block() as block:
        @block.sync
        def _(sp):
            sp.dma_start(WoT_sb[:], WoT.rearrange("(k p) d -> p k d", p=P)).then_inc(loaded, 16)
            if bo is not None:
                sp.dma_start(bo_sb[:], bo.partition_broadcast(P)).then_inc(loaded, 16)

        @block.tensor
        def _(pe):
            def attended(c):
                if c >= 1:
                    pe.wait_ge(copied, KD * c)
                for h in range(KD):
                    for t in range(TPB):
                        last = nc.tensor.transpose(turn_ps[h][:, t * P:(t + 1) * P], ATT[:, t, c * D + h * P:c * D + (h + 1) * P], ident[:])
                    last.then_inc(turned, 1)

            pe.wait_ge(loaded, need)
            for c in range(B + 1):
                if c < B:
                    attended(c)
                if c == 0:
                    continue
                pe.wait_ge(copied, KD * c)
                for t in range((c - 1) * TPB, c * TPB):
                    if t >= TPB:
                        pe.wait_ge(sum_ready, t - TPB + 1)
                    for k in range(KD):
                        last = nc.tensor.matmul(out_ps[t % TPB][:, 0:D], XT[:, k, t * P:(t + 1) * P], WoT_sb[:, k, :],
                                                start=(k == 0), stop=(k == KD - 1))
                    last.then_inc(out_ready, 1)
            for c in range(B):
                turn_group(nc, pe, X, ident[:], back_ps, c, norm.normed, copied2, turned2)

        @block.scalar
        def _(act):
            for c in range(B):
                copy_turned(nc, act, XT, turn_ps, c, turned, copied)
            act.wait_ge(out_ready, NT)
            for c in range(B):
                copy_turned(nc, act, XT, back_ps, c, turned2, copied2)

        @block.gpsimd
        def _(pool):
            norm.setup(pool)
            for c in range(B):
                norm.inverse_deviation(pool, c)

        @block.vector
        def _(dve):
            if bo is not None:
                dve.wait_ge(loaded, need)
                for t in range(NT):
                    nc.vector.tensor_tensor(X[:, t, :], X[:, t, :], bo_sb[:], ALU.add).then_inc(base_ready, 1)
                dve.wait_ge(base_ready, NT)
            for c in range(B):
                for t in range(c * TPB, (c + 1) * TPB):
                    dve.wait_ge(out_ready, t + 1)
                    nc.vector.tensor_tensor(X[:, t, :], out_ps[t % TPB][:, 0:D], X[:, t, :], ALU.add).then_inc(sum_ready, 1)
                norm.statistics(dve, c, sum_ready)
            for c in range(B):
                norm.normalize(dve, c)


def narrow_identities(nc, ctx, name):
    return [ctx.enter_context(nc.sbuf_tensor(f"{name}_ident{i}", [P, P], dt)) for i, dt in enumerate((BF16, F16))]


def run_heads(nc, heads):
    with nc.Block() as block:
        @block.sync
        def _(sp):
            heads.sync(sp)

        @block.tensor
        def _(pe):
            heads.tensor(pe)

        @block.scalar
        def _(act):
            heads.scalar(act)

        @block.vector
        def _(dve):
            heads.vector(dve)


CAUSAL = 2 * (TPB - 1)


def phase_self(nc, ctx, dram, X, XT, ident):
    qd = nc.dram_tensor("D_qd", (UNITS, STACK + CAUSAL, S), BF16, kind="Internal").ap()
    kd = nc.dram_tensor("D_kd", (UNITS, STACK + CAUSAL + 2, S), BF16, kind="Internal").ap()
    V = ctx.enter_context(nc.sbuf_tensor("D_V", [P, TPB, UNITS * VW], F32))
    ATT = ctx.enter_context(nc.sbuf_tensor("D_ATT", [P, TPB, UNITS * DH], F32))
    idents = narrow_identities(nc, ctx, "D")
    tri = ctx.enter_context(nc.sbuf_tensor("D_tri", [P, 2, P], F16))
    with ExitStack() as own:
        sb = lambda n, s, dt=F32: own.enter_context(nc.sbuf_tensor(f"D_{n}", s, dt))
        sem = lambda n: ctx.enter_context(nc.semaphore(f"D_{n}"))
        w = sb("w", [P, KD, 3 * D])
        tri_f = sb("tri_f", [P, 2, P])
        rows_f = sb("rows_f", [UNITS, 2 * CAUSAL + 2, S])
        rows_b = sb("rows_b", [UNITS, 2 * CAUSAL + 2, S], BF16)
        banks = [own.enter_context(nc.psum_tensor(f"D_bank{i}", [P, S], F32)) for i in range(4)]
        split = Split(ctx, nc, "D_split") if False else Split(own, nc, "D_split")
        loaded, rows_ready, rows_stored, ones_ready = sem("loaded"), sem("rows_ready"), sem("rows_stored"), sem("ones_ready")
        cast_ready = sem("cast_ready")
        product = [sem(f"product{i}") for i in range(2)]
        v_product, v_copied = sem("v_product"), sem("v_copied")
        items = [(which, hf) for hf in range(KD) for which in range(2)]

        with nc.Block() as block:
            @block.sync
            def _(sp):
                sp.dma_start(w[:], dram["wqkvT"].rearrange("(k p) e -> p k e", p=P)).then_inc(loaded, 16)
                sp.dma_start(tri_f[:], dram["causal_tri"]).then_inc(loaded, 16)
                sp.dma_start(rows_f[:], dram["causal_rows"]).then_inc(loaded, 16)
                with sp.Fori(0, B) as b:
                    for k, (which, hf) in enumerate(items):
                        split.sync(sp, k % 2, b * 2 + k // 2, S, (qd, kd)[which], (Q_PARTS, K_PARTS)[which],
                                   b * H + hf * (H // KD), 0)
                sp.wait_ge(rows_ready, 1)
                sp.dma_start(qd[:, STACK:, :], rows_b[:, 0:CAUSAL, :]).then_inc(rows_stored, 16)
                sp.dma_start(kd[:, STACK:, :], rows_b[:, CAUSAL:, :]).then_inc(rows_stored, 16)
                sp.wait_ge(rows_stored, 32)
                for i in range(2):
                    sp.wait_ge(split.stored[i], 2 * B * 16 * len(Q_PARTS))

            @block.tensor
            def _(pe):
                mm = nc.tensor.matmul
                pe.wait_ge(loaded, 48)
                for t in range(NT):
                    if t >= 2:
                        pe.wait_ge(v_copied, t - 1)
                    for k in range(KD):
                        last = mm(banks[2 + t % 2][:, 0:D], XT[:, k, t * P:(t + 1) * P], w[:, k, 2 * D:3 * D], start=(k == 0), stop=(k == KD - 1))
                    last.then_inc(v_product, 1)
                with pe.Fori(0, B) as b:
                    for n, (which, hf) in enumerate(items):
                        slot, turn = n % 2, b * 2 + n // 2
                        pe.wait_ge(split.t_ready[slot], turn)
                        for k in range(KD):
                            last = mm(banks[slot][:], w[:, k, which * D + hf * P:which * D + (hf + 1) * P], XT[:, k, ds(b * S, S)],
                                      start=(k == 0), stop=(k == KD - 1))
                        last.then_inc(product[slot], 1)

            @block.scalar
            def _(act):
                with act.Fori(0, B) as b:
                    for n in range(len(items)):
                        split.scalar(act, n % 2, b * 2 + n // 2, S)

            @block.gpsimd
            def _(pool):
                nc.gpsimd.memset(V[:].rearrange("p t (u v) -> p t u v", v=VW)[:, :, :, DH], 1.0).then_inc(ones_ready, 1)
                pool.wait_ge(loaded, 48)
                nc.gpsimd.tensor_copy(rows_b[:], rows_f[:]).then_inc(rows_ready, 1)
                with pool.Fori(0, B) as b:
                    for n in range(len(items)):
                        split.pool(pool, n % 2, b * 2 + n // 2, S)

            @block.vector
            def _(dve):
                v = nc.vector
                dve.wait_ge(loaded, 48)
                v.tensor_copy(idents[0][:], ident[:]).then_inc(cast_ready, 1)
                v.tensor_copy(idents[1][:], ident[:]).then_inc(cast_ready, 1)
                v.tensor_copy(tri[:], tri_f[:]).then_inc(cast_ready, 1)
                for t in range(NT):
                    b, kt = divmod(t, TPB)
                    dve.wait_ge(v_product, t + 1)
                    v.tensor_copy(V[:, kt, b * H * VW:(b + 1) * H * VW].rearrange("p (h v) -> p h v", v=VW)[:, :, 0:DH],
                                  banks[2 + t % 2][:, 0:D].rearrange("p (h d) -> p h d", d=DH)).then_inc(v_copied, 1)
                with dve.Fori(0, B) as b:
                    for n, (which, hf) in enumerate(items):
                        slot, turn = n % 2, b * 2 + n // 2
                        split.before_t(dve, slot, turn)
                        dve.wait_ge(product[slot], turn + 1)
                        v.tensor_scalar(split.t[:, slot, :], banks[slot][:], 0.25 if which == 0 else 1.0, None, ALU.mult).then_inc(split.t_ready[slot], 1)

    with ExitStack() as own:
        run_heads(nc, Heads(own, nc, "Dh", S, CAUSAL, True, qd, kd, V, ATT, idents, tri))
    with ExitStack() as own:
        project_out(nc, own, "Do", X, XT, ATT, ident, dram["self_WoT"], None)


def phase_cross1(nc, ctx, dram, X, XT, ident):
    KC = 4
    kw = -(-S2 // KC)
    chunks = [(c * kw, min(kw, S2 - c * kw)) for c in range(KC)]
    qd = nc.dram_tensor("E_qd", (UNITS, STACK + 1, S), BF16, kind="Internal").ap()
    kd = nc.dram_tensor("E_kd", (UNITS, STACK + 3, S2), BF16, kind="Internal").ap()
    V = ctx.enter_context(nc.sbuf_tensor("E_V", [P, NK2, UNITS * VW], F32))
    idents = narrow_identities(nc, ctx, "E")
    with ExitStack() as own:
        sb = lambda n, s, dt=F32: own.enter_context(nc.sbuf_tensor(f"E_{n}", s, dt))
        sem = lambda n: ctx.enter_context(nc.semaphore(f"E_{n}"))
        wq, wqs, wk, wks, wv = (sb(n, [P, KD, D]) for n in ("wq", "wqs", "wk", "wks", "wv"))
        bq, bqs, bk, bks = (sb(n, [P, KD]) for n in ("bq", "bqs", "bk", "bks"))
        bv = sb("bv", [P, D])
        cosq, sinq, cosk, sink = sb("cosq", [P, S]), sb("sinq", [P, S]), sb("cosk", [P, S2]), sb("sink", [P, S2])
        cosm, sinm = sb("cosm", [P, S2]), sb("sinm", [P, S2])
        mask = sb("mask", [P, S2], I32)
        keep = sb("keep", [P, S2])
        ctxT = sb("ctxT", [P, KD, S2])
        mask_row = sb("mask_row", [H, S2], BF16)
        ones = sb("ones", [UNITS, S2], BF16)
        swap = sb("swap", [P, 2, S])
        main_ps = [own.enter_context(nc.psum_tensor(f"E_main{i}", [P, S], F32)) for i in range(2)]
        swap_ps = [own.enter_context(nc.psum_tensor(f"E_swap{i}", [P, S], F32)) for i in range(2)]
        v_ps = [own.enter_context(nc.psum_tensor(f"E_v{i}", [P, D], F32)) for i in range(2)]
        split = Split(own, nc, "E_split")
        loaded, ctx_loaded, mask_loaded = sem("loaded"), sem("ctx_loaded"), sem("mask_loaded")
        ones_ready, rows_stored, row_ready, row_stored = sem("ones_ready"), sem("rows_stored"), sem("row_ready"), sem("row_stored")
        v_ones, cast_ready = sem("v_ones"), sem("cast_ready")
        keep_ready, table_ready = sem("keep_ready"), sem("table_ready")
        product, rotated = [sem(f"product{i}") for i in range(2)], [sem(f"rotated{i}") for i in range(2)]
        v_product, v_copied, keys_done = sem("v_product"), sem("v_copied"), sem("keys_done")
        items = [(0, hf, 0, S) for hf in range(KD)] + [(1, hf, c, w) for hf in range(KD) for c, w in chunks]
        PER = len(items) // 2

        with nc.Block() as block:
            @block.sync
            def _(sp):
                for t, n in ((wq, "wqT"), (wqs, "wqT_swapped"), (wk, "wkT"), (wks, "wkT_swapped"), (wv, "wvT")):
                    sp.dma_start(t[:], dram[n].rearrange("(k p) e -> p k e", p=P)).then_inc(loaded, 16)
                for t, n in ((bq, "bq"), (bqs, "bq_swapped"), (bk, "bk"), (bks, "bk_swapped"), (cosq, "cosq"), (sinq, "sinq"), (cosk, "cosk"), (sink, "sink")):
                    sp.dma_start(t[:], dram[n]).then_inc(loaded, 16)
                sp.dma_start(bv[:], dram["bv"].partition_broadcast(P)).then_inc(loaded, 16)
                sp.wait_ge(ones_ready, 1)
                sp.dma_start(qd[:, STACK, :], ones[:, 0:S]).then_inc(rows_stored, 16)
                for r in (STACK + 1, STACK + 2):
                    sp.dma_start(kd[:, r, :], ones[:]).then_inc(rows_stored, 16)
                with sp.Fori(0, B) as b:
                    sp.wait_ge(keys_done, b)
                    sp.dma_start(ctxT[:], dram["ctxT"][ds(b, 1)].rearrange("b (k p) s -> p (b k) s", p=P)).then_inc(ctx_loaded, 16)
                    sp.wait_ge(table_ready, b * 2)
                    sp.dma_start(mask[:], dram["mask"][ds(b, 1)].rearrange("b r s -> (b r) s")).then_inc(mask_loaded, 16)
                    for n, (which, hf, c, w) in enumerate(items):
                        split.sync(sp, n % 2, b * PER + n // 2, w, (qd, kd)[which], (Q_PARTS, K_PARTS)[which],
                                   b * H + hf * (H // KD), c)
                    sp.wait_ge(row_ready, b + 1)
                    sp.dma_start(kd[ds(b * H, H), STACK, :], mask_row[:]).then_inc(row_stored, 16)
                sp.wait_ge(rows_stored, 48)
                sp.wait_ge(row_stored, 16 * B)
                for i in range(2):
                    sp.wait_ge(split.stored[i], PER * B * 16 * len(Q_PARTS))

            @block.tensor
            def _(pe):
                mm = nc.tensor.matmul
                pe.wait_ge(loaded, 224)
                with pe.Fori(0, B) as b:
                    for n, (which, hf, c, w) in enumerate(items):
                        slot, turn = n % 2, b * PER + n // 2
                        if n == 2:
                            pe.wait_ge(ctx_loaded, b * 16 + 16)
                        pe.wait_ge(rotated[slot], turn)
                        for bank, wt in ((main_ps[slot], (wq, wk)[which]), (swap_ps[slot], (wqs, wks)[which])):
                            for k in range(KD):
                                rhs = XT[:, k, ds(b * S, S)] if which == 0 else ctxT[:, k, c:c + w]
                                last = mm(bank[:, 0:w], wt[:, k, hf * P:(hf + 1) * P], rhs, start=(k == 0), stop=(k == KD - 1))
                        last.then_inc(product[slot], 1)
                    for kt in range(NK2):
                        r = key_rows(kt)
                        pe.wait_ge(v_copied, b * NK2 + kt - 1 if kt >= 2 else b * NK2)
                        for k in range(KD):
                            last = mm(v_ps[kt % 2][0:r, :], ctxT[:, k, kt * P:kt * P + r], wv[:, k, :], start=(k == 0), stop=(k == KD - 1))
                        last.then_inc(v_product, 1)
                    pe.wait_ge(v_copied, (b + 1) * NK2)
                    pe.sem_inc(keys_done, 1)

            @block.scalar
            def _(act):
                with act.Fori(0, B) as b:
                    for n, (which, hf, c, w) in enumerate(items):
                        split.scalar(act, n % 2, b * PER + n // 2, w)

            @block.gpsimd
            def _(pool):
                nc.gpsimd.memset(ones[:], 1.0).then_inc(ones_ready, 1)
                nc.gpsimd.memset(V[:].rearrange("p t (u v) -> p t u v", v=VW)[:, :, :, DH], 1.0).then_inc(v_ones, 1)
                with pool.Fori(0, B) as b:
                    for n, (which, hf, c, w) in enumerate(items):
                        split.pool(pool, n % 2, b * PER + n // 2, w)

            @block.vector
            def _(dve):
                v = nc.vector
                dve.wait_ge(loaded, 224)
                v.tensor_copy(idents[0][:], ident[:]).then_inc(cast_ready, 1)
                v.tensor_copy(idents[1][:], ident[:]).then_inc(cast_ready, 1)
                with dve.Fori(0, B) as b:
                    for n, (which, hf, c, w) in enumerate(items):
                        slot, turn = n % 2, b * PER + n // 2
                        if n == 2:
                            dve.wait_ge(mask_loaded, b * 16 + 16)
                            dve.wait_ge(row_stored, b * 16)
                            v.tensor_scalar(keep[:], mask[:], 0.0, None, ALU.not_equal).then_inc(keep_ready, 1)
                            dve.wait_ge(keep_ready, b + 1)
                            v.tensor_tensor(cosm[:], cosk[:], keep[:], ALU.mult).then_inc(table_ready, 1)
                            v.tensor_tensor(sinm[:], sink[:], keep[:], ALU.mult).then_inc(table_ready, 1)
                            v.tensor_scalar(mask_row[:], keep[0:H, :], 1.0, -NEG, ALU.subtract, ALU.mult).then_inc(row_ready, 1)
                            dve.wait_ge(table_ready, b * 2 + 2)
                        b0, b1 = (bq, bqs) if which == 0 else (bk, bks)
                        cos, sin = (cosq[:, 0:w], sinq[:, 0:w]) if which == 0 else (cosm[:, c:c + w], sinm[:, c:c + w])
                        split.before_t(dve, slot, turn)
                        dve.wait_ge(product[slot], turn + 1)
                        v.scalar_tensor_tensor(split.t[:, slot, 0:w], main_ps[slot][:, 0:w], b0[:, hf:hf + 1], cos, ALU.add, ALU.mult)
                        v.scalar_tensor_tensor(swap[:, slot, 0:w], swap_ps[slot][:, 0:w], b1[:, hf:hf + 1], sin, ALU.add, ALU.mult).then_inc(rotated[slot], 1)
                        dve.wait_ge(rotated[slot], turn + 1)
                        v.tensor_tensor(split.t[:, slot, 0:w], split.t[:, slot, 0:w], swap[:, slot, 0:w], ALU.add).then_inc(split.t_ready[slot], 1)
                    for kt in range(NK2):
                        r = key_rows(kt)
                        dve.wait_ge(v_product, b * NK2 + kt + 1)
                        v.tensor_tensor(V[0:r, kt, ds(b * H * VW, H * VW)].rearrange("p (h v) -> p h v", v=VW)[:, :, 0:DH],
                                        v_ps[kt % 2][0:r, :].rearrange("p (h d) -> p h d", d=DH),
                                        bv[0:r, :].rearrange("p (h d) -> p h d", d=DH), ALU.add).then_inc(v_copied, 1)

    ATT = ctx.enter_context(nc.sbuf_tensor("E_ATT", [P, TPB, UNITS * DH], F32))
    with ExitStack() as own:
        run_heads(nc, Heads(own, nc, "Eh", S2, 1, False, qd, kd, V, ATT, idents, None))
    with ExitStack() as own:
        project_out(nc, own, "Eo", X, XT, ATT, ident, dram["cross_WoT"], dram["bo"])


def phase_ffn(nc, ctx, dram, X, XT, ident, out):
    sb = lambda n, s, dt=F32: ctx.enter_context(nc.sbuf_tensor(f"F_{n}", s, dt))
    ps = lambda n, s: ctx.enter_context(nc.psum_tensor(f"F_{n}", s, F32))
    sem = lambda n: ctx.enter_context(nc.semaphore(f"F_{n}"))

    q1, s1, w1 = sb("q1", [P, KD, F], I32), sb("s1", [P, KD, F]), sb("w1", [P, KD, F])
    q2, s2, w2 = sb("q2", [P, NF, D], I32), sb("s2", [P, NF, D]), sb("w2", [P, NF, D])
    b1, b2 = sb("b1", [P, NF]), sb("b2", [P, D])
    gamma, beta = sb("gamma", [P, KD]), sb("beta", [P, KD])
    XN = sb("XN", [P, NT, D])
    HT = sb("HT", [P, KD, T])
    sig = sb("sig", [P, 2, S])
    act_T = sb("act_T", [P, NF, S])
    turn_ps = [ps(f"turn{h}", [P, S]) for h in range(KD)]
    y1_ps = [ps(f"y1_{i}", [P, S]) for i in range(2)]
    y2_ps = [ps(f"y2_{i}", [P, D]) for i in range(2)]

    norm_in = Norm(ctx, nc, "F_in", X, 1e-5)
    norm_out = Norm(ctx, nc, "F_out", X, LN_EPS)
    loaded1, loaded2, loaded_small = sem("loaded1"), sem("loaded2"), sem("loaded_small")
    w_ready = sem("w_ready")
    turned, copied = sem("turned"), sem("copied")
    y1_ready, sig_ready, act_ready = sem("y1_ready"), sem("sig_ready"), sem("act_ready")
    y2_ready, sum_ready, xb_ready = sem("y2_ready"), sem("sum_ready"), sem("xb_ready")
    half_b2 = sem("half_b2")
    stored = sem("stored")

    with nc.Block() as block:
        @block.sync
        def _(sp):
            sp.dma_start(gamma[:], dram["L1_ffn_ln_gamma"]).then_inc(loaded_small, 16)
            sp.dma_start(beta[:], dram["L1_ffn_ln_beta"]).then_inc(loaded_small, 16)
            sp.dma_start(b1[:], dram["L1_ffn_fc1_bias"]).then_inc(loaded_small, 16)
            sp.dma_start(b2[:], dram["L1_ffn_fc2_bias"].partition_broadcast(P)).then_inc(loaded_small, 16)
            sp.dma_start(q1[:], dram["L1_ffn_fc1_q"].rearrange("(k p) f -> p k f", p=P)).then_inc(loaded1, 16)
            sp.dma_start(s1[:], dram["L1_ffn_fc1_scales"].partition_broadcast(P)).then_inc(loaded1, 16)
            sp.dma_start(q2[:], dram["L1_ffn_fc2_q"].rearrange("(k p) f -> p k f", p=P)).then_inc(loaded2, 16)
            sp.dma_start(s2[:], dram["L1_ffn_fc2_scales"].partition_broadcast(P)).then_inc(loaded2, 16)
            for c in range(B):
                sp.wait_ge(norm_out.normed, (c + 1) * TPB)
                sp.dma_start(out[c * S:(c + 1) * S, :].rearrange("(t p) d -> p t d", p=P),
                             X[:, c * TPB:(c + 1) * TPB, :]).then_inc(stored, 16)
            sp.wait_ge(stored, 16 * B)

        @block.gpsimd
        def _(pool):
            norm_in.setup(pool)
            norm_out.setup(pool)
            for c in range(B):
                norm_in.inverse_deviation(pool, c)
            for c in range(B):
                norm_out.inverse_deviation(pool, c)

        @block.scalar
        def _(act):
            act.wait_ge(loaded_small, 64)
            for c in range(B):
                for h in range(KD):
                    act.wait_ge(turned, KD * c + h + 1)
                    nc.scalar.activation(HT[:, h, c * S:(c + 1) * S], turn_ps[h][:], ACT.Identity,
                                         bias=beta[:, h:h + 1], scale=gamma[:, h:h + 1]).then_inc(copied, 1)
            with act.Fori(0, B) as c:
                for j in range(NF):
                    n = c * NF + j
                    act.wait_ge(y1_ready, n + 1)
                    if j >= 2:
                        act.wait_ge(act_ready, n - 1)
                    nc.scalar.activation(sig[:, j % 2, :], y1_ps[j % 2][:], ACT.Sigmoid,
                                         bias=b1[:, j:j + 1]).then_inc(sig_ready, 1)

        @block.vector
        def _(dve):
            for c in range(B):
                for t in range(c * TPB, (c + 1) * TPB):
                    nc.vector.bn_stats(norm_in.stats_buf[:, t, :], X[:, t, :]).then_inc(norm_in.stats_ready, 1)
                for t in range(c * TPB, (c + 1) * TPB):
                    dve.wait_ge(norm_in.stats_ready, t + 1)
                    nc.vector.bn_aggr(norm_in.mv[:, t, :], norm_in.stats_buf[:, t, :]).then_inc(norm_in.mv_ready, 1)
            dve.wait_ge(loaded1, 32)
            nc.vector.scalar_tensor_tensor(w1[:].rearrange("p k f -> p (k f)"), q1[:].rearrange("p k f -> p (k f)"), -128.0, s1[:].rearrange("p k f -> p (k f)"), ALU.add, ALU.mult).then_inc(w_ready, 1)
            for c in range(B):
                norm_in.normalize(dve, c, XN)
            dve.wait_ge(loaded2, 32)
            nc.vector.scalar_tensor_tensor(w2[:].rearrange("p k f -> p (k f)"), q2[:].rearrange("p k f -> p (k f)"), -128.0, s2[:].rearrange("p k f -> p (k f)"), ALU.add, ALU.mult).then_inc(w_ready, 1)
            dve.wait_ge(loaded_small, 64)
            nc.vector.tensor_scalar(b2[:], b2[:], 0.5, None, ALU.mult).then_inc(half_b2, 1)
            dve.wait_ge(half_b2, 1)
            for t in range(NT):
                nc.vector.scalar_tensor_tensor(X[:, t, :], X[:, t, :], 2.0, b2[:], ALU.mult, ALU.add).then_inc(xb_ready, 1)
            dve.wait_ge(xb_ready, NT)
            with dve.Fori(0, B) as c:
                for j in range(NF):
                    n = c * NF + j
                    dve.wait_ge(sig_ready, n + 1)
                    nc.vector.scalar_tensor_tensor(act_T[:, j, :], y1_ps[j % 2][:], b1[:, j:j + 1], sig[:, j % 2, :],
                                                   ALU.add, ALU.mult).then_inc(act_ready, 1)
                for t in range(TPB):
                    n = c * TPB + t
                    dve.wait_ge(y2_ready, n + 1)
                    x = X[:, ds(n, 1), :].rearrange("p a d -> p (a d)")
                    nc.vector.scalar_tensor_tensor(x, y2_ps[t % 2][:], 0.5, x, ALU.mult, ALU.add).then_inc(sum_ready, 1)
            for c in range(B):
                norm_out.statistics(dve, c, sum_ready)
            for c in range(B):
                norm_out.normalize(dve, c)

        @block.tensor
        def _(pe):
            for c in range(B):
                turn_group(nc, pe, XN, ident[:], turn_ps, c, norm_in.normed, copied, turned)
            pe.wait_ge(copied, KD * B)
            pe.wait_ge(w_ready, 2)
            with pe.Fori(0, B) as c:
                for j in range(NF):
                    n = c * NF + j
                    if j >= 2:
                        pe.wait_ge(act_ready, n - 1)
                    for k in range(KD):
                        last = nc.tensor.matmul(y1_ps[j % 2][:], w1[:, k, j * P:(j + 1) * P], HT[:, k, ds(c * S, S)],
                                                start=(k == 0), stop=(k == KD - 1))
                    last.then_inc(y1_ready, 1)
                pe.wait_ge(act_ready, (c + 1) * NF)
                for t in range(TPB):
                    n = c * TPB + t
                    if t >= 2:
                        pe.wait_ge(sum_ready, n - 1)
                    for j in range(NF):
                        last = nc.tensor.matmul(y2_ps[t % 2][:], act_T[:, j, t * P:(t + 1) * P], w2[:, j, :],
                                                start=(j == 0), stop=(j == NF - 1))
                    last.then_inc(y2_ready, 1)
                pe.wait_ge(sum_ready, (c + 1) * TPB)


def lay_out(a, rows, columns):
    x = a["x"].reshape(T, D)
    i, j = np.meshgrid(np.arange(P), np.arange(P))
    quadrant = [((i >> m + 1) == (j >> m + 1)) & ((i >> m) % 2 == 1) & ((j >> m) % 2 == 0) for m in range(LEVELS)]
    ttt_masks = np.stack([q.astype(np.float32) for q in quadrant] + [quadrant[0].T.astype(np.float32),
                         np.where(j <= i, -ETA, 0.0).astype(np.float32)], axis=1)
    causal_tri = np.where(np.stack([i > j, j > i], axis=1), -10000.0, 0.0).astype(np.float32)
    block = np.arange(S) // P
    q_rows = [(block == t) * 1.0 for t in range(TPB - 1) for _ in range(2)]
    k_rows = [(block > t) * v for t in range(TPB - 1) for v in (-9984.0, -16.0)] + [np.ones(S)] * 2
    causal_rows = np.tile(np.array(q_rows + k_rows, np.float32), (UNITS, 1, 1))
    swapped = np.arange(D) ^ 1
    inv_freq = (1.0 / 10000.0 ** (np.arange(0, DH, 2, dtype=np.float32) / np.float32(DH))).astype(np.float32)
    angle = np.arange(S2, dtype=np.float32)[None, :] * np.concatenate([inv_freq, inv_freq])[:, None]
    sign = np.where(np.arange(DH) % 2 == 0, -1.0, 1.0)[:, None]
    cos = np.tile(np.cos(angle.astype(np.float64)), (P // DH, 1)).astype(np.float32)
    sin = np.tile(np.sin(angle.astype(np.float64)) * sign, (P // DH, 1)).astype(np.float32)
    laid = {
        "ttt_masks": ttt_masks,
        "L0_xattn_W1": a["L0_xattn_W1"], "xW2T": a["L0_xattn_W2"].T,
        "L0_xattn_b1": columns(a["L0_xattn_b1"]), "L0_xattn_b2": columns(a["L0_xattn_b2"]),
        "ctx": a["ctx_1024"], "ctxT": a["ctx_1024"].transpose(0, 2, 1), "fside": a["fside_1xSxS2_0"][0],
        "L0_ffn_Wr": a["L0_ffn_Wr"].reshape(KD, P, E).transpose(1, 0, 2), "L0_ffn_br": np.tile(a["L0_ffn_br"], (P, 1)),
        "lanes": np.tile(np.arange(E, dtype=np.float32), (P, 1)),
        "L0_ffn_bi": a["L0_ffn_bi"].reshape(E, NF, P).transpose(2, 0, 1),
        "L0_ffn_bg": a["L0_ffn_bg"].reshape(E, NF, P).transpose(2, 0, 1),
        "L0_ffn_Wi": a["L0_ffn_Wi"], "L0_ffn_Wg": a["L0_ffn_Wg"], "L0_ffn_Wo": a["L0_ffn_Wo"],
        "expert_tail": np.tile(np.stack([a["L0_ffn_bo"], a["L0_ffn_gamma"], a["L0_ffn_beta"]], axis=1), (P, 1, 1, 1)),
        "wqkvT": a["L1_attn_w_qkv"].T, "self_WoT": a["L1_attn_w_out"].T,
        "causal_tri": causal_tri, "causal_rows": causal_rows,
        "wqT": a["L1_xattn_Wq"].T, "wqT_swapped": a["L1_xattn_Wq"].T[:, swapped],
        "wkT": a["L1_xattn_Wk"].T, "wkT_swapped": a["L1_xattn_Wk"].T[:, swapped], "wvT": a["L1_xattn_Wv"].T,
        "bq": columns(a["L1_xattn_bq"]), "bq_swapped": columns(a["L1_xattn_bq"][swapped]),
        "bk": columns(a["L1_xattn_bk"]), "bk_swapped": columns(a["L1_xattn_bk"][swapped]),
        "bv": a["L1_xattn_bv"], "bo": a["L1_xattn_bo"], "cross_WoT": a["L1_xattn_Wo"].T,
        "cosq": cos[:, :S] * np.float32(0.25), "sinq": sin[:, :S] * np.float32(0.25), "cosk": cos, "sink": sin,
        "mask": np.repeat(a["mask_BxS2_if1"][:, None, :], P, axis=1),
        "thKT": a["L0_attn_theta_K"].T, "thQT": a["L0_attn_theta_Q"].T, "thVT": a["L0_attn_theta_V"].T,
        "L0_attn_theta_K": a["L0_attn_theta_K"], "L0_attn_theta_Q": a["L0_attn_theta_Q"],
        "W0T": a["L0_attn_W0"].T, "L0_attn_b0": a["L0_attn_b0"],
        "identity": np.eye(P, dtype=np.float32),
        "x": x,
        "xT": x.T,
        "L1_ffn_ln_gamma": columns(a["L1_ffn_ln_gamma"]),
        "L1_ffn_ln_beta": columns(a["L1_ffn_ln_beta"]),
        "L1_ffn_fc1_q": a["L1_ffn_fc1_q"],
        "L1_ffn_fc1_scales": a["L1_ffn_fc1_scales"],
        "L1_ffn_fc1_bias": columns(a["L1_ffn_fc1_bias"]),
        "L1_ffn_fc2_q": a["L1_ffn_fc2_q"],
        "L1_ffn_fc2_scales": a["L1_ffn_fc2_scales"],
        "L1_ffn_fc2_bias": a["L1_ffn_fc2_bias"],
    }
    return laid


def phase_load(nc, ctx, dram, X, XT, ident):
    loaded = ctx.enter_context(nc.semaphore("load_loaded"))
    with nc.Block() as block:
        @block.sync
        def _(sp):
            sp.dma_start(ident[:], dram["identity"]).then_inc(loaded, 16)
            sp.dma_start(XT[:], dram["xT"].rearrange("(k p) t -> p k t", p=P)).then_inc(loaded, 16)
            sp.dma_start(X[:], dram["x"].rearrange("(t p) d -> p t d", p=P)).then_inc(loaded, 16)
            sp.wait_ge(loaded, 48)


def phase_store(nc, ctx, X, out):
    stored = ctx.enter_context(nc.semaphore("store_stored"))
    with nc.Block() as block:
        @block.sync
        def _(sp):
            sp.dma_start(out.rearrange("(t p) d -> p t d", p=P), X[:]).then_inc(stored, 16)
            sp.wait_ge(stored, 16)


def renew_semaphores(nc):
    released = nc.released_uncleared_semaphores
    nc.all_engine_barrier(sems_to_clear=range(min(released), max(released) + 1))


def build_program(nc, dram, out):
    with ExitStack() as ctx:
        X = ctx.enter_context(nc.sbuf_tensor("X", [P, NT, D], F32))
        XT = ctx.enter_context(nc.sbuf_tensor("XT", [P, KD, T], F32))
        ident = ctx.enter_context(nc.sbuf_tensor("ident", [P, P], F32))
        phase_load(nc, ctx, dram, X, XT, ident)
        table = {"A": phase_ttt, "B": phase_cross0, "C": phase_moe, "D": phase_self, "E": phase_cross1}
        for name in PHASES:
            with ExitStack() as own:
                if name == "F":
                    phase_ffn(nc, own, dram, X, XT, ident, out)
                else:
                    table[name](nc, own, dram, X, XT, ident)
            renew_semaphores(nc)
        if "F" not in PHASES:
            phase_store(nc, ctx, X, out)


def kernel(**inputs):
    import concourse.bacc as bacc
    from concourse.bass_utils import run_bass_kernel_spmd

    a = {k: np.asarray(v) for k, v in inputs.items()}
    rows = lambda v: v.reshape(1, -1)
    columns = lambda v: np.ascontiguousarray(v.reshape(-1, P).T)
    laid = lay_out(a, rows, columns)
    nc = bacc.Bacc("TRN2", target_bir_lowering=False, num_devices=1)
    arrays, dram = {}, {}
    for name, v in laid.items():
        v = np.ascontiguousarray(v)
        arrays[f"in_{name}_dram"] = v
        dram[name] = nc.dram_tensor(f"in_{name}_dram", v.shape, mybir.dt.from_np(v.dtype), kind="ExternalInput").ap()
    out = nc.dram_tensor("out_0_dram", (T, D), F32, kind="ExternalOutput").ap()
    build_program(nc, dram, out)
    r = run_bass_kernel_spmd(nc, [arrays], core_ids=[0])
    return r.results[0]["out_0_dram"].reshape(B, S, D)
```

```python
from contextlib import ExitStack

import numpy as np

import concourse.bass as bass
from concourse import mybir

P = 128
B, S, D = 4, 512, 256
T = B * S
NT = T // P
KD = D // P
TPB = S // P
S2 = 1601
NK2 = (S2 + P - 1) // P
F = 1024
NF = F // P
E = 8
H, DH = 16, 16
LN_EPS = 1e-5

F32 = mybir.dt.float32
F16 = mybir.dt.float16
BF16 = mybir.dt.bfloat16
I32 = mybir.dt.int32
ALU = mybir.AluOpType
ACT = mybir.ActivationFunctionType
AX_X = mybir.AxisListType.X
ds = bass.ds

PHASES = "ABCDEF"


class Norm:

    def __init__(self, ctx, nc, name, X, eps):
        self.nc, self.X, self.eps = nc, X, eps
        sb = lambda n, s: ctx.enter_context(nc.sbuf_tensor(f"{name}_{n}", s, F32))
        sem = lambda n: ctx.enter_context(nc.semaphore(f"{name}_{n}"))
        self.stats_buf = sb("stats", [P, NT, 6])
        self.mv = sb("mv", [P, NT, 2])
        self.var_eps = sb("var_eps", [P, NT])
        self.rstd = sb("rstd", [P, NT])
        self.neg_half = sb("neg_half", [P, NT])
        self.half_ready = sem("half_ready")
        self.stats_ready = sem("stats_ready")
        self.mv_ready = sem("mv_ready")
        self.ve_ready = sem("ve_ready")
        self.rstd_ready = sem("rstd_ready")
        self.normed = sem("normed")

    def setup(self, pool):
        self.nc.gpsimd.memset(self.neg_half[:], -0.5).then_inc(self.half_ready, 1)
        pool.wait_ge(self.half_ready, 1)

    def statistics(self, dve, c, sum_ready, first=0):
        for t in range(c * TPB, (c + 1) * TPB):
            dve.wait_ge(sum_ready, first + t + 1)
            self.nc.vector.bn_stats(self.stats_buf[:, t, :], self.X[:, t, :]).then_inc(self.stats_ready, 1)
        for t in range(c * TPB, (c + 1) * TPB):
            dve.wait_ge(self.stats_ready, t + 1)
            self.nc.vector.bn_aggr(self.mv[:, t, :], self.stats_buf[:, t, :]).then_inc(self.mv_ready, 1)

    def inverse_deviation(self, pool, c):
        g = slice(c * TPB, (c + 1) * TPB)
        pool.wait_ge(self.mv_ready, (c + 1) * TPB)
        self.nc.gpsimd.tensor_scalar(self.var_eps[:, g], self.mv[:, g, 1], self.eps, 1.0,
                                     ALU.add, ALU.mult).then_inc(self.ve_ready, 1)
        pool.wait_ge(self.ve_ready, c + 1)
        self.nc.gpsimd.tensor_tensor(self.rstd[:, g], self.var_eps[:, g], self.neg_half[:, g],
                                     ALU.pow).then_inc(self.rstd_ready, 1)

    def normalize(self, dve, c, out=None):
        out = self.X if out is None else out
        dve.wait_ge(self.rstd_ready, c + 1)
        for t in range(c * TPB, (c + 1) * TPB):
            self.nc.vector.tensor_scalar(out[:, t, :], self.X[:, t, :], self.mv[:, t, 0:1], self.rstd[:, t:t + 1],
                                         ALU.subtract, ALU.mult).then_inc(self.normed, 1)


def turn_group(nc, pe, src, ident, banks, c, normed, copied, turned):
    pe.wait_ge(normed, (c + 1) * TPB)
    if c >= 1:
        pe.wait_ge(copied, KD * c)
    for h in range(KD):
        for t in range(TPB):
            last = nc.tensor.transpose(banks[h][:, t * P:(t + 1) * P], src[:, c * TPB + t, h * P:(h + 1) * P], ident)
        last.then_inc(turned, 1)


def copy_turned(nc, act, dst, banks, c, turned, copied):
    for h in range(KD):
        act.wait_ge(turned, KD * c + h + 1)
        nc.scalar.activation(dst[:, h, c * S:(c + 1) * S], banks[h][:], ACT.Copy).then_inc(copied, 1)


LEVELS = 7
ETA = 0.01 * 2.0 / D


def phase_ttt(nc, ctx, dram, X, XT, ident):
    sb = lambda n, s, dt=F32: ctx.enter_context(nc.sbuf_tensor(f"A_{n}", s, dt))
    sem = lambda n: ctx.enter_context(nc.semaphore(f"A_{n}"))
    thKT, thQT, thVT = (sb(n, [P, KD, D]) for n in ("thKT", "thQT", "thVT"))
    thK, thQ, W0T = (sb(n, [P, KD, D]) for n in ("thK", "thQ", "W0T"))
    b0 = sb("b0", [P, D])
    masks = sb("masks", [P, LEVELS + 2, P])
    M1, M2 = sb("M1", [P, KD, D]), sb("M2", [P, KD, D])
    KT, QT = sb("KT", [P, KD, T]), sb("QT", [P, KD, T])
    ROW = TPB * S
    GN = sb("GN", [P, B * ROW + S])
    GQ = sb("GQ", [P, B * ROW])
    XI, YI = sb("XI", [P, B, S]), sb("YI", [P, B, S])
    CT = sb("CT", [P, 4, S])
    P1 = sb("P1", [P, 2, S])
    R = sb("R", [P, 2, D])
    U = KT[:, :, :].rearrange("p k t -> p (k t)").rearrange("p (n d) -> p n d", d=D)
    banks = [ctx.enter_context(nc.psum_tensor(f"A_bank{i}", [P, S], F32)) for i in range(8)]

    norm = Norm(ctx, nc, "A_norm", X, LN_EPS)
    loaded = sem("loaded")
    product, act_copied, dve_copied = sem("product"), sem("act_copied"), sem("dve_copied")
    mask_ready, start_tmp, start_ready = sem("mask_ready"), sem("start_tmp"), sem("start_ready")
    cx_ready, cx_copied = sem("cx_ready"), sem("cx_copied")
    xcx_ready, inv_ready = sem("xcx_ready"), sem("inv_ready")
    acc_ready, rhs_ready, u_ready, u_copied = sem("acc_ready"), sem("rhs_ready"), sem("u_ready"), sem("u_copied")
    out_ready, sum_ready, xb_ready = sem("out_ready"), sem("sum_ready"), sem("xb_ready")
    turned, copied = sem("turned"), sem("copied")

    plain = [("M2", h) for h in range(KD)] + [("M1", h) for h in range(KD)]
    plain += [(w, (h, b)) for b in range(B) for h in range(KD) for w in ("KT", "QT")]
    plain += [(w, (b, j)) for b in range(B) for j in range(TPB) for w in ("GK", "GQ")]
    by_act = {"M2", "KT", "GK"}
    order = []
    for kind, _ in plain:
        mine = kind in by_act
        order.append((mine, 1 + sum(1 for m, _ in order if m == mine)))

    def wait_copied(eng, n):
        mine, count = order[n]
        eng.wait_ge(act_copied if mine else dve_copied, count)

    last_proj = max(n for n, (k, _) in enumerate(plain) if k in ("KT", "QT"))
    pairs = [(0, 1), (2, 3)]
    steps = [(m, b) for pair in pairs for m in range(1, LEVELS) for b in pair]
    step_no = {s: n for n, s in enumerate(steps)}
    blocks = [(b, i) for i in range(TPB) for b in range(B)]

    def diagonal(b):
        v = GN[:, b * ROW:b * ROW + TPB * (S + P)].rearrange("p (j c) -> p j c", c=S + P)
        return v[:, :, 0:P]

    def four(m):
        return masks[:, m:m + 1, :].broadcast_to([P, TPB, P])

    def view(t):
        return t.rearrange("p (j c) -> p j c", c=P)

    with nc.Block() as block:
        @block.sync
        def _(sp):
            for t, n in ((thQ, "L0_attn_theta_Q"), (thK, "L0_attn_theta_K"), (W0T, "W0T"), (thVT, "thVT"), (thKT, "thKT"), (thQT, "thQT")):
                sp.dma_start(t[:], dram[n].rearrange("(k p) d -> p k d", p=P)).then_inc(loaded, 16)
            sp.dma_start(b0[:], dram["L0_attn_b0"].partition_broadcast(P)).then_inc(loaded, 16)
            sp.dma_start(masks[:], dram["ttt_masks"]).then_inc(loaded, 16)

        @block.tensor
        def _(pe):
            mm = nc.tensor.matmul
            pe.wait_ge(loaded, 128)
            for n, (kind, w) in enumerate(plain):
                bank = banks[n % 8]
                if n >= 8:
                    wait_copied(pe, n - 8)
                if kind in ("GK", "GQ") and w == (0, 0) and kind == "GK":
                    wait_copied(pe, last_proj)
                    wait_copied(pe, last_proj - 1)
                for k in range(KD):
                    if kind in ("M1", "M2"):
                        lhsT, rhs, o = (thK if kind == "M1" else thQ)[:, k, w * P:(w + 1) * P], W0T[:, k, :], bank[:, 0:D]
                    elif kind in ("KT", "QT"):
                        h, b = w
                        lhsT, rhs, o = (thKT if kind == "KT" else thQT)[:, k, h * P:(h + 1) * P], XT[:, k, b * S:(b + 1) * S], bank[:]
                    else:
                        b, j = w
                        at = b * S + j * P
                        lhsT = KT[:, k, at:at + P]
                        rhs = (KT if kind == "GK" else QT)[:, k, at:(b + 1) * S]
                        o = bank[:, j * P:S]
                    last = mm(o, lhsT, rhs, start=(k == 0), stop=(k == KD - 1))
                last.then_inc(product, 1)
            for n in range(len(plain) - 8, len(plain)):
                wait_copied(pe, n)
            for n, (m, b) in enumerate(steps):
                s = b % 2
                cx, xcx, ycx = banks[3 * s], banks[3 * s + 1], banks[3 * s + 2]
                pe.wait_ge(mask_ready, n + 1)
                if m == 1:
                    pe.wait_ge(start_ready, 2 * (b + 1))
                else:
                    pe.wait_ge(inv_ready, 2 * (step_no[(m - 1, b)] + 1))
                if b >= 2 and m == 1:
                    pe.wait_ge(inv_ready, 2 * (step_no[(LEVELS - 1, b - 2)] + 1))
                for j in range(TPB):
                    c = slice(j * P, (j + 1) * P)
                    last = mm(cx[:, c], CT[:, n % 4, c], XI[:, b, c], start=True, stop=True)
                last.then_inc(cx_ready, 1)
                pe.wait_ge(cx_copied, n + 1)
                for j in range(TPB):
                    c = slice(j * P, (j + 1) * P)
                    mm(xcx[:, c], YI[:, b, c], P1[:, s, c], start=True, stop=True)
                for j in range(TPB):
                    c = slice(j * P, (j + 1) * P)
                    last = mm(ycx[:, c], P1[:, s, c], YI[:, b, c], start=True, stop=True)
                last.then_inc(xcx_ready, 1)
            pe.wait_ge(inv_ready, 2 * len(steps))
            for n, (b, i) in enumerate(blocks):
                tok = slice(b * S + i * P, b * S + (i + 1) * P)
                acc, u_ps, out_ps = banks[n % 2], banks[2 + n % 2], banks[4 + n % 2]
                if n >= 2:
                    pe.wait_ge(rhs_ready, n - 1)
                for k in range(KD):
                    last = mm(acc[:, 0:D], XT[:, k, tok], M1[:, k, :], start=(k == 0), stop=(i == 0 and k == KD - 1))
                if i > 0:
                    pe.wait_ge(u_copied, (i - 1) * B + b + 1)
                for j in range(i):
                    last = mm(acc[:, 0:D], GN[:, b * ROW + j * S + i * P:b * ROW + j * S + (i + 1) * P],
                              U[:, b * TPB + j, :], start=False, stop=(j == i - 1))
                last.then_inc(acc_ready, 1)
                if n >= 2:
                    pe.wait_ge(sum_ready, n - 1)
                for k in range(KD):
                    mm(out_ps[:, 0:D], XT[:, k, tok], M2[:, k, :], start=(k == 0), stop=False)
                for j in range(i):
                    mm(out_ps[:, 0:D], GQ[:, b * ROW + j * S + i * P:b * ROW + j * S + (i + 1) * P],
                       U[:, b * TPB + j, :], start=False, stop=False)
                pe.wait_ge(rhs_ready, n + 1)
                if n >= 2:
                    pe.wait_ge(u_copied, n - 1)
                mm(u_ps[:, 0:D], YI[:, b, i * P:(i + 1) * P], R[:, n % 2, :], start=True, stop=True).then_inc(u_ready, 1)
                pe.wait_ge(u_copied, n + 1)
                mm(out_ps[:, 0:D], GQ[:, b * ROW + i * (S + P):b * ROW + i * (S + P) + P],
                   U[:, b * TPB + i, :], start=False, stop=True).then_inc(out_ready, 1)
            pe.wait_ge(sum_ready, NT)
            for c in range(B):
                turn_group(nc, pe, X, ident[:], banks, c, norm.normed, copied, turned)

        @block.scalar
        def _(act):
            for n, (kind, w) in enumerate(plain):
                if kind not in by_act:
                    continue
                act.wait_ge(product, n + 1)
                bank = banks[n % 8]
                if kind == "M2":
                    o = nc.scalar.activation(M2[:, w, :], bank[:, 0:D], ACT.Copy)
                elif kind == "KT":
                    h, b = w
                    o = nc.scalar.activation(KT[:, h, b * S:(b + 1) * S], bank[:], ACT.Copy)
                else:
                    b, j = w
                    o = nc.scalar.activation(GN[:, b * ROW + j * (S + P):b * ROW + (j + 1) * S], bank[:, j * P:S],
                                             ACT.Copy, bias=-ETA, scale=-ETA)
                o.then_inc(act_copied, 1)
            for n, (m, b) in enumerate(steps):
                act.wait_ge(cx_ready, n + 1)
                if n >= 2:
                    act.wait_ge(xcx_ready, n - 1)
                nc.scalar.activation(P1[:, b % 2, :], banks[3 * (b % 2)][:], ACT.Copy).then_inc(cx_copied, 1)
            for n, (b, i) in enumerate(blocks):
                act.wait_ge(u_ready, n + 1)
                nc.scalar.activation(U[:, b * TPB + i, :], banks[2 + n % 2][:, 0:D], ACT.Copy).then_inc(u_copied, 1)
            for c in range(B):
                copy_turned(nc, act, XT, banks, c, turned, copied)

        @block.gpsimd
        def _(pool):
            norm.setup(pool)
            pool.wait_ge(loaded, 128)
            tt = nc.gpsimd.tensor_tensor

            def start(b, tmp):
                for q, (m, dst) in enumerate(((LEVELS, XI), (0, YI))):
                    tt(view(dst[:, b, :]), diagonal(b), four(m), ALU.mult).then_inc(start_tmp, 1)
                    pool.wait_ge(start_tmp, 2 * b + q + 1)
                    tt(view(dst[:, b, :]), view(dst[:, b, :]), ident[:].rearrange("p (a c) -> p a c", a=1).broadcast_to([P, TPB, P]),
                       ALU.add).then_inc(start_ready, 1)

            for n, (m, b) in enumerate(steps):
                if m == 1:
                    wait_copied(pool, plain.index(("GK", (b, TPB - 1))))
                    start(b, None)
                if n >= 4:
                    pool.wait_ge(cx_ready, n - 3)
                tt(view(CT[:, n % 4, :]), diagonal(b), four(m), ALU.mult).then_inc(mask_ready, 1)
            for c in range(B):
                norm.inverse_deviation(pool, c)

        @block.vector
        def _(dve):
            dve.wait_ge(loaded, 128)
            for t in range(NT):
                nc.vector.tensor_tensor(X[:, t, :], X[:, t, :], b0[:], ALU.add).then_inc(xb_ready, 1)
            for n, (kind, w) in enumerate(plain):
                if kind in by_act:
                    continue
                dve.wait_ge(product, n + 1)
                bank = banks[n % 8]
                if kind == "M1":
                    o = nc.vector.tensor_tensor(M1[:, w, :], bank[:, 0:D], thVT[:, w, :], ALU.subtract)
                elif kind == "QT":
                    h, b = w
                    o = nc.vector.tensor_copy(QT[:, h, b * S:(b + 1) * S], bank[:])
                else:
                    b, j = w
                    at = b * ROW + j * (S + P)
                    o = nc.vector.scalar_tensor_tensor(GQ[:, at:at + P], bank[:, j * P:(j + 1) * P], 1.0,
                                                       masks[:, LEVELS + 1, :], ALU.add, ALU.mult)
                    if j < TPB - 1:
                        o = nc.vector.tensor_scalar(GQ[:, at + P:b * ROW + (j + 1) * S], bank[:, (j + 1) * P:S],
                                                    1.0, -ETA, ALU.add, ALU.mult)
                o.then_inc(dve_copied, 1)
            for n, (m, b) in enumerate(steps):
                dve.wait_ge(xcx_ready, n + 1)
                s = b % 2
                nc.vector.tensor_tensor(XI[:, b, :], XI[:, b, :], banks[3 * s + 1][:], ALU.add).then_inc(inv_ready, 1)
                nc.vector.tensor_tensor(YI[:, b, :], YI[:, b, :], banks[3 * s + 2][:], ALU.add).then_inc(inv_ready, 1)
            dve.wait_ge(xb_ready, NT)

            def add_out(n):
                b, i = blocks[n]
                dve.wait_ge(out_ready, n + 1)
                x = X[:, b * TPB + i, :]
                nc.vector.tensor_tensor(x, banks[4 + n % 2][:, 0:D], x, ALU.add).then_inc(sum_ready, 1)

            for n in range(NT):
                dve.wait_ge(acc_ready, n + 1)
                if n >= 2:
                    dve.wait_ge(u_ready, n - 1)
                nc.vector.tensor_tensor(R[:, n % 2, :], banks[n % 2][:, 0:D], b0[:], ALU.add).then_inc(rhs_ready, 1)
                add_out(n)
            dve.wait_ge(sum_ready, NT)
            for c in range(B):
                norm.statistics(dve, c, sum_ready)
            for c in range(B):
                norm.normalize(dve, c)


def key_rows(kt):
    return min(P, S2 - kt * P)


def phase_cross0(nc, ctx, dram, X, XT, ident):
    sb = lambda n, s, dt=F32: ctx.enter_context(nc.sbuf_tensor(f"B_{n}", s, dt))
    sem = lambda n: ctx.enter_context(nc.semaphore(f"B_{n}"))
    W1, W2T = sb("W1", [P, KD, D]), sb("W2T", [P, KD, D])
    b1, b2, b12 = sb("b1", [P, KD]), sb("b2", [P, KD]), sb("b12", [P, KD])
    W12T, W12 = sb("W12T", [P, KD, D]), sb("W12", [P, KD, D])
    ctxT = sb("ctxT", [P, 2, KD, S2])
    ctxN = sb("ctxN", [P, 2, NK2, D])
    bias = sb("bias", [P, TPB, S2])
    qpT, q2T = sb("qpT", [P, KD, S]), sb("q2T", [P, KD, S])
    probs = sb("probs", [P, 2, S2])
    PT = sb("PT", [P, 2, NK2, P])
    top, neg_top, total, inv_total = (sb(n, [P, 2]) for n in ("top", "neg_top", "total", "inv_total"))
    fence = sb("fence", [P, 1])
    scores_ps = ctx.enter_context(nc.psum_tensor("B_scores", [P, 4 * S], F32))
    ring = [ctx.enter_context(nc.psum_tensor(f"B_ring{i}", [P, S], F32)) for i in range(2)]
    av_ps = ctx.enter_context(nc.psum_tensor("B_av", [P, D], F32))

    norm = Norm(ctx, nc, "B_norm", X, LN_EPS)
    loaded, bias_loaded = sem("loaded"), sem("bias_loaded")
    ctx_loaded = [sem(f"ctx_loaded{i}") for i in range(2)]
    w_product, w_copied = sem("w_product"), sem("w_copied")
    ring_ready, act_copied, dve_copied = sem("ring_ready"), sem("act_copied"), sem("dve_copied")
    scores_ready, scores_read, max_ready, probs_ready = sem("scores_ready"), sem("scores_read"), sem("max_ready"), sem("probs_ready")
    av_ready, inv_ready, sum_ready = sem("av_ready"), sem("inv_ready"), sem("sum_ready")
    turned, copied = sem("turned"), sem("copied")

    RING, BY_ACT, BY_DVE = 4 + 4 * TPB, 4 + 2 * TPB, 2 * TPB
    groups = [range(g * 4, min(g * 4 + 4, NK2)) for g in range(4)]

    with nc.Block() as block:
        @block.sync
        def _(sp):
            sp.dma_start(W1[:], dram["L0_xattn_W1"].rearrange("(k p) d -> p k d", p=P)).then_inc(loaded, 16)
            sp.dma_start(W2T[:], dram["xW2T"].rearrange("(k p) d -> p k d", p=P)).then_inc(loaded, 16)
            sp.dma_start(b1[:], dram["L0_xattn_b1"]).then_inc(loaded, 16)
            sp.dma_start(b2[:], dram["L0_xattn_b2"]).then_inc(loaded, 16)
            with sp.Fori(0, B // 2) as bb:
                for u in range(2):
                    b = bb * 2 + u
                    sp.wait_ge(av_ready, bb * 2 * TPB)
                    sp.dma_start(ctxT[:, u], dram["ctxT"][ds(b, 1)].rearrange("b (k p) s -> p (b k) s", p=P)).then_inc(ctx_loaded[u], 16)
                    sp.dma_start(ctxN[:, u, 0:NK2 - 1, :], dram["ctx"][ds(b, 1), 0:(NK2 - 1) * P].rearrange("b (k p) d -> p (b k) d", p=P)).then_inc(ctx_loaded[u], 16)
                    sp.dma_start(ctxN[0:key_rows(NK2 - 1), u, NK2 - 1, :], dram["ctx"][ds(b, 1), (NK2 - 1) * P:S2].rearrange("b p d -> (b p) d")).then_inc(ctx_loaded[u], 16)

        @block.tensor
        def _(pe):
            mm = nc.tensor.matmul
            pe.wait_ge(loaded, 64)
            for n in range(6):
                kind, h = n // 2, n % 2
                if n >= 2:
                    pe.wait_ge(w_copied, n - 1)
                for k in range(KD):
                    lhsT = (W1 if kind == 0 else W2T)[:, k, h * P:(h + 1) * P]
                    rhs = (W2T[:, k, :], W1[:, k, :], b1[:, k:k + 1])[kind]
                    last = mm(ring[h][:, 0:1] if kind == 2 else ring[h][:, 0:D], lhsT, rhs, start=(k == 0), stop=(k == KD - 1))
                last.then_inc(w_product, 1)
            pe.wait_ge(w_copied, 6)

            def scores(b, u, t):
                n = b * TPB + t
                pe.wait_ge(scores_read, n)
                for c in range(4):
                    w = min(S, S2 - c * S)
                    for k in range(KD):
                        last = mm(scores_ps[:, c * S:c * S + w], q2T[:, k, t * P:(t + 1) * P], ctxT[:, u, k, c * S:c * S + w],
                                  start=(k == 0), stop=(k == KD - 1))
                last.then_inc(scores_ready, 1)

            with pe.Fori(0, B // 2) as bb:
                for u in range(2):
                    b = bb * 2 + u
                    pe.wait_ge(dve_copied, b * BY_DVE)
                    pe.wait_ge(act_copied, b * BY_ACT)
                    for m in range(KD):
                        for k in range(KD):
                            last = mm(ring[m][:], W12T[:, k, m * P:(m + 1) * P], XT[:, k, ds(b * S, S)], start=(k == 0), stop=(k == KD - 1))
                        last.then_inc(ring_ready, 1)
                    pe.wait_ge(act_copied, b * BY_ACT + 2)
                    for m in range(KD):
                        for k in range(KD):
                            last = mm(ring[m][:], W12[:, k, m * P:(m + 1) * P], qpT[:, k, :], start=(k == 0), stop=(k == KD - 1))
                        last.then_inc(ring_ready, 1)
                    pe.wait_ge(act_copied, b * BY_ACT + 4)
                    pe.wait_ge(ctx_loaded[u], bb * 48 + 48)
                    scores(b, u, 0)
                    for t in range(TPB):
                        n = b * TPB + t
                        if t + 1 < TPB:
                            scores(b, u, t + 1)
                        pe.wait_ge(probs_ready, n + 1)
                        for g in range(4):
                            if g % 2 == 0:
                                pe.wait_ge(dve_copied, b * BY_DVE + 2 * t + g // 2)
                            else:
                                pe.wait_ge(act_copied, b * BY_ACT + 4 + 2 * t + g // 2)
                            for q, kt in enumerate(groups[g]):
                                r = key_rows(kt)
                                last = nc.tensor.transpose(ring[g % 2][0:r, q * P:(q + 1) * P], probs[:, t % 2, kt * P:kt * P + r], ident[:])
                            last.then_inc(ring_ready, 1)
                        pe.wait_ge(dve_copied, b * BY_DVE + 2 * t + 2)
                        pe.wait_ge(act_copied, b * BY_ACT + 4 + 2 * t + 2)
                        pe.wait_ge(sum_ready, n)
                        for kt in range(NK2):
                            r = key_rows(kt)
                            last = mm(av_ps[:], PT[0:r, t % 2, kt, :], ctxN[0:r, u, kt, :], start=(kt == 0), stop=(kt == NK2 - 1))
                        last.then_inc(av_ready, 1)
            for c in range(B):
                turn_group(nc, pe, X, ident[:], ring, c, norm.normed, copied, turned)

        def copy_group(eng_copy, t, g):
            k0, k1 = groups[g][0], groups[g][-1] + 1
            r = key_rows(k1 - 1) if k1 - k0 == 1 else P
            return eng_copy(PT[0:r, t % 2, k0:k1, :], ring[g % 2][0:r, 0:(k1 - k0) * P].rearrange("p (k c) -> p k c", c=P))

        @block.scalar
        def _(act):
            act.dma_start(bias[:], dram["fside"].rearrange("(t p) s -> p t s", p=P)).then_inc(bias_loaded, 16)
            act.wait_ge(loaded, 64)
            for n in range(6):
                kind, h = n // 2, n % 2
                act.wait_ge(w_product, n + 1)
                if kind == 2:
                    o = nc.scalar.activation(b12[:, h:h + 1], ring[h][:, 0:1], ACT.Identity, bias=b2[:, h:h + 1])
                else:
                    o = nc.scalar.activation((W12T if kind == 0 else W12)[:, h, :], ring[h][:, 0:D], ACT.Copy)
                o.then_inc(w_copied, 1)
            act.wait_ge(w_copied, 6)

            def exponentials(b, t):
                n = b * TPB + t
                act.wait_ge(max_ready, n + 1)
                nc.scalar.activation(probs[:, t % 2, :], probs[:, t % 2, :], ACT.Exp, bias=neg_top[:, t % 2:t % 2 + 1],
                                     accum_out=total[:, t % 2:t % 2 + 1]).then_inc(probs_ready, 1)

            with act.Fori(0, B // 2) as bb:
                for u in range(2):
                    b = bb * 2 + u
                    for m in range(KD):
                        act.wait_ge(ring_ready, b * RING + m + 1)
                        nc.scalar.activation(qpT[:, m, :], ring[m][:], ACT.Identity, bias=b12[:, m:m + 1]).then_inc(act_copied, 1)
                    for m in range(KD):
                        act.wait_ge(ring_ready, b * RING + m + 3)
                        nc.scalar.activation(q2T[:, m, :], ring[m][:], ACT.Copy, scale=float(D) ** -0.5).then_inc(act_copied, 1)
                    exponentials(b, 0)
                    for t in range(TPB):
                        for g in (1, 3):
                            act.wait_ge(ring_ready, b * RING + 4 + 4 * t + g + 1)
                            copy_group(nc.scalar.copy, t, g).then_inc(act_copied, 1)
                        if t + 1 < TPB:
                            exponentials(b, t + 1)
            for c in range(B):
                copy_turned(nc, act, XT, ring, c, turned, copied)

        @block.gpsimd
        def _(pool):
            norm.setup(pool)
            for c in range(B):
                norm.inverse_deviation(pool, c)

        @block.vector
        def _(dve):
            dve.wait_ge(bias_loaded, 16)

            def maximum(b, t):
                n = b * TPB + t
                dve.wait_ge(scores_ready, n + 1)
                nc.vector.memset(fence[:], 0.0)
                nc.vector.tensor_tensor_reduce(out=probs[:, t % 2, :], in0=scores_ps[:, 0:S2], in1=bias[:, t, :], scale=1.0,
                                               scalar=-3.0e38, op0=ALU.add, op1=ALU.max,
                                               accum_out=top[:, t % 2:t % 2 + 1]).then_inc(scores_read, 1)
                dve.wait_ge(scores_read, n + 1)
                nc.vector.tensor_scalar(neg_top[:, t % 2:t % 2 + 1], top[:, t % 2:t % 2 + 1], -1.0, None, ALU.mult).then_inc(max_ready, 1)

            with dve.Fori(0, B // 2) as bb:
                for u in range(2):
                    b = bb * 2 + u
                    maximum(b, 0)
                    for t in range(TPB):
                        n = b * TPB + t
                        for g in (0, 2):
                            dve.wait_ge(ring_ready, b * RING + 4 + 4 * t + g + 1)
                            copy_group(nc.vector.tensor_copy, t, g).then_inc(dve_copied, 1)
                        if t + 1 < TPB:
                            maximum(b, t + 1)
                        dve.wait_ge(probs_ready, n + 1)
                        nc.vector.reciprocal(inv_total[:, t % 2:t % 2 + 1], total[:, t % 2:t % 2 + 1]).then_inc(inv_ready, 1)
                        dve.wait_ge(inv_ready, n + 1)
                        dve.wait_ge(av_ready, n + 1)
                        x = X[:, ds(n, 1), :].rearrange("p a d -> p (a d)")
                        nc.vector.scalar_tensor_tensor(x, av_ps[:], inv_total[:, t % 2:t % 2 + 1], x, ALU.mult, ALU.add).then_inc(sum_ready, 1)
            for c in range(B):
                norm.statistics(dve, c, sum_ready)
            for c in range(B):
                norm.normalize(dve, c)


def phase_moe(nc, ctx, dram, X, XT, ident):
    sb = lambda n, s, dt=F32: ctx.enter_context(nc.sbuf_tensor(f"C_{n}", s, dt))
    ps = lambda n, s: ctx.enter_context(nc.psum_tensor(f"C_{n}", s, F32))
    sem = lambda n: ctx.enter_context(nc.semaphore(f"C_{n}"))
    Wr, br, lanes = sb("Wr", [P, KD, E]), sb("br", [P, E]), sb("lanes", [P, E])
    logits, best = sb("logits", [P, NT, E]), sb("best", [P, NT])
    top8, index8, index_f = sb("top8", [P, NT, 8]), sb("index8", [P, NT, 8], mybir.dt.uint32), sb("index_f", [P, NT, 2])
    pair_sum, first, second = sb("pair_sum", [P, NT]), sb("first", [P, NT, E]), sb("second", [P, NT, E])
    comb = sb("comb", [P, NT, E])
    bi, bg, half_bg = sb("bi", [P, E, NF]), sb("bg", [P, E, NF]), sb("half_bg", [P, E, NF])
    Wi, Wg, Wo = (sb(n, [P, 2, KD * F]) for n in ("Wi", "Wg", "Wo"))
    tail = sb("tail", [P, 2, 3, D])
    gelu, gate = sb("gelu", [P, 2, S]), sb("gate", [P, 2, S])
    hT = sb("hT", [P, NF, S])
    R = sb("R", [P, TPB, D])
    N = sb("N", [P, 2, D])
    OUT = sb("OUT", [P, NT, D])
    stats, mv, ve, rstd = sb("stats", [P, TPB, 6]), sb("mv", [P, TPB, 2]), sb("ve", [P, TPB]), sb("rstd", [P, TPB])
    neg_half, eps, fence = sb("neg_half", [P, 1]), sb("eps", [P, 1]), sb("fence", [P, 1])
    router_ps = ps("router", [P, NT * E])
    yi_ps, yg_ps, y2_ps = ([ps(f"{n}{i}", [P, w]) for i in range(2)] for n, w in (("yi", S), ("yg", S), ("y2", D)))

    norm = Norm(ctx, nc, "C_norm", OUT, LN_EPS)
    loaded = sem("loaded")
    w_loaded = [sem(f"w_loaded{u}") for u in range(2)]
    routed, r_step, exp_ready, comb_ready = sem("routed"), sem("r_step"), sem("exp_ready"), sem("comb_ready")
    bias_scaled, out_started = sem("bias_scaled"), sem("out_started")
    yi_ready, yg_ready, gelu_ready, gate_ready = sem("yi_ready"), sem("yg_ready"), sem("gelu_ready"), sem("gate_ready")
    act_ready = sem("act_ready")
    base_ready, y2_ready, r_ready = sem("base_ready"), sem("y2_ready"), sem("r_ready")
    stats_ready, mv_ready, ve_ready, rstd_ready = sem("stats_ready"), sem("mv_ready"), sem("ve_ready"), sem("rstd_ready")
    n_ready, g_ready, b_ready, mixed = sem("n_ready"), sem("g_ready"), sem("b_ready"), sem("mixed")
    half_ready = sem("half_ready")
    turned, copied = sem("turned"), sem("copied")
    turn_ps = yi_ps

    with nc.Block() as block:
        @block.sync
        def _(sp):
            for t, n in ((Wr, "L0_ffn_Wr"), (br, "L0_ffn_br"), (lanes, "lanes"), (bi, "L0_ffn_bi"), (bg, "L0_ffn_bg")):
                sp.dma_start(t[:], dram[n]).then_inc(loaded, 16)

            def load(e, u):
                one = ds(e, 1)
                sp.dma_start(Wi[:, u, :].rearrange("p (k f) -> p k f", k=KD), dram["L0_ffn_Wi"][one].rearrange("e (k p) f -> p (e k) f", p=P)).then_inc(w_loaded[u], 16)
                sp.dma_start(Wg[:, u, :].rearrange("p (k f) -> p k f", k=KD), dram["L0_ffn_Wg"][one].rearrange("e (k p) f -> p (e k) f", p=P)).then_inc(w_loaded[u], 16)
                sp.dma_start(Wo[:, u, :].rearrange("p (k f) -> p k f", k=NF), dram["L0_ffn_Wo"][one].rearrange("e (k p) f -> p (e k) f", p=P)).then_inc(w_loaded[u], 16)
                sp.dma_start(tail[:, u], dram["expert_tail"][:, one].rearrange("q e r d -> q (e r) d")).then_inc(w_loaded[u], 16)

            for u in range(2):
                load(u, u)
            with sp.Fori(0, E // 2 - 1) as ee:
                for u in range(2):
                    sp.wait_ge(mixed, (ee * 2 + u + 1) * NT)
                    load(ee * 2 + 2 + u, u)

        @block.tensor
        def _(pe):
            mm = nc.tensor.matmul
            pe.wait_ge(loaded, 80)
            for t in range(NT):
                for k in range(KD):
                    last = mm(router_ps[:, t * E:(t + 1) * E], XT[:, k, t * P:(t + 1) * P], Wr[:, k, :], start=(k == 0), stop=(k == KD - 1))
            last.then_inc(routed, 1)
            with pe.Fori(0, E // 2) as ee:
                for u in range(2):
                    with pe.Fori(0, B) as c:
                        pe.wait_ge(w_loaded[u], ee * 64 + 64)
                        it = (ee * 2 + u) * B + c
                        for j in range(NF):
                            n = it * NF + j
                            if j >= 2:
                                pe.wait_ge(gate_ready, n - 1)
                            for w, banks, ready in ((Wi, yi_ps, yi_ready), (Wg, yg_ps, yg_ready)):
                                for k in range(KD):
                                    last = mm(banks[j % 2][:], w[:, u, k * F + j * P:k * F + (j + 1) * P], XT[:, k, ds(c * S, S)],
                                              start=(k == 0), stop=(k == KD - 1))
                                last.then_inc(ready, 1)
                        for t in range(TPB):
                            n = it * TPB + t
                            pe.wait_ge(r_ready, n - 1) if t >= 2 else None
                            for j in range(NF):
                                if t == 0:
                                    pe.wait_ge(act_ready, it * NF + j + 1)
                                last = mm(y2_ps[t % 2][:], hT[:, j, t * P:(t + 1) * P], Wo[:, u, j * D:(j + 1) * D],
                                          start=(j == 0), stop=(j == NF - 1))
                            last.then_inc(y2_ready, 1)
                        pe.wait_ge(r_ready, (it + 1) * TPB)
            for c in range(B):
                turn_group(nc, pe, X, ident[:], turn_ps, c, norm.normed, copied, turned)

        @block.scalar
        def _(act):
            act.wait_ge(r_step, 2)
            nc.scalar.activation(logits[:], logits[:], ACT.Exp).then_inc(exp_ready, 1)
            act.wait_ge(bias_scaled, 1)
            with act.Fori(0, E) as e:
                with act.Fori(0, B) as c:
                    for j in range(NF):
                        n = (e * B + c) * NF + j
                        act.wait_ge(yi_ready, n + 1)
                        if j >= 2:
                            act.wait_ge(act_ready, n - 1)
                        b = bi[:, ds(e, 1), j:j + 1].rearrange("p a b -> p (a b)")
                        nc.scalar.activation(gelu[:, j % 2, :], yi_ps[j % 2][:], ACT.Gelu, bias=b).then_inc(gelu_ready, 1)
                        act.wait_ge(yg_ready, n + 1)
                        b = half_bg[:, ds(e, 1), j:j + 1].rearrange("p a b -> p (a b)")
                        nc.scalar.activation(gate[:, j % 2, :], yg_ps[j % 2][:], ACT.Tanh, bias=b, scale=0.5).then_inc(gate_ready, 1)
            for c in range(B):
                copy_turned(nc, act, XT, turn_ps, c, turned, copied)

        @block.gpsimd
        def _(pool):
            norm.setup(pool)
            nc.gpsimd.memset(neg_half[:], -0.5).then_inc(half_ready, 1)
            nc.gpsimd.memset(eps[:], 1e-12).then_inc(half_ready, 1)
            pool.wait_ge(half_ready, 2)
            for c in range(B):
                nc.gpsimd.tensor_copy(OUT[:, c * TPB:(c + 1) * TPB, :], X[:, c * TPB:(c + 1) * TPB, :]).then_inc(out_started, 1)
            with pool.Fori(0, E // 2) as ee:
                for u in range(2):
                    with pool.Fori(0, B) as c:
                        pool.wait_ge(w_loaded[u], ee * 64 + 64)
                        it = (ee * 2 + u) * B + c
                        pool.wait_ge(n_ready, it * TPB)
                        for t in range(TPB):
                            nc.gpsimd.tensor_tensor(R[:, t, :], X[:, ds(c * TPB + t, 1), :].rearrange("p a d -> p (a d)"),
                                                    tail[:, u, 0, :], ALU.add).then_inc(base_ready, 1)
                        for t in range(TPB):
                            n = it * TPB + t
                            pool.wait_ge(mv_ready, n + 1)
                            nc.gpsimd.tensor_tensor(ve[:, t:t + 1], mv[:, t, 1:2], eps[:], ALU.add).then_inc(ve_ready, 1)
                            pool.wait_ge(ve_ready, n + 1)
                            nc.gpsimd.tensor_tensor(rstd[:, t:t + 1], ve[:, t:t + 1], neg_half[:], ALU.pow).then_inc(rstd_ready, 1)
            for c in range(B):
                norm.inverse_deviation(pool, c)

        @block.vector
        def _(dve):
            v = nc.vector
            dve.wait_ge(loaded, 80)
            v.tensor_scalar(half_bg[:], bg[:], 0.5, None, ALU.mult).then_inc(bias_scaled, 1)
            dve.wait_ge(routed, 1)
            v.tensor_tensor(logits[:], router_ps[:].rearrange("p (t e) -> p t e", e=E),
                            br[:].rearrange("p (a e) -> p a e", a=1).broadcast_to([P, NT, E]), ALU.add).then_inc(r_step, 1)
            dve.wait_ge(r_step, 1)
            v.tensor_reduce(best[:], logits[:], AX_X, ALU.max).then_inc(comb_ready, 1)
            dve.wait_ge(comb_ready, 1)
            v.tensor_tensor(logits[:], logits[:], best[:].rearrange("p (t a) -> p t a", a=1).broadcast_to([P, NT, E]), ALU.subtract).then_inc(r_step, 1)
            dve.wait_ge(exp_ready, 1)
            for t in range(NT):
                v.max(top8[:, t, :], logits[:, t, :]).then_inc(comb_ready, 1)
            dve.wait_ge(comb_ready, 1 + NT)
            for t in range(NT):
                v.max_index(index8[:, t, :], top8[:, t, :], logits[:, t, :]).then_inc(comb_ready, 1)
            v.tensor_tensor(pair_sum[:], top8[:, :, 0], top8[:, :, 1], ALU.add).then_inc(comb_ready, 1)
            dve.wait_ge(comb_ready, 2 + 2 * NT)
            v.tensor_copy(index_f[:], index8[:, :, 0:2]).then_inc(comb_ready, 1)
            v.reciprocal(pair_sum[:], pair_sum[:]).then_inc(comb_ready, 1)
            dve.wait_ge(comb_ready, 4 + 2 * NT)
            for t in range(NT):
                for q, dst in ((0, first), (1, second)):
                    v.tensor_scalar(dst[:, t, :], lanes[:], index_f[:, t, q:q + 1], top8[:, t, q:q + 1], ALU.is_equal, ALU.mult).then_inc(comb_ready, 1)
            dve.wait_ge(comb_ready, 4 + 4 * NT)
            v.tensor_tensor(first[:], first[:], second[:], ALU.add).then_inc(comb_ready, 1)
            dve.wait_ge(comb_ready, 5 + 4 * NT)
            v.tensor_tensor(comb[:], first[:], pair_sum[:].rearrange("p (t a) -> p t a", a=1).broadcast_to([P, NT, E]), ALU.mult).then_inc(comb_ready, 1)
            dve.wait_ge(comb_ready, 6 + 4 * NT)
            dve.wait_ge(out_started, B)

            with dve.Fori(0, E // 2) as ee:
                for u in range(2):
                    e = ee * 2 + u
                    with dve.Fori(0, B) as c:
                        it = e * B + c
                        for j in range(NF):
                            n = it * NF + j
                            dve.wait_ge(gelu_ready, n + 1)
                            dve.wait_ge(gate_ready, n + 1)
                            v.scalar_tensor_tensor(hT[:, j, :], gate[:, j % 2, :], 1.0, gelu[:, j % 2, :], ALU.add, ALU.mult).then_inc(act_ready, 1)

                        def finish(t):
                            n = it * TPB + t
                            dve.wait_ge(rstd_ready, n + 1)
                            v.tensor_scalar(N[:, t % 2, :], R[:, t, :], mv[:, t, 0:1], rstd[:, t:t + 1], ALU.subtract, ALU.mult).then_inc(n_ready, 1)
                            dve.wait_ge(n_ready, n + 1)
                            v.tensor_tensor(N[:, t % 2, :], N[:, t % 2, :], tail[:, u, 1, :], ALU.mult).then_inc(g_ready, 1)
                            dve.wait_ge(g_ready, n + 1)
                            v.tensor_tensor(N[:, t % 2, :], N[:, t % 2, :], tail[:, u, 2, :], ALU.add).then_inc(b_ready, 1)
                            dve.wait_ge(b_ready, n + 1)
                            o = OUT[:, ds(c * TPB + t, 1), :].rearrange("p a d -> p (a d)")
                            w = comb[:, ds(c * TPB + t, 1), ds(e, 1)].rearrange("p a b -> p (a b)")
                            v.scalar_tensor_tensor(o, N[:, t % 2, :], w, o, ALU.mult, ALU.add).then_inc(mixed, 1)

                        for t in range(TPB):
                            n = it * TPB + t
                            dve.wait_ge(base_ready, n + 1)
                            dve.wait_ge(y2_ready, n + 1)
                            v.scalar_tensor_tensor(R[:, t, :], y2_ps[t % 2][:], 0.5, R[:, t, :], ALU.mult, ALU.add).then_inc(r_ready, 1)
                            dve.wait_ge(r_ready, n + 1)
                            v.bn_stats(stats[:, t, :], R[:, t, :]).then_inc(stats_ready, 1)
                            dve.wait_ge(stats_ready, n + 1)
                            v.memset(fence[:], 0.0)
                            v.bn_aggr(mv[:, t, :], stats[:, t, :]).then_inc(mv_ready, 1)
                            if t > 0:
                                finish(t - 1)
                        finish(TPB - 1)
            dve.wait_ge(mixed, E * NT)
            for c in range(B):
                norm.statistics(dve, c, mixed, (E - 1) * NT)
            for c in range(B):
                norm.normalize(dve, c, X)


PARTS = 3
Q_PARTS = (0, 0, 1, 1, 0, 2)
K_PARTS = (0, 1, 0, 1, 2, 0)
STACK = len(Q_PARTS) * DH
NEG = 2.0 ** 100
UNITS = B * H
VW = DH + 1
STRIP = 32
STRIPS = P // STRIP


class Heads:

    def __init__(self, ctx, nc, name, n_keys, extra, causal, qd, kd, V, ATT, ident16, tri, strip_sum, slots, lag, order,
                 copy_after):
        self.nc, self.n_keys, self.causal = nc, n_keys, causal
        self.qd, self.kd, self.V, self.ATT, self.tri = qd, kd, V, ATT, tri
        self.slots, self.lag, self.copy_after = slots, lag, copy_after
        self.ident_bf, self.ident_half = ident16
        self.strip_sum_dram = strip_sum
        self.R = STACK + extra
        self.tiles = [(kt, min(P, n_keys - kt * P)) for kt in range((n_keys + P - 1) // P)]
        self.groups = [self.tiles[i:i + 2] for i in range(0, len(self.tiles), 2)]
        self.NG = len(self.groups)
        self.quads = [range(g, min(g + 2, self.NG)) for g in range(0, self.NG, 2)]
        n_chunks = (n_keys + S - 1) // S
        w = -(-n_keys // n_chunks)
        self.chunks = [(qt, c, min(w, n_keys - c)) for qt in range(TPB) for c in range(0, n_keys, w)]
        self.per_q = n_chunks
        counts = {"scores": 0, "max": 0, "values": 0}
        self.order = []
        for kind in order.split():
            self.order.append((kind, counts.get(kind, 0)))
            if kind in counts:
                counts[kind] += 1
        assert counts == {"scores": self.NG, "max": len(self.chunks), "values": len(self.quads) - 1}
        assert (slots * self.NG) % 4 == 0 and slots % 2 == 0
        sb = lambda n, s, dt=F32: ctx.enter_context(nc.sbuf_tensor(f"{name}_{n}", s, dt))
        ps = lambda n, s, dt=F32: ctx.enter_context(nc.psum_tensor(f"{name}_{n}", s, dt))
        sem = lambda n: ctx.enter_context(nc.semaphore(f"{name}_{n}"))
        self.KS = sb("KS", [self.R + 2, slots, n_keys], BF16)
        self.QS = sb("QS", [self.R + 2, slots, S], BF16)
        self.VS = sb("VS", [P, 2, len(self.tiles), STRIP])
        self.strip_sum = sb("strip_sum", [P, VW])
        self.probs = sb("probs", [P, 4, 2 * S])
        self.maxima = sb("maxima", [P, TPB, n_chunks])
        self.neg = sb("neg", [P, TPB])
        self.neg_parts = sb("neg_parts", [P, 2, TPB], BF16)
        self.neg_rows = sb("neg_rows", [2 * TPB, 2, P], BF16)
        self.av = sb("av", [P, S])
        self.inv = sb("inv", [P, TPB])
        self.score_ps = [ps(f"score{i}", [P, 2 * S]) for i in range(2)]
        self.max_ps = [ps(f"max{i}", [P, S]) for i in range(2)]
        self.av_ps = ps("av_ps", [P, S])
        small_ps = ps("small", [P, S])
        self.token_ps = small_ps[:, 0:TPB * VW]
        self.row_ps = small_ps[0:2 * TPB, P:P + P // 2].bitcast(BF16)
        self.loaded = [sem(f"loaded{i}") for i in range(slots)]
        self.rows_loaded = [sem(f"rows_loaded{i}") for i in range(slots)]
        self.sum_loaded = sem("sum_loaded")
        self.chunk_ready, self.chunk_read = sem("chunk_ready"), sem("chunk_read")
        self.neg_f, self.neg_a, self.neg_ready = sem("neg_f"), sem("neg_a"), sem("neg_ready")
        self.rows_turned, self.rows_copied = sem("rows_turned"), sem("rows_copied")
        self.scores_ready, self.probs_ready, self.probs_used = sem("scores_ready"), sem("probs_ready"), sem("probs_used")
        self.padded, self.values_ready = sem("padded"), sem("values_ready")
        self.av_copied, self.token_ready = sem("av_copied"), sem("token_ready")
        self.inv_ready, self.unit_read = sem("inv_ready"), sem("unit_read")

    def walk(self, eng, step, unroll=None):
        n = unroll or self.slots
        for u in range(n):
            step(u, u, 0)
        with eng.Fori(1, UNITS // n - 1) as i:
            for u in range(n):
                step(i * n + u, u, i)
        for u in range(n):
            step(UNITS - n + u, u, UNITS // n - 1)

    def ahead(self, s, n):
        return not isinstance(s, int) or s + n < UNITS

    def at(self, s, n):
        return not isinstance(s, int) or s >= n

    def load(self, sp, unit, slot):
        sp.dma_start(self.KS[:, slot, :], self.kd[ds(unit, 1)].rearrange("u r s -> (u r) s")).then_inc(self.loaded[slot], 16)
        sp.dma_start(self.QS[0:self.R, slot, :], self.qd[ds(unit, 1)].rearrange("u r s -> (u r) s")).then_inc(self.loaded[slot], 16)

    def load_rows(self, sp, unit, slot):
        sp.wait_ge(self.rows_copied, unit + 1)
        sp.dma_start(self.QS[self.R:self.R + 2, slot, :].rearrange("a (t q) -> a t q", q=P),
                     self.neg_rows[:, slot % 2, :]).then_inc(self.rows_loaded[slot], 16)

    def sync(self, sp):
        sp.dma_start(self.strip_sum[:], self.strip_sum_dram).then_inc(self.sum_loaded, 16)
        for u in range(self.slots):
            self.load(sp, u, u)
        for u in range(self.lag - 1):
            self.load_rows(sp, u, u)

        def step(s, u, i):
            if self.ahead(s, self.lag - 1):
                self.load_rows(sp, s + self.lag - 1, (u + self.lag - 1) % self.slots)
            if self.ahead(s, self.slots):
                sp.wait_ge(self.scores_ready, (s + 1) * self.NG)
                self.load(sp, s + self.slots, u)

        self.walk(sp, step)

    def max_chunk(self, pe, unit, slot, m):
        nc = self.nc
        qt, c, w = self.chunks[m]
        n = unit * len(self.chunks) + m
        if not isinstance(unit, int) or n >= 2:
            pe.wait_ge(self.chunk_read, n - 1)
        out = self.max_ps[m % 2]
        last = nc.tensor.matmul(out[:, 0:w], self.QS[0:self.R, slot, qt * P:(qt + 1) * P], self.KS[0:self.R, slot, c:c + w],
                                start=True, stop=True)
        if self.causal:
            last = nc.tensor.matmul(out[:, qt * P:(qt + 1) * P], self.ident_half[:], self.tri[:, 0, :], start=False, stop=True,
                                    skip_group_check=True)
        last.then_inc(self.chunk_ready, 1)

    def turn_rows(self, pe, unit):
        pe.wait_ge(self.neg_ready, unit + 1)
        if self.at(unit, 1):
            pe.wait_ge(self.rows_copied, unit)
        if self.at(unit, self.lag + 1):
            pe.wait_ge(self.unit_read, unit - self.lag)
        self.nc.tensor.transpose(self.row_ps, self.neg_parts[:].rearrange("p a t -> p (a t)"), self.ident_bf[:]).then_inc(self.rows_turned, 1)

    def scores(self, pe, s, u, g):
        nc = self.nc
        n = s * self.NG + g
        if self.at(s, 1) or g >= 2:
            pe.wait_ge(self.probs_ready, n - 1)
        bank = self.score_ps[(u * self.NG + g) % 2]
        for q, (kt, r) in enumerate(self.groups[g]):
            last = nc.tensor.matmul(bank[0:r, q * S:(q + 1) * S], self.KS[:, u, kt * P:kt * P + r], self.QS[:, u, :], start=True, stop=True)
            if self.causal:
                last = nc.tensor.matmul(bank[:, q * S + kt * P:q * S + (kt + 1) * P], self.ident_half[:], self.tri[:, 1, :],
                                        start=False, stop=True, skip_group_check=True)
        last.then_inc(self.scores_ready, 1)

    def values(self, pe, s, u, quad):
        nc = self.nc
        groups = self.quads[quad]
        if quad == 0:
            pe.wait_ge(self.values_ready, s + 1)
            if self.at(s, 1):
                pe.wait_ge(self.av_copied, s)
        pe.wait_ge(self.probs_ready, s * self.NG + groups[-1] + 1)
        tiles = [(kt, r, (u * self.NG + g) % 4, q * S) for g in groups for q, (kt, r) in enumerate(self.groups[g])]
        final = quad == len(self.quads) - 1
        if len(tiles) == STRIPS:
            parts = [(j, t, 0, S) for j, t in enumerate(tiles)]
        else:
            parts = [(j, t, j * P, P) for t in tiles for j in range(STRIPS)]
        for j, (kt, r, buf, off), q0, w in parts:
            last = nc.tensor.matmul(self.av_ps[j * STRIP:(j + 1) * STRIP, q0:q0 + w], self.VS[0:r, u % 2, kt, :],
                                    self.probs[0:r, buf, off + q0:off + q0 + w], start=(quad == 0), stop=final,
                                    tile_position=(0, j * STRIP), skip_group_check=True)
        last.then_inc(self.probs_used, len(groups))

    def token_major(self, pe, unit):
        nc = self.nc
        pe.wait_ge(self.av_copied, unit + 1)
        if self.at(unit, 1):
            pe.wait_ge(self.unit_read, unit)
        turned = unit + 1 + self.lag
        pe.wait_ge(self.rows_copied, min(turned, UNITS) if isinstance(unit, int) else turned)
        for qt in range(TPB):
            last = nc.tensor.matmul(self.token_ps[:, qt * VW:(qt + 1) * VW], self.av[:, qt * P:(qt + 1) * P], self.strip_sum[:],
                                    start=True, stop=True)
        last.then_inc(self.token_ready, 1)

    def tensor(self, pe):
        for unit in range(self.lag):
            pe.wait_ge(self.loaded[unit], 32)
            for m in range(len(self.chunks)):
                self.max_chunk(pe, unit, unit, m)
            if unit >= 1:
                self.turn_rows(pe, unit - 1)
        pe.wait_ge(self.sum_loaded, 16)

        def step(s, u, i):
            pe.wait_ge(self.rows_loaded[u], i * 16 + 16)
            ahead = u + self.lag
            if self.ahead(s, self.lag):
                pe.wait_ge(self.loaded[ahead % self.slots], (i + ahead // self.slots) * 32 + 32)
            for kind, k in self.order:
                if kind == "scores":
                    self.scores(pe, s, u, k)
                elif kind == "max" and self.ahead(s, self.lag):
                    self.max_chunk(pe, s + self.lag, ahead % self.slots, k)
                elif kind == "turn" and self.ahead(s, self.lag - 1):
                    self.turn_rows(pe, s + self.lag - 1)
                elif kind == "values":
                    self.values(pe, s, u, k)
                elif kind == "last" and self.at(s, 1):
                    self.values(pe, s - 1, (u - 1) % self.slots, len(self.quads) - 1)
                elif kind == "token" and self.at(s, 1):
                    self.token_major(pe, s - 1)

        self.walk(pe, step)
        self.values(pe, UNITS - 1, self.slots - 1, len(self.quads) - 1)
        self.token_major(pe, UNITS - 1)

    def copy_sums(self, act, unit):
        act.wait_ge(self.probs_used, (unit + 1) * self.NG)
        if self.at(unit, 1):
            act.wait_ge(self.token_ready, unit)
        self.nc.scalar.activation(self.av[:], self.av_ps[:], ACT.Copy).then_inc(self.av_copied, 1)

    def scalar(self, act):
        nc, NG = self.nc, self.NG

        def step(s, u, i):
            for g, group in enumerate(self.groups):
                n = s * NG + g
                act.wait_ge(self.scores_ready, n + 1)
                if not isinstance(n, int) or n >= 4:
                    act.wait_ge(self.probs_used, n - 3)
                r, w = group[-1][1], len(group) * S
                nc.scalar.activation(self.probs[0:r, (u * NG + g) % 4, 0:w], self.score_ps[(u * NG + g) % 2][0:r, 0:w],
                                     ACT.Exp).then_inc(self.probs_ready, 1)
                if g == self.copy_after and self.at(s, 1):
                    self.copy_sums(act, s - 1)

        self.walk(act, step)
        self.copy_sums(act, UNITS - 1)

    def pool(self, pool):
        nc = self.nc
        nc.gpsimd.memset(self.VS[:], 0.0).then_inc(self.padded, 1)
        pool.wait_ge(self.padded, 1)

        def step(s, u, i):
            if self.at(s, 2):
                pool.wait_ge(self.probs_used, (s - 1) * self.NG)
            nc.gpsimd.tensor_copy(self.VS[:, u % 2, :, 0:VW], self.V[:, :, ds(s * VW, VW)]).then_inc(self.values_ready, 1)

        self.walk(pool, step, 2)

    def maximum(self, dve, unit, m):
        qt, c, w = self.chunks[m]
        dve.wait_ge(self.chunk_ready, unit * len(self.chunks) + m + 1)
        self.nc.vector.tensor_reduce(self.maxima[:, qt, m % self.per_q:m % self.per_q + 1], self.max_ps[m % 2][:, 0:w], AX_X,
                                     ALU.max).then_inc(self.chunk_read, 1)

    def negate(self, dve, unit):
        v = self.nc.vector
        dve.wait_ge(self.chunk_read, (unit + 1) * len(self.chunks))
        v.tensor_reduce(self.neg[:], self.maxima[:], AX_X, ALU.max, negate=True).then_inc(self.neg_f, 1)
        dve.wait_ge(self.neg_f, unit + 1)
        if self.at(unit, 1):
            dve.wait_ge(self.rows_turned, unit)
        v.tensor_copy(self.neg_parts[:, 0, :], self.neg[:]).then_inc(self.neg_a, 1)
        dve.wait_ge(self.neg_a, unit + 1)
        v.tensor_tensor(self.neg_parts[:, 1, :], self.neg[:], self.neg_parts[:, 0, :], ALU.subtract).then_inc(self.neg_ready, 1)

    def copy_rows(self, dve, unit, slot, round_):
        if self.at(unit, 2):
            dve.wait_ge(self.rows_loaded[(slot - 2) % self.slots], round_ * 16 + 16)
        dve.wait_ge(self.rows_turned, unit + 1)
        self.nc.vector.tensor_copy(self.neg_rows[:, slot % 2, :], self.row_ps).then_inc(self.rows_copied, 1)

    def divide(self, dve, unit):
        v = self.nc.vector
        dve.wait_ge(self.token_ready, unit + 1)
        token = self.token_ps.rearrange("p (t v) -> p t v", v=VW)
        v.reciprocal(self.inv[:], token[:, :, DH]).then_inc(self.inv_ready, 1)
        dve.wait_ge(self.inv_ready, unit + 1)
        v.tensor_tensor(self.ATT[:, :, ds(unit * DH, DH)], token[:, :, 0:DH],
                        self.inv[:].rearrange("p (t a) -> p t a", a=1).broadcast_to([P, TPB, DH]), ALU.mult).then_inc(self.unit_read, 1)

    def vector(self, dve):
        for unit in range(self.lag):
            for m in range(len(self.chunks)):
                self.maximum(dve, unit, m)
            if unit >= 1:
                self.copy_rows(dve, unit - 1, unit - 1, 0)
            self.negate(dve, unit)

        def step(s, u, i):
            for kind, k in self.order:
                if kind == "max" and self.ahead(s, self.lag):
                    self.maximum(dve, s + self.lag, k)
                elif kind == "turn" and self.ahead(s, self.lag - 1):
                    ahead = u + self.lag - 1
                    self.copy_rows(dve, s + self.lag - 1, ahead % self.slots, i + (ahead - 2) // self.slots)
                elif kind == "token" and self.at(s, 1):
                    self.divide(dve, s - 1)
            if self.ahead(s, self.lag):
                self.negate(dve, s + self.lag)

        self.walk(dve, step)
        self.divide(dve, UNITS - 1)


class Split:

    def __init__(self, ctx, nc, name):
        self.nc = nc
        sb = lambda n, dt: ctx.enter_context(nc.sbuf_tensor(f"{name}_{n}", [P, 2, S], dt))
        sems = lambda n: [ctx.enter_context(nc.semaphore(f"{name}_{n}{i}")) for i in range(2)]
        self.t = sb("t", F32)
        self.parts = [sb(f"part{i}", BF16) for i in range(PARTS)]
        self.t_ready, self.a_ready, self.r_ready, self.b_ready, self.c_ready, self.stored = (
            sems(n) for n in ("t_ready", "a_ready", "r_ready", "b_ready", "c_ready", "stored"))

    def before_t(self, dve, slot, turn):
        dve.wait_ge(self.c_ready[slot], turn)

    def scalar(self, act, slot, turn, w):
        nc, (a, b, _) = self.nc, self.parts
        act.wait_ge(self.stored[slot], turn * 16 * len(Q_PARTS))
        act.wait_ge(self.t_ready[slot], turn + 1)
        nc.scalar.copy(a[:, slot, 0:w], self.t[:, slot, 0:w]).then_inc(self.a_ready[slot], 1)
        act.wait_ge(self.r_ready[slot], turn + 1)
        nc.scalar.copy(b[:, slot, 0:w], self.t[:, slot, 0:w]).then_inc(self.b_ready[slot], 1)

    def pool(self, pool, slot, turn, w):
        nc, (a, b, c) = self.nc, self.parts
        t = self.t[:, slot, 0:w]
        pool.wait_ge(self.a_ready[slot], turn + 1)
        nc.gpsimd.tensor_tensor(t, t, a[:, slot, 0:w], ALU.subtract).then_inc(self.r_ready[slot], 1)
        pool.wait_ge(self.b_ready[slot], turn + 1)
        nc.gpsimd.tensor_tensor(c[:, slot, 0:w], t, b[:, slot, 0:w], ALU.subtract).then_inc(self.c_ready[slot], 1)

    def sync(self, sp, slot, turn, w, dst, order, unit0, c0):
        sp.wait_ge(self.c_ready[slot], turn + 1)
        for block, part in enumerate(order):
            sp.dma_start(dst[ds(unit0, P // DH), block * DH:(block + 1) * DH, ds(c0, w)],
                         self.parts[part][:, slot, 0:w]).then_inc(self.stored[slot], 16)


def project_out(nc, ctx, name, X, XT, ATT, ident, WoT, bo):
    sem = lambda n: ctx.enter_context(nc.semaphore(f"{name}_{n}"))
    ps = [ctx.enter_context(nc.psum_tensor(f"{name}_out{i}", [P, S], F32)) for i in range(8)]
    turn_ps, out_ps, back_ps = ps[0:2], ps[2:6], ps[6:8]
    norm = Norm(ctx, nc, f"{name}_norm", X, LN_EPS)
    loaded, turned, copied = sem("loaded"), sem("turned"), sem("copied")
    out_ready, base_ready, sum_ready, turned2, copied2 = sem("out_ready"), sem("base_ready"), sem("sum_ready"), sem("turned2"), sem("copied2")
    WoT_sb = ctx.enter_context(nc.sbuf_tensor(f"{name}_WoT", [P, KD, D], F32))
    bo_sb = ctx.enter_context(nc.sbuf_tensor(f"{name}_bo", [P, D], F32)) if bo is not None else None
    need = 16 if bo is None else 32
    with nc.Block() as block:
        @block.sync
        def _(sp):
            sp.dma_start(WoT_sb[:], WoT.rearrange("(k p) d -> p k d", p=P)).then_inc(loaded, 16)
            if bo is not None:
                sp.dma_start(bo_sb[:], bo.partition_broadcast(P)).then_inc(loaded, 16)

        @block.tensor
        def _(pe):
            def attended(c):
                if c >= 1:
                    pe.wait_ge(copied, KD * c)
                for h in range(KD):
                    for t in range(TPB):
                        last = nc.tensor.transpose(turn_ps[h][:, t * P:(t + 1) * P], ATT[:, t, c * D + h * P:c * D + (h + 1) * P], ident[:])
                    last.then_inc(turned, 1)

            pe.wait_ge(loaded, need)
            for c in range(B + 1):
                if c < B:
                    attended(c)
                if c == 0:
                    continue
                pe.wait_ge(copied, KD * c)
                for t in range((c - 1) * TPB, c * TPB):
                    if t >= TPB:
                        pe.wait_ge(sum_ready, t - TPB + 1)
                    for k in range(KD):
                        last = nc.tensor.matmul(out_ps[t % TPB][:, 0:D], XT[:, k, t * P:(t + 1) * P], WoT_sb[:, k, :],
                                                start=(k == 0), stop=(k == KD - 1))
                    last.then_inc(out_ready, 1)
            for c in range(B):
                turn_group(nc, pe, X, ident[:], back_ps, c, norm.normed, copied2, turned2)

        @block.scalar
        def _(act):
            for c in range(B):
                copy_turned(nc, act, XT, turn_ps, c, turned, copied)
            act.wait_ge(out_ready, NT)
            for c in range(B):
                copy_turned(nc, act, XT, back_ps, c, turned2, copied2)

        @block.gpsimd
        def _(pool):
            norm.setup(pool)
            for c in range(B):
                norm.inverse_deviation(pool, c)

        @block.vector
        def _(dve):
            if bo is not None:
                dve.wait_ge(loaded, need)
                for t in range(NT):
                    nc.vector.tensor_tensor(X[:, t, :], X[:, t, :], bo_sb[:], ALU.add).then_inc(base_ready, 1)
                dve.wait_ge(base_ready, NT)
            for c in range(B):
                for t in range(c * TPB, (c + 1) * TPB):
                    dve.wait_ge(out_ready, t + 1)
                    nc.vector.tensor_tensor(X[:, t, :], out_ps[t % TPB][:, 0:D], X[:, t, :], ALU.add).then_inc(sum_ready, 1)
                norm.statistics(dve, c, sum_ready)
            for c in range(B):
                norm.normalize(dve, c)


def narrow_identities(nc, ctx, name):
    return [ctx.enter_context(nc.sbuf_tensor(f"{name}_ident{i}", [P, P], dt)) for i, dt in enumerate((BF16, F16))]


def run_heads(nc, heads):
    with nc.Block() as block:
        @block.sync
        def _(sp):
            heads.sync(sp)

        @block.tensor
        def _(pe):
            heads.tensor(pe)

        @block.scalar
        def _(act):
            heads.scalar(act)

        @block.gpsimd
        def _(pool):
            heads.pool(pool)

        @block.vector
        def _(dve):
            heads.vector(dve)


CAUSAL = 2 * (TPB - 1)


def phase_self(nc, ctx, dram, X, XT, ident):
    qd = nc.dram_tensor("D_qd", (UNITS, STACK + CAUSAL, S), BF16, kind="Internal").ap()
    kd = nc.dram_tensor("D_kd", (UNITS, STACK + CAUSAL + 2, S), BF16, kind="Internal").ap()
    V = ctx.enter_context(nc.sbuf_tensor("D_V", [P, TPB, UNITS * VW], F32))
    ATT = ctx.enter_context(nc.sbuf_tensor("D_ATT", [P, TPB, UNITS * DH], F32))
    idents = narrow_identities(nc, ctx, "D")
    tri = ctx.enter_context(nc.sbuf_tensor("D_tri", [P, 2, P], F16))
    with ExitStack() as own:
        sb = lambda n, s, dt=F32: own.enter_context(nc.sbuf_tensor(f"D_{n}", s, dt))
        sem = lambda n: ctx.enter_context(nc.semaphore(f"D_{n}"))
        w = sb("w", [P, KD, 3 * D])
        tri_f = sb("tri_f", [P, 2, P])
        rows_f = sb("rows_f", [UNITS, 2 * CAUSAL + 2, S])
        rows_b = sb("rows_b", [UNITS, 2 * CAUSAL + 2, S], BF16)
        banks = [own.enter_context(nc.psum_tensor(f"D_bank{i}", [P, S], F32)) for i in range(4)]
        split = Split(own, nc, "D_split")
        loaded, rows_ready, rows_stored, ones_ready = sem("loaded"), sem("rows_ready"), sem("rows_stored"), sem("ones_ready")
        cast_ready = sem("cast_ready")
        product = [sem(f"product{i}") for i in range(2)]
        v_product, v_copied = sem("v_product"), sem("v_copied")
        items = [(which, hf) for hf in range(KD) for which in range(2)]

        with nc.Block() as block:
            @block.sync
            def _(sp):
                sp.dma_start(w[:], dram["wqkvT"].rearrange("(k p) e -> p k e", p=P)).then_inc(loaded, 16)
                sp.dma_start(tri_f[:], dram["causal_tri"]).then_inc(loaded, 16)
                sp.dma_start(rows_f[:], dram["causal_rows"]).then_inc(loaded, 16)
                with sp.Fori(0, B) as b:
                    for k, (which, hf) in enumerate(items):
                        split.sync(sp, k % 2, b * 2 + k // 2, S, (qd, kd)[which], (Q_PARTS, K_PARTS)[which],
                                   b * H + hf * (H // KD), 0)
                sp.wait_ge(rows_ready, 1)
                sp.dma_start(qd[:, STACK:, :], rows_b[:, 0:CAUSAL, :]).then_inc(rows_stored, 16)
                sp.dma_start(kd[:, STACK:, :], rows_b[:, CAUSAL:, :]).then_inc(rows_stored, 16)
                sp.wait_ge(rows_stored, 32)
                for i in range(2):
                    sp.wait_ge(split.stored[i], 2 * B * 16 * len(Q_PARTS))

            @block.tensor
            def _(pe):
                mm = nc.tensor.matmul
                pe.wait_ge(loaded, 48)
                for t in range(NT):
                    if t >= 2:
                        pe.wait_ge(v_copied, t - 1)
                    for k in range(KD):
                        last = mm(banks[2 + t % 2][:, 0:D], XT[:, k, t * P:(t + 1) * P], w[:, k, 2 * D:3 * D], start=(k == 0), stop=(k == KD - 1))
                    last.then_inc(v_product, 1)
                with pe.Fori(0, B) as b:
                    for n, (which, hf) in enumerate(items):
                        slot, turn = n % 2, b * 2 + n // 2
                        pe.wait_ge(split.t_ready[slot], turn)
                        for k in range(KD):
                            last = mm(banks[slot][:], w[:, k, which * D + hf * P:which * D + (hf + 1) * P], XT[:, k, ds(b * S, S)],
                                      start=(k == 0), stop=(k == KD - 1))
                        last.then_inc(product[slot], 1)

            @block.scalar
            def _(act):
                with act.Fori(0, B) as b:
                    for n in range(len(items)):
                        split.scalar(act, n % 2, b * 2 + n // 2, S)

            @block.gpsimd
            def _(pool):
                nc.gpsimd.memset(V[:], 1.0).then_inc(ones_ready, 1)
                pool.wait_ge(loaded, 48)
                nc.gpsimd.tensor_copy(rows_b[:], rows_f[:]).then_inc(rows_ready, 1)
                with pool.Fori(0, B) as b:
                    for n in range(len(items)):
                        split.pool(pool, n % 2, b * 2 + n // 2, S)

            @block.vector
            def _(dve):
                v = nc.vector
                dve.wait_ge(loaded, 48)
                v.tensor_copy(idents[0][:], ident[:]).then_inc(cast_ready, 1)
                v.tensor_copy(idents[1][:], ident[:]).then_inc(cast_ready, 1)
                v.tensor_copy(tri[:], tri_f[:]).then_inc(cast_ready, 1)
                dve.wait_ge(ones_ready, 1)
                for t in range(NT):
                    b, kt = divmod(t, TPB)
                    dve.wait_ge(v_product, t + 1)
                    v.tensor_copy(V[:, kt, b * H * VW:(b + 1) * H * VW].rearrange("p (h v) -> p h v", v=VW)[:, :, 0:DH],
                                  banks[2 + t % 2][:, 0:D].rearrange("p (h d) -> p h d", d=DH)).then_inc(v_copied, 1)
                with dve.Fori(0, B) as b:
                    for n, (which, hf) in enumerate(items):
                        slot, turn = n % 2, b * 2 + n // 2
                        split.before_t(dve, slot, turn)
                        dve.wait_ge(product[slot], turn + 1)
                        v.tensor_scalar(split.t[:, slot, :], banks[slot][:], 0.25 if which == 0 else 1.0, None, ALU.mult).then_inc(split.t_ready[slot], 1)

    with ExitStack() as own:
        run_heads(nc, Heads(own, nc, "Dh", S, CAUSAL, True, qd, kd, V, ATT, idents, tri, dram["strip_sum"], 8, 3,
                            "scores last max max scores max turn max token", 0))
    with ExitStack() as own:
        project_out(nc, own, "Do", X, XT, ATT, ident, dram["self_WoT"], None)


def phase_cross1(nc, ctx, dram, X, XT, ident):
    KC = 4
    kw = -(-S2 // KC)
    chunks = [(c * kw, min(kw, S2 - c * kw)) for c in range(KC)]
    qd = nc.dram_tensor("E_qd", (UNITS, STACK + 1, S), BF16, kind="Internal").ap()
    kd = nc.dram_tensor("E_kd", (UNITS, STACK + 3, S2), BF16, kind="Internal").ap()
    V = ctx.enter_context(nc.sbuf_tensor("E_V", [P, NK2, UNITS * VW], F32))
    idents = narrow_identities(nc, ctx, "E")
    with ExitStack() as own:
        sb = lambda n, s, dt=F32: own.enter_context(nc.sbuf_tensor(f"E_{n}", s, dt))
        sem = lambda n: ctx.enter_context(nc.semaphore(f"E_{n}"))
        wq, wqs, wk, wks, wv = (sb(n, [P, KD, D]) for n in ("wq", "wqs", "wk", "wks", "wv"))
        bq, bqs, bk, bks = (sb(n, [P, KD]) for n in ("bq", "bqs", "bk", "bks"))
        bv = sb("bv", [P, D])
        cosq, sinq, cosk, sink = sb("cosq", [P, S]), sb("sinq", [P, S]), sb("cosk", [P, S2]), sb("sink", [P, S2])
        cosm, sinm = sb("cosm", [P, S2]), sb("sinm", [P, S2])
        mask = sb("mask", [P, S2], I32)
        keep = sb("keep", [P, S2])
        ctxT = sb("ctxT", [P, KD, S2])
        mask_row = sb("mask_row", [H, S2], BF16)
        ones = sb("ones", [UNITS, S2], BF16)
        swap = sb("swap", [P, 2, S])
        main_ps = [own.enter_context(nc.psum_tensor(f"E_main{i}", [P, S], F32)) for i in range(2)]
        swap_ps = [own.enter_context(nc.psum_tensor(f"E_swap{i}", [P, S], F32)) for i in range(2)]
        v_ps = [own.enter_context(nc.psum_tensor(f"E_v{i}", [P, D], F32)) for i in range(2)]
        split = Split(own, nc, "E_split")
        loaded, ctx_loaded, mask_loaded = sem("loaded"), sem("ctx_loaded"), sem("mask_loaded")
        ones_ready, rows_stored, row_ready, row_stored = sem("ones_ready"), sem("rows_stored"), sem("row_ready"), sem("row_stored")
        v_ones, cast_ready = sem("v_ones"), sem("cast_ready")
        keep_ready, table_ready = sem("keep_ready"), sem("table_ready")
        product, rotated = [sem(f"product{i}") for i in range(2)], [sem(f"rotated{i}") for i in range(2)]
        v_product, v_copied, keys_done = sem("v_product"), sem("v_copied"), sem("keys_done")
        items = [(0, hf, 0, S) for hf in range(KD)] + [(1, hf, c, w) for hf in range(KD) for c, w in chunks]
        PER = len(items) // 2

        with nc.Block() as block:
            @block.sync
            def _(sp):
                for t, n in ((wq, "wqT"), (wqs, "wqT_swapped"), (wk, "wkT"), (wks, "wkT_swapped"), (wv, "wvT")):
                    sp.dma_start(t[:], dram[n].rearrange("(k p) e -> p k e", p=P)).then_inc(loaded, 16)
                for t, n in ((bq, "bq"), (bqs, "bq_swapped"), (bk, "bk"), (bks, "bk_swapped"), (cosq, "cosq"), (sinq, "sinq"), (cosk, "cosk"), (sink, "sink")):
                    sp.dma_start(t[:], dram[n]).then_inc(loaded, 16)
                sp.dma_start(bv[:], dram["bv"].partition_broadcast(P)).then_inc(loaded, 16)
                sp.wait_ge(ones_ready, 1)
                sp.dma_start(qd[:, STACK, :], ones[:, 0:S]).then_inc(rows_stored, 16)
                for r in (STACK + 1, STACK + 2):
                    sp.dma_start(kd[:, r, :], ones[:]).then_inc(rows_stored, 16)
                with sp.Fori(0, B) as b:
                    sp.wait_ge(keys_done, b)
                    sp.dma_start(ctxT[:], dram["ctxT"][ds(b, 1)].rearrange("b (k p) s -> p (b k) s", p=P)).then_inc(ctx_loaded, 16)
                    sp.wait_ge(table_ready, b * 2)
                    sp.dma_start(mask[:], dram["mask"][ds(b, 1)].rearrange("b r s -> (b r) s")).then_inc(mask_loaded, 16)
                    for n, (which, hf, c, w) in enumerate(items):
                        split.sync(sp, n % 2, b * PER + n // 2, w, (qd, kd)[which], (Q_PARTS, K_PARTS)[which],
                                   b * H + hf * (H // KD), c)
                    sp.wait_ge(row_ready, b + 1)
                    sp.dma_start(kd[ds(b * H, H), STACK, :], mask_row[:]).then_inc(row_stored, 16)
                sp.wait_ge(rows_stored, 48)
                sp.wait_ge(row_stored, 16 * B)
                for i in range(2):
                    sp.wait_ge(split.stored[i], PER * B * 16 * len(Q_PARTS))

            @block.tensor
            def _(pe):
                mm = nc.tensor.matmul
                pe.wait_ge(loaded, 224)
                with pe.Fori(0, B) as b:
                    for n, (which, hf, c, w) in enumerate(items):
                        slot, turn = n % 2, b * PER + n // 2
                        if n == 2:
                            pe.wait_ge(ctx_loaded, b * 16 + 16)
                        pe.wait_ge(rotated[slot], turn)
                        for bank, wt in ((main_ps[slot], (wq, wk)[which]), (swap_ps[slot], (wqs, wks)[which])):
                            for k in range(KD):
                                rhs = XT[:, k, ds(b * S, S)] if which == 0 else ctxT[:, k, c:c + w]
                                last = mm(bank[:, 0:w], wt[:, k, hf * P:(hf + 1) * P], rhs, start=(k == 0), stop=(k == KD - 1))
                        last.then_inc(product[slot], 1)
                    for kt in range(NK2):
                        r = key_rows(kt)
                        pe.wait_ge(v_copied, b * NK2 + kt - 1 if kt >= 2 else b * NK2)
                        for k in range(KD):
                            last = mm(v_ps[kt % 2][0:r, :], ctxT[:, k, kt * P:kt * P + r], wv[:, k, :], start=(k == 0), stop=(k == KD - 1))
                        last.then_inc(v_product, 1)
                    pe.wait_ge(v_copied, (b + 1) * NK2)
                    pe.sem_inc(keys_done, 1)

            @block.scalar
            def _(act):
                with act.Fori(0, B) as b:
                    for n, (which, hf, c, w) in enumerate(items):
                        split.scalar(act, n % 2, b * PER + n // 2, w)

            @block.gpsimd
            def _(pool):
                nc.gpsimd.memset(ones[:], 1.0).then_inc(ones_ready, 1)
                nc.gpsimd.memset(V[:], 1.0).then_inc(v_ones, 1)
                with pool.Fori(0, B) as b:
                    for n, (which, hf, c, w) in enumerate(items):
                        split.pool(pool, n % 2, b * PER + n // 2, w)

            @block.vector
            def _(dve):
                v = nc.vector
                dve.wait_ge(loaded, 224)
                v.tensor_copy(idents[0][:], ident[:]).then_inc(cast_ready, 1)
                v.tensor_copy(idents[1][:], ident[:]).then_inc(cast_ready, 1)
                dve.wait_ge(v_ones, 1)
                with dve.Fori(0, B) as b:
                    for n, (which, hf, c, w) in enumerate(items):
                        slot, turn = n % 2, b * PER + n // 2
                        if n == 2:
                            dve.wait_ge(mask_loaded, b * 16 + 16)
                            dve.wait_ge(row_stored, b * 16)
                            v.tensor_scalar(keep[:], mask[:], 0.0, None, ALU.not_equal).then_inc(keep_ready, 1)
                            dve.wait_ge(keep_ready, b + 1)
                            v.tensor_tensor(cosm[:], cosk[:], keep[:], ALU.mult).then_inc(table_ready, 1)
                            v.tensor_tensor(sinm[:], sink[:], keep[:], ALU.mult).then_inc(table_ready, 1)
                            v.tensor_scalar(mask_row[:], keep[0:H, :], 1.0, -NEG, ALU.subtract, ALU.mult).then_inc(row_ready, 1)
                            dve.wait_ge(table_ready, b * 2 + 2)
                        b0, b1 = (bq, bqs) if which == 0 else (bk, bks)
                        cos, sin = (cosq[:, 0:w], sinq[:, 0:w]) if which == 0 else (cosm[:, c:c + w], sinm[:, c:c + w])
                        split.before_t(dve, slot, turn)
                        dve.wait_ge(product[slot], turn + 1)
                        v.scalar_tensor_tensor(split.t[:, slot, 0:w], main_ps[slot][:, 0:w], b0[:, hf:hf + 1], cos, ALU.add, ALU.mult)
                        v.scalar_tensor_tensor(swap[:, slot, 0:w], swap_ps[slot][:, 0:w], b1[:, hf:hf + 1], sin, ALU.add, ALU.mult).then_inc(rotated[slot], 1)
                        dve.wait_ge(rotated[slot], turn + 1)
                        v.tensor_tensor(split.t[:, slot, 0:w], split.t[:, slot, 0:w], swap[:, slot, 0:w], ALU.add).then_inc(split.t_ready[slot], 1)
                    for kt in range(NK2):
                        r = key_rows(kt)
                        dve.wait_ge(v_product, b * NK2 + kt + 1)
                        v.tensor_tensor(V[0:r, kt, ds(b * H * VW, H * VW)].rearrange("p (h v) -> p h v", v=VW)[:, :, 0:DH],
                                        v_ps[kt % 2][0:r, :].rearrange("p (h d) -> p h d", d=DH),
                                        bv[0:r, :].rearrange("p (h d) -> p h d", d=DH), ALU.add).then_inc(v_copied, 1)

    ATT = ctx.enter_context(nc.sbuf_tensor("E_ATT", [P, TPB, UNITS * DH], F32))
    with ExitStack() as own:
        run_heads(nc, Heads(own, nc, "Eh", S2, 1, False, qd, kd, V, ATT, idents, None, dram["strip_sum"], 4, 2,
                            "scores max max scores max last scores max max scores max turn max values token scores "
                            "max max scores max max values max scores max max max max values", 1))
    with ExitStack() as own:
        project_out(nc, own, "Eo", X, XT, ATT, ident, dram["cross_WoT"], dram["bo"])


def phase_ffn(nc, ctx, dram, X, XT, ident, out):
    sb = lambda n, s, dt=F32: ctx.enter_context(nc.sbuf_tensor(f"F_{n}", s, dt))
    ps = lambda n, s: ctx.enter_context(nc.psum_tensor(f"F_{n}", s, F32))
    sem = lambda n: ctx.enter_context(nc.semaphore(f"F_{n}"))

    q1, s1, w1 = sb("q1", [P, KD, F], I32), sb("s1", [P, KD, F]), sb("w1", [P, KD, F])
    q2, s2, w2 = sb("q2", [P, NF, D], I32), sb("s2", [P, NF, D]), sb("w2", [P, NF, D])
    b1, b2 = sb("b1", [P, NF]), sb("b2", [P, D])
    gamma, beta = sb("gamma", [P, KD]), sb("beta", [P, KD])
    XN = sb("XN", [P, NT, D])
    HT = sb("HT", [P, KD, T])
    sig = sb("sig", [P, 2, S])
    act_T = sb("act_T", [P, NF, S])
    turn_ps = [ps(f"turn{h}", [P, S]) for h in range(KD)]
    y1_ps = [ps(f"y1_{i}", [P, S]) for i in range(2)]
    y2_ps = [ps(f"y2_{i}", [P, D]) for i in range(2)]

    norm_in = Norm(ctx, nc, "F_in", X, 1e-5)
    norm_out = Norm(ctx, nc, "F_out", X, LN_EPS)
    loaded1, loaded2, loaded_small = sem("loaded1"), sem("loaded2"), sem("loaded_small")
    w_ready = sem("w_ready")
    turned, copied = sem("turned"), sem("copied")
    y1_ready, sig_ready, act_ready = sem("y1_ready"), sem("sig_ready"), sem("act_ready")
    y2_ready, sum_ready, xb_ready = sem("y2_ready"), sem("sum_ready"), sem("xb_ready")
    half_b2 = sem("half_b2")
    stored = sem("stored")

    with nc.Block() as block:
        @block.sync
        def _(sp):
            sp.dma_start(gamma[:], dram["L1_ffn_ln_gamma"]).then_inc(loaded_small, 16)
            sp.dma_start(beta[:], dram["L1_ffn_ln_beta"]).then_inc(loaded_small, 16)
            sp.dma_start(b1[:], dram["L1_ffn_fc1_bias"]).then_inc(loaded_small, 16)
            sp.dma_start(b2[:], dram["L1_ffn_fc2_bias"].partition_broadcast(P)).then_inc(loaded_small, 16)
            sp.dma_start(q1[:], dram["L1_ffn_fc1_q"].rearrange("(k p) f -> p k f", p=P)).then_inc(loaded1, 16)
            sp.dma_start(s1[:], dram["L1_ffn_fc1_scales"].partition_broadcast(P)).then_inc(loaded1, 16)
            sp.dma_start(q2[:], dram["L1_ffn_fc2_q"].rearrange("(k p) f -> p k f", p=P)).then_inc(loaded2, 16)
            sp.dma_start(s2[:], dram["L1_ffn_fc2_scales"].partition_broadcast(P)).then_inc(loaded2, 16)
            for c in range(B):
                sp.wait_ge(norm_out.normed, (c + 1) * TPB)
                sp.dma_start(out[c * S:(c + 1) * S, :].rearrange("(t p) d -> p t d", p=P),
                             X[:, c * TPB:(c + 1) * TPB, :]).then_inc(stored, 16)
            sp.wait_ge(stored, 16 * B)

        @block.gpsimd
        def _(pool):
            norm_in.setup(pool)
            norm_out.setup(pool)
            for c in range(B):
                norm_in.inverse_deviation(pool, c)
            for c in range(B):
                norm_out.inverse_deviation(pool, c)

        @block.scalar
        def _(act):
            act.wait_ge(loaded_small, 64)
            for c in range(B):
                for h in range(KD):
                    act.wait_ge(turned, KD * c + h + 1)
                    nc.scalar.activation(HT[:, h, c * S:(c + 1) * S], turn_ps[h][:], ACT.Identity,
                                         bias=beta[:, h:h + 1], scale=gamma[:, h:h + 1]).then_inc(copied, 1)
            with act.Fori(0, B) as c:
                for j in range(NF):
                    n = c * NF + j
                    act.wait_ge(y1_ready, n + 1)
                    if j >= 2:
                        act.wait_ge(act_ready, n - 1)
                    nc.scalar.activation(sig[:, j % 2, :], y1_ps[j % 2][:], ACT.Sigmoid,
                                         bias=b1[:, j:j + 1]).then_inc(sig_ready, 1)

        @block.vector
        def _(dve):
            for c in range(B):
                for t in range(c * TPB, (c + 1) * TPB):
                    nc.vector.bn_stats(norm_in.stats_buf[:, t, :], X[:, t, :]).then_inc(norm_in.stats_ready, 1)
                for t in range(c * TPB, (c + 1) * TPB):
                    dve.wait_ge(norm_in.stats_ready, t + 1)
                    nc.vector.bn_aggr(norm_in.mv[:, t, :], norm_in.stats_buf[:, t, :]).then_inc(norm_in.mv_ready, 1)
            dve.wait_ge(loaded1, 32)
            nc.vector.scalar_tensor_tensor(w1[:].rearrange("p k f -> p (k f)"), q1[:].rearrange("p k f -> p (k f)"), -128.0, s1[:].rearrange("p k f -> p (k f)"), ALU.add, ALU.mult).then_inc(w_ready, 1)
            for c in range(B):
                norm_in.normalize(dve, c, XN)
            dve.wait_ge(loaded2, 32)
            nc.vector.scalar_tensor_tensor(w2[:].rearrange("p k f -> p (k f)"), q2[:].rearrange("p k f -> p (k f)"), -128.0, s2[:].rearrange("p k f -> p (k f)"), ALU.add, ALU.mult).then_inc(w_ready, 1)
            dve.wait_ge(loaded_small, 64)
            nc.vector.tensor_scalar(b2[:], b2[:], 0.5, None, ALU.mult).then_inc(half_b2, 1)
            dve.wait_ge(half_b2, 1)
            for t in range(NT):
                nc.vector.scalar_tensor_tensor(X[:, t, :], X[:, t, :], 2.0, b2[:], ALU.mult, ALU.add).then_inc(xb_ready, 1)
            dve.wait_ge(xb_ready, NT)
            with dve.Fori(0, B) as c:
                for j in range(NF):
                    n = c * NF + j
                    dve.wait_ge(sig_ready, n + 1)
                    nc.vector.scalar_tensor_tensor(act_T[:, j, :], y1_ps[j % 2][:], b1[:, j:j + 1], sig[:, j % 2, :],
                                                   ALU.add, ALU.mult).then_inc(act_ready, 1)
                for t in range(TPB):
                    n = c * TPB + t
                    dve.wait_ge(y2_ready, n + 1)
                    x = X[:, ds(n, 1), :].rearrange("p a d -> p (a d)")
                    nc.vector.scalar_tensor_tensor(x, y2_ps[t % 2][:], 0.5, x, ALU.mult, ALU.add).then_inc(sum_ready, 1)
            for c in range(B):
                norm_out.statistics(dve, c, sum_ready)
            for c in range(B):
                norm_out.normalize(dve, c)

        @block.tensor
        def _(pe):
            for c in range(B):
                turn_group(nc, pe, XN, ident[:], turn_ps, c, norm_in.normed, copied, turned)
            pe.wait_ge(copied, KD * B)
            pe.wait_ge(w_ready, 2)
            with pe.Fori(0, B) as c:
                for j in range(NF):
                    n = c * NF + j
                    if j >= 2:
                        pe.wait_ge(act_ready, n - 1)
                    for k in range(KD):
                        last = nc.tensor.matmul(y1_ps[j % 2][:], w1[:, k, j * P:(j + 1) * P], HT[:, k, ds(c * S, S)],
                                                start=(k == 0), stop=(k == KD - 1))
                    last.then_inc(y1_ready, 1)
                pe.wait_ge(act_ready, (c + 1) * NF)
                for t in range(TPB):
                    n = c * TPB + t
                    if t >= 2:
                        pe.wait_ge(sum_ready, n - 1)
                    for j in range(NF):
                        last = nc.tensor.matmul(y2_ps[t % 2][:], act_T[:, j, t * P:(t + 1) * P], w2[:, j, :],
                                                start=(j == 0), stop=(j == NF - 1))
                    last.then_inc(y2_ready, 1)
                pe.wait_ge(sum_ready, (c + 1) * TPB)


def lay_out(a, rows, columns):
    x = a["x"].reshape(T, D)
    i, j = np.meshgrid(np.arange(P), np.arange(P))
    quadrant = [((i >> m + 1) == (j >> m + 1)) & ((i >> m) % 2 == 1) & ((j >> m) % 2 == 0) for m in range(LEVELS)]
    ttt_masks = np.stack([q.astype(np.float32) for q in quadrant] + [quadrant[0].T.astype(np.float32),
                         np.where(j <= i, -ETA, 0.0).astype(np.float32)], axis=1)
    causal_tri = np.where(np.stack([i > j, j > i], axis=1), -10000.0, 0.0).astype(np.float32)
    block = np.arange(S) // P
    q_rows = [(block == t) * 1.0 for t in range(TPB - 1) for _ in range(2)]
    k_rows = [(block > t) * v for t in range(TPB - 1) for v in (-9984.0, -16.0)] + [np.ones(S)] * 2
    causal_rows = np.tile(np.array(q_rows + k_rows, np.float32), (UNITS, 1, 1))
    swapped = np.arange(D) ^ 1
    inv_freq = (1.0 / 10000.0 ** (np.arange(0, DH, 2, dtype=np.float32) / np.float32(DH))).astype(np.float32)
    angle = np.arange(S2, dtype=np.float32)[None, :] * np.concatenate([inv_freq, inv_freq])[:, None]
    sign = np.where(np.arange(DH) % 2 == 0, -1.0, 1.0)[:, None]
    cos = np.tile(np.cos(angle.astype(np.float64)), (P // DH, 1)).astype(np.float32)
    sin = np.tile(np.sin(angle.astype(np.float64)) * sign, (P // DH, 1)).astype(np.float32)
    laid = {
        "ttt_masks": ttt_masks,
        "L0_xattn_W1": a["L0_xattn_W1"], "xW2T": a["L0_xattn_W2"].T,
        "L0_xattn_b1": columns(a["L0_xattn_b1"]), "L0_xattn_b2": columns(a["L0_xattn_b2"]),
        "ctx": a["ctx_1024"], "ctxT": a["ctx_1024"].transpose(0, 2, 1), "fside": a["fside_1xSxS2_0"][0],
        "L0_ffn_Wr": a["L0_ffn_Wr"].reshape(KD, P, E).transpose(1, 0, 2), "L0_ffn_br": np.tile(a["L0_ffn_br"], (P, 1)),
        "lanes": np.tile(np.arange(E, dtype=np.float32), (P, 1)),
        "L0_ffn_bi": a["L0_ffn_bi"].reshape(E, NF, P).transpose(2, 0, 1),
        "L0_ffn_bg": a["L0_ffn_bg"].reshape(E, NF, P).transpose(2, 0, 1),
        "L0_ffn_Wi": a["L0_ffn_Wi"], "L0_ffn_Wg": a["L0_ffn_Wg"], "L0_ffn_Wo": a["L0_ffn_Wo"],
        "expert_tail": np.tile(np.stack([a["L0_ffn_bo"], a["L0_ffn_gamma"], a["L0_ffn_beta"]], axis=1), (P, 1, 1, 1)),
        "wqkvT": a["L1_attn_w_qkv"].T, "self_WoT": a["L1_attn_w_out"].T,
        "causal_tri": causal_tri, "causal_rows": causal_rows,
        "wqT": a["L1_xattn_Wq"].T, "wqT_swapped": a["L1_xattn_Wq"].T[:, swapped],
        "wkT": a["L1_xattn_Wk"].T, "wkT_swapped": a["L1_xattn_Wk"].T[:, swapped], "wvT": a["L1_xattn_Wv"].T,
        "bq": columns(a["L1_xattn_bq"]), "bq_swapped": columns(a["L1_xattn_bq"][swapped]),
        "bk": columns(a["L1_xattn_bk"]), "bk_swapped": columns(a["L1_xattn_bk"][swapped]),
        "bv": a["L1_xattn_bv"], "bo": a["L1_xattn_bo"], "cross_WoT": a["L1_xattn_Wo"].T,
        "cosq": cos[:, :S] * np.float32(0.25), "sinq": sin[:, :S] * np.float32(0.25), "cosk": cos, "sink": sin,
        "mask": np.repeat(a["mask_BxS2_if1"][:, None, :], P, axis=1),
        "thKT": a["L0_attn_theta_K"].T, "thQT": a["L0_attn_theta_Q"].T, "thVT": a["L0_attn_theta_V"].T,
        "L0_attn_theta_K": a["L0_attn_theta_K"], "L0_attn_theta_Q": a["L0_attn_theta_Q"],
        "W0T": a["L0_attn_W0"].T, "L0_attn_b0": a["L0_attn_b0"],
        "strip_sum": np.tile(np.eye(STRIP, VW, dtype=np.float32), (STRIPS, 1)),
        "identity": np.eye(P, dtype=np.float32),
        "x": x,
        "xT": x.T,
        "L1_ffn_ln_gamma": columns(a["L1_ffn_ln_gamma"]),
        "L1_ffn_ln_beta": columns(a["L1_ffn_ln_beta"]),
        "L1_ffn_fc1_q": a["L1_ffn_fc1_q"],
        "L1_ffn_fc1_scales": a["L1_ffn_fc1_scales"],
        "L1_ffn_fc1_bias": columns(a["L1_ffn_fc1_bias"]),
        "L1_ffn_fc2_q": a["L1_ffn_fc2_q"],
        "L1_ffn_fc2_scales": a["L1_ffn_fc2_scales"],
        "L1_ffn_fc2_bias": a["L1_ffn_fc2_bias"],
    }
    return laid


def phase_load(nc, ctx, dram, X, XT, ident):
    loaded = ctx.enter_context(nc.semaphore("load_loaded"))
    with nc.Block() as block:
        @block.sync
        def _(sp):
            sp.dma_start(ident[:], dram["identity"]).then_inc(loaded, 16)
            sp.dma_start(XT[:], dram["xT"].rearrange("(k p) t -> p k t", p=P)).then_inc(loaded, 16)
            sp.dma_start(X[:], dram["x"].rearrange("(t p) d -> p t d", p=P)).then_inc(loaded, 16)
            sp.wait_ge(loaded, 48)


def phase_store(nc, ctx, X, out):
    stored = ctx.enter_context(nc.semaphore("store_stored"))
    with nc.Block() as block:
        @block.sync
        def _(sp):
            sp.dma_start(out.rearrange("(t p) d -> p t d", p=P), X[:]).then_inc(stored, 16)
            sp.wait_ge(stored, 16)


def renew_semaphores(nc):
    released = nc.released_uncleared_semaphores
    nc.all_engine_barrier(sems_to_clear=range(min(released), max(released) + 1))


def build_program(nc, dram, out):
    with ExitStack() as ctx:
        X = ctx.enter_context(nc.sbuf_tensor("X", [P, NT, D], F32))
        XT = ctx.enter_context(nc.sbuf_tensor("XT", [P, KD, T], F32))
        ident = ctx.enter_context(nc.sbuf_tensor("ident", [P, P], F32))
        phase_load(nc, ctx, dram, X, XT, ident)
        table = {"A": phase_ttt, "B": phase_cross0, "C": phase_moe, "D": phase_self, "E": phase_cross1}
        for name in PHASES:
            with ExitStack() as own:
                if name == "F":
                    phase_ffn(nc, own, dram, X, XT, ident, out)
                else:
                    table[name](nc, own, dram, X, XT, ident)
            renew_semaphores(nc)
        if "F" not in PHASES:
            phase_store(nc, ctx, X, out)


def kernel(**inputs):
    import concourse.bacc as bacc
    from concourse.bass_utils import run_bass_kernel_spmd

    a = {k: np.asarray(v) for k, v in inputs.items()}
    rows = lambda v: v.reshape(1, -1)
    columns = lambda v: np.ascontiguousarray(v.reshape(-1, P).T)
    laid = lay_out(a, rows, columns)
    nc = bacc.Bacc("TRN2", target_bir_lowering=False, num_devices=1)
    arrays, dram = {}, {}
    for name, v in laid.items():
        v = np.ascontiguousarray(v)
        arrays[f"in_{name}_dram"] = v
        dram[name] = nc.dram_tensor(f"in_{name}_dram", v.shape, mybir.dt.from_np(v.dtype), kind="ExternalInput").ap()
    out = nc.dram_tensor("out_0_dram", (T, D), F32, kind="ExternalOutput").ap()
    build_program(nc, dram, out)
    r = run_bass_kernel_spmd(nc, [arrays], core_ids=[0])
    return r.results[0]["out_0_dram"].reshape(B, S, D)
```

```python
from contextlib import ExitStack

import numpy as np

import concourse.bass as bass
from concourse import mybir

P = 128
B, S, D = 4, 512, 256
T = B * S
NT = T // P
KD = D // P
TPB = S // P
S2 = 1601
NK2 = (S2 + P - 1) // P
F = 1024
NF = F // P
E = 8
H, DH = 16, 16
LN_EPS = 1e-5

F32 = mybir.dt.float32
F16 = mybir.dt.float16
BF16 = mybir.dt.bfloat16
I32 = mybir.dt.int32
ALU = mybir.AluOpType
ACT = mybir.ActivationFunctionType
AX_X = mybir.AxisListType.X
ds = bass.ds


class Norm:

    def __init__(self, ctx, nc, name, X, eps):
        self.nc, self.X, self.eps = nc, X, eps
        sb = lambda n, s: ctx.enter_context(nc.sbuf_tensor(f"{name}_{n}", s, F32))
        sem = lambda n: ctx.enter_context(nc.semaphore(f"{name}_{n}"))
        self.stats_buf = sb("stats", [P, NT, 6])
        self.mv = sb("mv", [P, NT, 2])
        self.var_eps = sb("var_eps", [P, NT])
        self.rstd = sb("rstd", [P, NT])
        self.neg_half = sb("neg_half", [P, NT])
        self.half_ready = sem("half_ready")
        self.stats_ready = sem("stats_ready")
        self.mv_ready = sem("mv_ready")
        self.ve_ready = sem("ve_ready")
        self.rstd_ready = sem("rstd_ready")
        self.normed = sem("normed")

    def setup(self, pool):
        self.nc.gpsimd.memset(self.neg_half[:], -0.5).then_inc(self.half_ready, 1)
        pool.wait_ge(self.half_ready, 1)

    def statistics(self, dve, c, sum_ready, first=0):
        for t in range(c * TPB, (c + 1) * TPB):
            dve.wait_ge(sum_ready, first + t + 1)
            self.nc.vector.bn_stats(self.stats_buf[:, t, :], self.X[:, t, :]).then_inc(self.stats_ready, 1)
        for t in range(c * TPB, (c + 1) * TPB):
            dve.wait_ge(self.stats_ready, t + 1)
            self.nc.vector.bn_aggr(self.mv[:, t, :], self.stats_buf[:, t, :]).then_inc(self.mv_ready, 1)

    def inverse_deviation(self, pool, c):
        g = slice(c * TPB, (c + 1) * TPB)
        pool.wait_ge(self.mv_ready, (c + 1) * TPB)
        self.nc.gpsimd.tensor_scalar(self.var_eps[:, g], self.mv[:, g, 1], self.eps, 1.0,
                                     ALU.add, ALU.mult).then_inc(self.ve_ready, 1)
        pool.wait_ge(self.ve_ready, c + 1)
        self.nc.gpsimd.tensor_tensor(self.rstd[:, g], self.var_eps[:, g], self.neg_half[:, g],
                                     ALU.pow).then_inc(self.rstd_ready, 1)

    def normalize(self, dve, c, out=None):
        out = self.X if out is None else out
        dve.wait_ge(self.rstd_ready, c + 1)
        for t in range(c * TPB, (c + 1) * TPB):
            self.nc.vector.tensor_scalar(out[:, t, :], self.X[:, t, :], self.mv[:, t, 0:1], self.rstd[:, t:t + 1],
                                         ALU.subtract, ALU.mult).then_inc(self.normed, 1)

    def finish(self, dve, sum_ready, first=0, out=None):
        for c in range(B + 1):
            if c < B:
                self.statistics(dve, c, sum_ready, first)
            if c >= 1:
                self.normalize(dve, c - 1, out)


def turn_group(nc, pe, src, ident, banks, c, normed, copied, turned):
    pe.wait_ge(normed, (c + 1) * TPB)
    if c >= 1:
        pe.wait_ge(copied, KD * c)
    for h in range(KD):
        for t in range(TPB):
            last = nc.tensor.transpose(banks[h][:, t * P:(t + 1) * P], src[:, c * TPB + t, h * P:(h + 1) * P], ident)
        last.then_inc(turned, 1)


def copy_turned(nc, act, dst, banks, c, turned, copied):
    for h in range(KD):
        act.wait_ge(turned, KD * c + h + 1)
        nc.scalar.activation(dst[:, h, c * S:(c + 1) * S], banks[h][:], ACT.Copy).then_inc(copied, 1)


LEVELS = 7
ETA = 0.01 * 2.0 / D


def phase_ttt(nc, ctx, dram, X, XT, ident):
    sb = lambda n, s, dt=F32: ctx.enter_context(nc.sbuf_tensor(f"A_{n}", s, dt))
    sem = lambda n: ctx.enter_context(nc.semaphore(f"A_{n}"))
    thKT, thQT, thVT = (sb(n, [P, KD, D]) for n in ("thKT", "thQT", "thVT"))
    thK, thQ, W0T = (sb(n, [P, KD, D]) for n in ("thK", "thQ", "W0T"))
    b0 = sb("b0", [P, D])
    masks = sb("masks", [P, LEVELS + 2, P])
    M1, M2 = sb("M1", [P, KD, D]), sb("M2", [P, KD, D])
    KT, QT = sb("KT", [P, KD, T]), sb("QT", [P, KD, T])
    ROW = TPB * S
    GN = sb("GN", [P, B * ROW + S])
    GQ = sb("GQ", [P, B * ROW])
    XI, YI = sb("XI", [P, B, S]), sb("YI", [P, B, S])
    CT = sb("CT", [P, 4, S])
    P1 = sb("P1", [P, 2, S])
    R = sb("R", [P, 2, D])
    U = KT[:, :, :].rearrange("p k t -> p (k t)").rearrange("p (n d) -> p n d", d=D)
    banks = [ctx.enter_context(nc.psum_tensor(f"A_bank{i}", [P, S], F32)) for i in range(8)]

    norm = Norm(ctx, nc, "A_norm", X, LN_EPS)
    loaded, small_loaded, xT_loaded, x_loaded = sem("loaded"), sem("small_loaded"), sem("xT_loaded"), sem("x_loaded")
    product, act_copied, dve_copied = sem("product"), sem("act_copied"), sem("dve_copied")
    mask_ready, start_tmp, start_ready = sem("mask_ready"), sem("start_tmp"), sem("start_ready")
    cx_ready, cx_copied = sem("cx_ready"), sem("cx_copied")
    xcx_ready, inv_ready = sem("xcx_ready"), sem("inv_ready")
    acc_ready, rhs_ready, u_ready, u_copied = sem("acc_ready"), sem("rhs_ready"), sem("u_ready"), sem("u_copied")
    out_ready, sum_ready, xb_ready = sem("out_ready"), sem("sum_ready"), sem("xb_ready")
    turned, copied = sem("turned"), sem("copied")

    plain = [("M2", h) for h in range(KD)] + [("M1", h) for h in range(KD)]
    plain += [(w, (h, b)) for b in range(B) for h in range(KD) for w in ("KT", "QT")]
    plain += [(w, (b, j)) for b in range(B) for j in range(TPB) for w in ("GK", "GQ")]
    by_act = {"M2", "KT", "GK"}
    order = []
    for kind, _ in plain:
        mine = kind in by_act
        order.append((mine, 1 + sum(1 for m, _ in order if m == mine)))

    def wait_copied(eng, n):
        mine, count = order[n]
        eng.wait_ge(act_copied if mine else dve_copied, count)

    last_proj = max(n for n, (k, _) in enumerate(plain) if k in ("KT", "QT"))
    pairs = [(0, 1), (2, 3)]
    steps = [(m, b) for pair in pairs for m in range(1, LEVELS) for b in pair]
    step_no = {s: n for n, s in enumerate(steps)}
    blocks = [(b, i) for i in range(TPB) for b in range(B)]

    def diagonal(b):
        v = GN[:, b * ROW:b * ROW + TPB * (S + P)].rearrange("p (j c) -> p j c", c=S + P)
        return v[:, :, 0:P]

    def four(m):
        return masks[:, m:m + 1, :].broadcast_to([P, TPB, P])

    def view(t):
        return t.rearrange("p (j c) -> p j c", c=P)

    with nc.Block() as block:
        @block.sync
        def _(sp):
            sp.dma_start(ident[:], dram["identity"]).then_inc(loaded, 16)
            for t, n in ((thQ, "L0_attn_theta_Q"), (thK, "L0_attn_theta_K"), (W0T, "W0T"), (thVT, "thVT"), (thKT, "thKT"), (thQT, "thQT")):
                sp.dma_start(t[:], dram[n].rearrange("(k p) d -> p k d", p=P)).then_inc(loaded, 16)
            sp.dma_start(XT[:], dram["xT"].rearrange("(k p) t -> p k t", p=P)).then_inc(xT_loaded, 16)
            sp.dma_start(b0[:], dram["L0_attn_b0"].partition_broadcast(P)).then_inc(small_loaded, 16)
            sp.dma_start(masks[:], dram["ttt_masks"]).then_inc(small_loaded, 16)
            sp.dma_start(X[:], dram["x"].rearrange("(t p) d -> p t d", p=P)).then_inc(x_loaded, 16)

        @block.tensor
        def _(pe):
            mm = nc.tensor.matmul
            pe.wait_ge(loaded, 112)
            for n, (kind, w) in enumerate(plain):
                bank = banks[n % 8]
                if n >= 8:
                    wait_copied(pe, n - 8)
                if n == 2 * KD:
                    pe.wait_ge(xT_loaded, 16)
                if kind in ("GK", "GQ") and w == (0, 0) and kind == "GK":
                    wait_copied(pe, last_proj)
                    wait_copied(pe, last_proj - 1)
                for k in range(KD):
                    if kind in ("M1", "M2"):
                        lhsT, rhs, o = (thK if kind == "M1" else thQ)[:, k, w * P:(w + 1) * P], W0T[:, k, :], bank[:, 0:D]
                    elif kind in ("KT", "QT"):
                        h, b = w
                        lhsT, rhs, o = (thKT if kind == "KT" else thQT)[:, k, h * P:(h + 1) * P], XT[:, k, b * S:(b + 1) * S], bank[:]
                    else:
                        b, j = w
                        at = b * S + j * P
                        lhsT = KT[:, k, at:at + P]
                        rhs = (KT if kind == "GK" else QT)[:, k, at:(b + 1) * S]
                        o = bank[:, j * P:S]
                    last = mm(o, lhsT, rhs, start=(k == 0), stop=(k == KD - 1))
                last.then_inc(product, 1)
            for n in range(len(plain) - 8, len(plain)):
                wait_copied(pe, n)
            for n, (m, b) in enumerate(steps):
                s = b % 2
                cx, xcx, ycx = banks[3 * s], banks[3 * s + 1], banks[3 * s + 2]
                pe.wait_ge(mask_ready, n + 1)
                if m == 1:
                    pe.wait_ge(start_ready, 2 * (b + 1))
                else:
                    pe.wait_ge(inv_ready, 2 * (step_no[(m - 1, b)] + 1))
                if b >= 2 and m == 1:
                    pe.wait_ge(inv_ready, 2 * (step_no[(LEVELS - 1, b - 2)] + 1))
                for j in range(TPB):
                    c = slice(j * P, (j + 1) * P)
                    last = mm(cx[:, c], CT[:, n % 4, c], XI[:, b, c], start=True, stop=True)
                last.then_inc(cx_ready, 1)
                pe.wait_ge(cx_copied, n + 1)
                for j in range(TPB):
                    c = slice(j * P, (j + 1) * P)
                    mm(xcx[:, c], YI[:, b, c], P1[:, s, c], start=True, stop=True)
                for j in range(TPB):
                    c = slice(j * P, (j + 1) * P)
                    last = mm(ycx[:, c], P1[:, s, c], YI[:, b, c], start=True, stop=True)
                last.then_inc(xcx_ready, 1)
            pe.wait_ge(inv_ready, 2 * len(steps))
            for n, (b, i) in enumerate(blocks):
                tok = slice(b * S + i * P, b * S + (i + 1) * P)
                acc, u_ps, out_ps = banks[n % 2], banks[2 + n % 2], banks[4 + n % 2]
                if n >= 2:
                    pe.wait_ge(rhs_ready, n - 1)
                for k in range(KD):
                    last = mm(acc[:, 0:D], XT[:, k, tok], M1[:, k, :], start=(k == 0), stop=(i == 0 and k == KD - 1))
                if i > 0:
                    pe.wait_ge(u_copied, (i - 1) * B + b + 1)
                for j in range(i):
                    last = mm(acc[:, 0:D], GN[:, b * ROW + j * S + i * P:b * ROW + j * S + (i + 1) * P],
                              U[:, b * TPB + j, :], start=False, stop=(j == i - 1))
                last.then_inc(acc_ready, 1)
                if n >= 2:
                    pe.wait_ge(sum_ready, n - 1)
                for k in range(KD):
                    mm(out_ps[:, 0:D], XT[:, k, tok], M2[:, k, :], start=(k == 0), stop=False)
                for j in range(i):
                    mm(out_ps[:, 0:D], GQ[:, b * ROW + j * S + i * P:b * ROW + j * S + (i + 1) * P],
                       U[:, b * TPB + j, :], start=False, stop=False)
                pe.wait_ge(rhs_ready, n + 1)
                if n >= 2:
                    pe.wait_ge(u_copied, n - 1)
                mm(u_ps[:, 0:D], YI[:, b, i * P:(i + 1) * P], R[:, n % 2, :], start=True, stop=True).then_inc(u_ready, 1)
                pe.wait_ge(u_copied, n + 1)
                mm(out_ps[:, 0:D], GQ[:, b * ROW + i * (S + P):b * ROW + i * (S + P) + P],
                   U[:, b * TPB + i, :], start=False, stop=True).then_inc(out_ready, 1)
            pe.wait_ge(sum_ready, NT)
            for c in range(B):
                turn_group(nc, pe, X, ident[:], banks, c, norm.normed, copied, turned)

        @block.scalar
        def _(act):
            for n, (kind, w) in enumerate(plain):
                if kind not in by_act:
                    continue
                act.wait_ge(product, n + 1)
                bank = banks[n % 8]
                if kind == "M2":
                    o = nc.scalar.activation(M2[:, w, :], bank[:, 0:D], ACT.Copy)
                elif kind == "KT":
                    h, b = w
                    o = nc.scalar.activation(KT[:, h, b * S:(b + 1) * S], bank[:], ACT.Copy)
                else:
                    b, j = w
                    o = nc.scalar.activation(GN[:, b * ROW + j * (S + P):b * ROW + (j + 1) * S], bank[:, j * P:S],
                                             ACT.Copy, bias=-ETA, scale=-ETA)
                o.then_inc(act_copied, 1)
            for n, (m, b) in enumerate(steps):
                act.wait_ge(cx_ready, n + 1)
                if n >= 2:
                    act.wait_ge(xcx_ready, n - 1)
                nc.scalar.activation(P1[:, b % 2, :], banks[3 * (b % 2)][:], ACT.Copy).then_inc(cx_copied, 1)
            for n, (b, i) in enumerate(blocks):
                act.wait_ge(u_ready, n + 1)
                nc.scalar.activation(U[:, b * TPB + i, :], banks[2 + n % 2][:, 0:D], ACT.Copy).then_inc(u_copied, 1)
            for c in range(B):
                copy_turned(nc, act, XT, banks, c, turned, copied)

        @block.gpsimd
        def _(pool):
            norm.setup(pool)
            pool.wait_ge(loaded, 112)
            pool.wait_ge(small_loaded, 32)
            tt = nc.gpsimd.tensor_tensor

            def start(b):
                for q, (m, dst) in enumerate(((LEVELS, XI), (0, YI))):
                    tt(view(dst[:, b, :]), diagonal(b), four(m), ALU.mult).then_inc(start_tmp, 1)
                    pool.wait_ge(start_tmp, 2 * b + q + 1)
                    tt(view(dst[:, b, :]), view(dst[:, b, :]), ident[:].rearrange("p (a c) -> p a c", a=1).broadcast_to([P, TPB, P]),
                       ALU.add).then_inc(start_ready, 1)

            for n, (m, b) in enumerate(steps):
                if m == 1:
                    wait_copied(pool, plain.index(("GK", (b, TPB - 1))))
                    start(b)
                if n >= 4:
                    pool.wait_ge(cx_ready, n - 3)
                tt(view(CT[:, n % 4, :]), diagonal(b), four(m), ALU.mult).then_inc(mask_ready, 1)
            for c in range(B):
                norm.inverse_deviation(pool, c)

        @block.vector
        def _(dve):
            dve.wait_ge(loaded, 112)
            dve.wait_ge(small_loaded, 32)
            for n, (kind, w) in enumerate(plain):
                if kind in by_act:
                    continue
                dve.wait_ge(product, n + 1)
                bank = banks[n % 8]
                if kind == "M1":
                    o = nc.vector.tensor_tensor(M1[:, w, :], bank[:, 0:D], thVT[:, w, :], ALU.subtract)
                elif kind == "QT":
                    h, b = w
                    o = nc.vector.tensor_copy(QT[:, h, b * S:(b + 1) * S], bank[:])
                else:
                    b, j = w
                    at = b * ROW + j * (S + P)
                    o = nc.vector.scalar_tensor_tensor(GQ[:, at:at + P], bank[:, j * P:(j + 1) * P], 1.0,
                                                       masks[:, LEVELS + 1, :], ALU.add, ALU.mult)
                    if j < TPB - 1:
                        o = nc.vector.tensor_scalar(GQ[:, at + P:b * ROW + (j + 1) * S], bank[:, (j + 1) * P:S],
                                                    1.0, -ETA, ALU.add, ALU.mult)
                o.then_inc(dve_copied, 1)
            dve.wait_ge(x_loaded, 16)
            for t in range(NT):
                nc.vector.tensor_tensor(X[:, t, :], X[:, t, :], b0[:], ALU.add).then_inc(xb_ready, 1)
            for n, (m, b) in enumerate(steps):
                dve.wait_ge(xcx_ready, n + 1)
                s = b % 2
                nc.vector.tensor_tensor(XI[:, b, :], XI[:, b, :], banks[3 * s + 1][:], ALU.add).then_inc(inv_ready, 1)
                nc.vector.tensor_tensor(YI[:, b, :], YI[:, b, :], banks[3 * s + 2][:], ALU.add).then_inc(inv_ready, 1)
            dve.wait_ge(xb_ready, NT)

            def add_out(n):
                b, i = blocks[n]
                dve.wait_ge(out_ready, n + 1)
                x = X[:, b * TPB + i, :]
                nc.vector.tensor_tensor(x, banks[4 + n % 2][:, 0:D], x, ALU.add).then_inc(sum_ready, 1)

            for n in range(NT):
                dve.wait_ge(acc_ready, n + 1)
                if n >= 2:
                    dve.wait_ge(u_ready, n - 1)
                nc.vector.tensor_tensor(R[:, n % 2, :], banks[n % 2][:, 0:D], b0[:], ALU.add).then_inc(rhs_ready, 1)
                add_out(n)
            dve.wait_ge(sum_ready, NT)
            norm.finish(dve, sum_ready)


def key_rows(kt):
    return min(P, S2 - kt * P)


def phase_cross0(nc, ctx, dram, X, XT, ident):
    sb = lambda n, s, dt=F32: ctx.enter_context(nc.sbuf_tensor(f"B_{n}", s, dt))
    sem = lambda n: ctx.enter_context(nc.semaphore(f"B_{n}"))
    W1, W2T = sb("W1", [P, KD, D]), sb("W2T", [P, KD, D])
    b1, b2, b12 = sb("b1", [P, KD]), sb("b2", [P, KD]), sb("b12", [P, KD])
    W12T, W12 = sb("W12T", [P, KD, D]), sb("W12", [P, KD, D])
    ctxT = sb("ctxT", [P, 2, KD, S2])
    ctxN = sb("ctxN", [P, 2, NK2, D])
    bias = sb("bias", [P, TPB, S2])
    qpT, q2T = sb("qpT", [P, KD, S]), sb("q2T", [P, KD, S])
    probs = sb("probs", [P, 2, S2])
    PT = sb("PT", [P, 2, NK2, P])
    top, neg_top, total, inv_total = (sb(n, [P, 2]) for n in ("top", "neg_top", "total", "inv_total"))
    fence = sb("fence", [P, 1])
    scores_ps = ctx.enter_context(nc.psum_tensor("B_scores", [P, 4 * S], F32))
    ring = [ctx.enter_context(nc.psum_tensor(f"B_ring{i}", [P, S], F32)) for i in range(2)]
    av_ps = ctx.enter_context(nc.psum_tensor("B_av", [P, D], F32))

    norm = Norm(ctx, nc, "B_norm", X, LN_EPS)
    loaded, bias_loaded = sem("loaded"), sem("bias_loaded")
    ctx_loaded = [sem(f"ctx_loaded{i}") for i in range(2)]
    w_product, w_copied = sem("w_product"), sem("w_copied")
    ring_ready, act_copied, dve_copied = sem("ring_ready"), sem("act_copied"), sem("dve_copied")
    scores_ready, scores_read, max_ready, probs_ready = sem("scores_ready"), sem("scores_read"), sem("max_ready"), sem("probs_ready")
    av_ready, inv_ready, sum_ready = sem("av_ready"), sem("inv_ready"), sem("sum_ready")
    turned, copied = sem("turned"), sem("copied")

    RING, BY_ACT, BY_DVE = 4 + 4 * TPB, 4 + 2 * TPB, 2 * TPB
    groups = [range(g * 4, min(g * 4 + 4, NK2)) for g in range(4)]

    with nc.Block() as block:
        @block.sync
        def _(sp):
            sp.dma_start(W1[:], dram["L0_xattn_W1"].rearrange("(k p) d -> p k d", p=P)).then_inc(loaded, 16)
            sp.dma_start(W2T[:], dram["xW2T"].rearrange("(k p) d -> p k d", p=P)).then_inc(loaded, 16)
            sp.dma_start(b1[:], dram["L0_xattn_b1"]).then_inc(loaded, 16)
            sp.dma_start(b2[:], dram["L0_xattn_b2"]).then_inc(loaded, 16)
            with sp.Fori(0, B // 2) as bb:
                for u in range(2):
                    b = bb * 2 + u
                    sp.wait_ge(av_ready, bb * 2 * TPB)
                    sp.dma_start(ctxT[:, u], dram["ctxT"][ds(b, 1)].rearrange("b (k p) s -> p (b k) s", p=P)).then_inc(ctx_loaded[u], 16)
                    sp.dma_start(ctxN[:, u, 0:NK2 - 1, :], dram["ctx"][ds(b, 1), 0:(NK2 - 1) * P].rearrange("b (k p) d -> p (b k) d", p=P)).then_inc(ctx_loaded[u], 16)
                    sp.dma_start(ctxN[0:key_rows(NK2 - 1), u, NK2 - 1, :], dram["ctx"][ds(b, 1), (NK2 - 1) * P:S2].rearrange("b p d -> (b p) d")).then_inc(ctx_loaded[u], 16)

        @block.tensor
        def _(pe):
            mm = nc.tensor.matmul
            pe.wait_ge(loaded, 64)
            for n in range(6):
                kind, h = n // 2, n % 2
                if n >= 2:
                    pe.wait_ge(w_copied, n - 1)
                for k in range(KD):
                    lhsT = (W1 if kind == 0 else W2T)[:, k, h * P:(h + 1) * P]
                    rhs = (W2T[:, k, :], W1[:, k, :], b1[:, k:k + 1])[kind]
                    last = mm(ring[h][:, 0:1] if kind == 2 else ring[h][:, 0:D], lhsT, rhs, start=(k == 0), stop=(k == KD - 1))
                last.then_inc(w_product, 1)
            pe.wait_ge(w_copied, 6)

            def scores(b, u, t):
                n = b * TPB + t
                pe.wait_ge(scores_read, n)
                for c in range(4):
                    w = min(S, S2 - c * S)
                    for k in range(KD):
                        last = mm(scores_ps[:, c * S:c * S + w], q2T[:, k, t * P:(t + 1) * P], ctxT[:, u, k, c * S:c * S + w],
                                  start=(k == 0), stop=(k == KD - 1))
                last.then_inc(scores_ready, 1)

            with pe.Fori(0, B // 2) as bb:
                for u in range(2):
                    b = bb * 2 + u
                    pe.wait_ge(dve_copied, b * BY_DVE)
                    pe.wait_ge(act_copied, b * BY_ACT)
                    for m in range(KD):
                        for k in range(KD):
                            last = mm(ring[m][:], W12T[:, k, m * P:(m + 1) * P], XT[:, k, ds(b * S, S)], start=(k == 0), stop=(k == KD - 1))
                        last.then_inc(ring_ready, 1)
                    pe.wait_ge(act_copied, b * BY_ACT + 2)
                    for m in range(KD):
                        for k in range(KD):
                            last = mm(ring[m][:], W12[:, k, m * P:(m + 1) * P], qpT[:, k, :], start=(k == 0), stop=(k == KD - 1))
                        last.then_inc(ring_ready, 1)
                    pe.wait_ge(act_copied, b * BY_ACT + 4)
                    pe.wait_ge(ctx_loaded[u], bb * 48 + 48)
                    scores(b, u, 0)
                    for t in range(TPB):
                        n = b * TPB + t
                        if t + 1 < TPB:
                            scores(b, u, t + 1)
                        pe.wait_ge(probs_ready, n + 1)
                        for g in range(4):
                            if g % 2 == 0:
                                pe.wait_ge(dve_copied, b * BY_DVE + 2 * t + g // 2)
                            else:
                                pe.wait_ge(act_copied, b * BY_ACT + 4 + 2 * t + g // 2)
                            for q, kt in enumerate(groups[g]):
                                r = key_rows(kt)
                                last = nc.tensor.transpose(ring[g % 2][0:r, q * P:(q + 1) * P], probs[:, t % 2, kt * P:kt * P + r], ident[:])
                            last.then_inc(ring_ready, 1)
                        pe.wait_ge(dve_copied, b * BY_DVE + 2 * t + 2)
                        pe.wait_ge(act_copied, b * BY_ACT + 4 + 2 * t + 2)
                        pe.wait_ge(sum_ready, n)
                        for kt in range(NK2):
                            r = key_rows(kt)
                            last = mm(av_ps[:], PT[0:r, t % 2, kt, :], ctxN[0:r, u, kt, :], start=(kt == 0), stop=(kt == NK2 - 1))
                        last.then_inc(av_ready, 1)
            for c in range(B):
                turn_group(nc, pe, X, ident[:], ring, c, norm.normed, copied, turned)

        def copy_group(eng_copy, t, g):
            k0, k1 = groups[g][0], groups[g][-1] + 1
            r = key_rows(k1 - 1) if k1 - k0 == 1 else P
            return eng_copy(PT[0:r, t % 2, k0:k1, :], ring[g % 2][0:r, 0:(k1 - k0) * P].rearrange("p (k c) -> p k c", c=P))

        @block.scalar
        def _(act):
            act.dma_start(bias[:], dram["fside"].rearrange("(t p) s -> p t s", p=P)).then_inc(bias_loaded, 16)
            act.wait_ge(loaded, 64)
            for n in range(6):
                kind, h = n // 2, n % 2
                act.wait_ge(w_product, n + 1)
                if kind == 2:
                    o = nc.scalar.activation(b12[:, h:h + 1], ring[h][:, 0:1], ACT.Identity, bias=b2[:, h:h + 1])
                else:
                    o = nc.scalar.activation((W12T if kind == 0 else W12)[:, h, :], ring[h][:, 0:D], ACT.Copy)
                o.then_inc(w_copied, 1)
            act.wait_ge(w_copied, 6)

            def exponentials(b, t):
                n = b * TPB + t
                act.wait_ge(max_ready, n + 1)
                nc.scalar.activation(probs[:, t % 2, :], probs[:, t % 2, :], ACT.Exp, bias=neg_top[:, t % 2:t % 2 + 1],
                                     accum_out=total[:, t % 2:t % 2 + 1]).then_inc(probs_ready, 1)

            with act.Fori(0, B // 2) as bb:
                for u in range(2):
                    b = bb * 2 + u
                    for m in range(KD):
                        act.wait_ge(ring_ready, b * RING + m + 1)
                        nc.scalar.activation(qpT[:, m, :], ring[m][:], ACT.Identity, bias=b12[:, m:m + 1]).then_inc(act_copied, 1)
                    for m in range(KD):
                        act.wait_ge(ring_ready, b * RING + m + 3)
                        nc.scalar.activation(q2T[:, m, :], ring[m][:], ACT.Copy, scale=float(D) ** -0.5).then_inc(act_copied, 1)
                    exponentials(b, 0)
                    for t in range(TPB):
                        for g in (1, 3):
                            act.wait_ge(ring_ready, b * RING + 4 + 4 * t + g + 1)
                            copy_group(nc.scalar.copy, t, g).then_inc(act_copied, 1)
                        if t + 1 < TPB:
                            exponentials(b, t + 1)
            for c in range(B):
                copy_turned(nc, act, XT, ring, c, turned, copied)

        @block.gpsimd
        def _(pool):
            norm.setup(pool)
            for c in range(B):
                norm.inverse_deviation(pool, c)

        @block.vector
        def _(dve):
            dve.wait_ge(bias_loaded, 16)

            def maximum(b, t):
                n = b * TPB + t
                dve.wait_ge(scores_ready, n + 1)
                nc.vector.memset(fence[:], 0.0)
                nc.vector.tensor_tensor_reduce(out=probs[:, t % 2, :], in0=scores_ps[:, 0:S2], in1=bias[:, t, :], scale=1.0,
                                               scalar=-3.0e38, op0=ALU.add, op1=ALU.max,
                                               accum_out=top[:, t % 2:t % 2 + 1]).then_inc(scores_read, 1)
                dve.wait_ge(scores_read, n + 1)
                nc.vector.tensor_scalar(neg_top[:, t % 2:t % 2 + 1], top[:, t % 2:t % 2 + 1], -1.0, None, ALU.mult).then_inc(max_ready, 1)

            with dve.Fori(0, B // 2) as bb:
                for u in range(2):
                    b = bb * 2 + u
                    maximum(b, 0)
                    for t in range(TPB):
                        n = b * TPB + t
                        for g in (0, 2):
                            dve.wait_ge(ring_ready, b * RING + 4 + 4 * t + g + 1)
                            copy_group(nc.vector.tensor_copy, t, g).then_inc(dve_copied, 1)
                        if t + 1 < TPB:
                            maximum(b, t + 1)
                        dve.wait_ge(probs_ready, n + 1)
                        nc.vector.reciprocal(inv_total[:, t % 2:t % 2 + 1], total[:, t % 2:t % 2 + 1]).then_inc(inv_ready, 1)
                        dve.wait_ge(inv_ready, n + 1)
                        dve.wait_ge(av_ready, n + 1)
                        x = X[:, ds(n, 1), :].rearrange("p a d -> p (a d)")
                        nc.vector.scalar_tensor_tensor(x, av_ps[:], inv_total[:, t % 2:t % 2 + 1], x, ALU.mult, ALU.add).then_inc(sum_ready, 1)
            norm.finish(dve, sum_ready)


QUARTERS = B
W_SCALE = 16.0


def phase_moe(nc, ctx, dram, X, XT, ident):
    sb = lambda n, s, dt=F32: ctx.enter_context(nc.sbuf_tensor(f"C_{n}", s, dt))
    ps = lambda n, s: ctx.enter_context(nc.psum_tensor(f"C_{n}", s, F32))
    sem = lambda n: ctx.enter_context(nc.semaphore(f"C_{n}"))
    Wr, br, lanes = sb("Wr", [P, KD, E]), sb("br", [P, E]), sb("lanes", [P, E])
    logits, best = sb("logits", [P, NT, E]), sb("best", [P, NT])
    top8, index8, index_f = sb("top8", [P, NT, 8]), sb("index8", [P, NT, 8], mybir.dt.uint32), sb("index_f", [P, NT, 2])
    pair_sum, first, second = sb("pair_sum", [P, NT]), sb("first", [P, NT, E]), sb("second", [P, NT, E])
    comb = sb("comb", [P, NT, E])
    bi, bg, half_bg = sb("bi", [P, E, NF]), sb("bg", [P, E, NF]), sb("half_bg", [P, E, NF])
    names = ("Wi", "Wg", "Wo")
    QW = KD * F // QUARTERS
    W = {n: sb(n, [P, KD * F]) for n in names}
    high, low = ({n: sb(f"{n}_{part}", [P, 2, KD * F], F16) for n in names} for part in ("high", "low"))
    X_high, X_low = sb("X_high", [P, KD, T], F16), sb("X_low", [P, KD, T], F16)
    tail = sb("tail", [P, 2, 3, D])
    gelu, gate = sb("gelu", [P, 4, S]), sb("gate", [P, 4, S])
    h = sb("h", [P, 4, S])
    h_high, h_low = sb("h_high", [P, NF, S], F16), sb("h_low", [P, NF, S], F16)
    R = sb("R", [P, TPB, D])
    N = sb("N", [P, 2, D])
    OUT = sb("OUT", [P, NT, D])
    stats, mv, ve, rstd = sb("stats", [P, TPB, 6]), sb("mv", [P, TPB, 2]), sb("ve", [P, TPB]), sb("rstd", [P, TPB])
    neg_half, eps, fence = sb("neg_half", [P, 1]), sb("eps", [P, 1]), sb("fence", [P, 1])
    router_ps = ps("router", [P, NT * E])
    yi_ps, yg_ps, y2_ps = ([ps(f"{n}{i}", [P, w]) for i in range(2)] for n, w in (("yi", S), ("yg", S), ("y2", D)))

    norm = Norm(ctx, nc, "C_norm", OUT, LN_EPS)
    loaded = sem("loaded")
    w_loaded = sem("w_loaded")
    tail_loaded = [sem(f"tail_loaded{u}") for u in range(2)]
    w_high, w_low = sem("w_high"), sem("w_low")
    x_high, x_low = sem("x_high"), sem("x_low")
    h_ready, h_high_ready = sem("h_ready"), sem("h_high_ready")
    routed, r_step, exp_ready, comb_ready = sem("routed"), sem("r_step"), sem("exp_ready"), sem("comb_ready")
    bias_scaled, out_started = sem("bias_scaled"), sem("out_started")
    yi_ready, yg_ready, gelu_ready, gate_ready = sem("yi_ready"), sem("yg_ready"), sem("gelu_ready"), sem("gate_ready")
    act_ready = sem("act_ready")
    base_ready, y2_ready, r_ready = sem("base_ready"), sem("y2_ready"), sem("r_ready")
    stats_ready, mv_ready, ve_ready, rstd_ready = sem("stats_ready"), sem("mv_ready"), sem("ve_ready"), sem("rstd_ready")
    n_ready, g_ready, b_ready, mixed = sem("n_ready"), sem("g_ready"), sem("b_ready"), sem("mixed")
    half_ready = sem("half_ready")
    turned, copied = sem("turned"), sem("copied")
    turn_ps = yi_ps

    with nc.Block() as block:
        @block.sync
        def _(sp):
            for t, n in ((Wr, "L0_ffn_Wr"), (br, "L0_ffn_br"), (lanes, "lanes"), (bi, "L0_ffn_bi"), (bg, "L0_ffn_bg")):
                sp.dma_start(t[:], dram[n]).then_inc(loaded, 16)

            def load_weights(e):
                for n, k in (("Wi", KD), ("Wg", KD), ("Wo", NF)):
                    sp.dma_start(W[n][:].rearrange("p (k f) -> p k f", k=k),
                                 dram[f"L0_ffn_{n}"][ds(e, 1)].rearrange("e (k p) f -> p (e k) f", p=P)).then_inc(w_loaded, 16)

            def load_tail(e, u):
                sp.dma_start(tail[:, u], dram["expert_tail"][:, ds(e, 1)].rearrange("q e r d -> q (e r) d")).then_inc(tail_loaded[u], 16)

            load_weights(0)
            for u in range(2):
                load_tail(u, u)
            sp.wait_ge(w_high, QUARTERS * 3)
            sp.wait_ge(w_low, QUARTERS * 3)
            load_weights(1)
            with sp.Fori(0, E // 2 - 1) as ee:
                for u in range(2):
                    e = ee * 2 + u
                    sp.wait_ge(w_high, (e + 2) * QUARTERS * 3)
                    sp.wait_ge(w_low, (e + 2) * QUARTERS * 3)
                    load_weights(e + 2)
                    sp.wait_ge(mixed, (e + 1) * NT)
                    load_tail(e + 2, u)

        @block.tensor
        def _(pe):
            mm = nc.tensor.matmul
            pe.wait_ge(loaded, 80)
            for t in range(NT):
                for k in range(KD):
                    last = mm(router_ps[:, t * E:(t + 1) * E], XT[:, k, t * P:(t + 1) * P], Wr[:, k, :], start=(k == 0), stop=(k == KD - 1))
            last.then_inc(routed, 1)
            pe.wait_ge(x_low, KD)
            with pe.Fori(0, E // 2) as ee:
                for u in range(2):
                    e = ee * 2 + u
                    with pe.Fori(0, B) as c:
                        pe.wait_ge(w_low, (e + 1) * QUARTERS * 3)
                        it = e * B + c
                        for j in range(NF):
                            n = it * NF + j
                            if j >= 2:
                                pe.wait_ge(gate_ready, n - 1)
                            for name, banks, ready in (("Wi", yi_ps, yi_ready), ("Wg", yg_ps, yg_ready)):
                                parts = [(k, w, x) for k in range(KD) for w, x in ((high, X_high), (high, X_low), (low, X_high))]
                                for q, (k, w, x) in enumerate(parts):
                                    last = mm(banks[j % 2][:], w[name][:, u, k * F + j * P:k * F + (j + 1) * P], x[:, k, ds(c * S, S)],
                                              start=(q == 0), stop=(q == len(parts) - 1))
                                last.then_inc(ready, 1)

                        def second(t, tiles):
                            for j in tiles:
                                pe.wait_ge(act_ready, it * NF + j + 1)
                                for q, (hp, w) in enumerate(((h_high, high), (h_high, low), (h_low, high))):
                                    last = mm(y2_ps[t % 2][:], hp[:, j, t * P:(t + 1) * P], w["Wo"][:, u, j * D:(j + 1) * D],
                                              start=(j == 0 and q == 0), stop=(j == NF - 1 and q == 2))
                            return last

                        for t0 in range(0, TPB, 2):
                            pe.wait_ge(r_ready, it * TPB + t0)
                            for t in (t0, t0 + 1):
                                second(t, range(NF - 1))
                            for t in (t0, t0 + 1):
                                second(t, range(NF - 1, NF)).then_inc(y2_ready, 1)
            for c in range(B):
                turn_group(nc, pe, X, ident[:], turn_ps, c, norm.normed, copied, turned)

        @block.scalar
        def _(act):
            for k in range(KD):
                nc.scalar.activation(X_high[:, k, :], XT[:, k, :], ACT.Copy).then_inc(x_high, 1)

            def split_high(e, u, c):
                act.wait_ge(w_loaded, (e + 1) * 48)
                for n in names:
                    nc.scalar.activation(high[n][:, u, ds(c * QW, QW)], W[n][:, ds(c * QW, QW)], ACT.Copy, scale=W_SCALE).then_inc(w_high, 1)

            with act.Fori(0, QUARTERS) as c:
                split_high(0, 0, c)
            act.wait_ge(r_step, 2)
            nc.scalar.activation(logits[:], logits[:], ACT.Exp).then_inc(exp_ready, 1)
            act.wait_ge(bias_scaled, 1)

            def expert(e, u, ahead):
                with act.Fori(0, B) as c:
                    def round_high(j):
                        n = (e * B + c) * NF + j
                        act.wait_ge(h_ready, n + 1)
                        nc.scalar.activation(h_high[:, j, :], h[:, j % 4, :], ACT.Copy).then_inc(h_high_ready, 1)

                    for j in range(NF):
                        n = (e * B + c) * NF + j
                        act.wait_ge(yi_ready, n + 1)
                        if j >= 4:
                            act.wait_ge(h_ready, n - 3)
                        b = bi[:, ds(e, 1), j:j + 1].rearrange("p a b -> p (a b)")
                        nc.scalar.activation(gelu[:, j % 4, :], yi_ps[j % 2][:], ACT.Gelu, bias=b, scale=1.0 / W_SCALE).then_inc(gelu_ready, 1)
                        act.wait_ge(yg_ready, n + 1)
                        b = half_bg[:, ds(e, 1), j:j + 1].rearrange("p a b -> p (a b)")
                        nc.scalar.activation(gate[:, j % 4, :], yg_ps[j % 2][:], ACT.Tanh, bias=b, scale=0.5 / W_SCALE).then_inc(gate_ready, 1)
                        if j >= 2:
                            round_high(j - 2)
                    round_high(NF - 2)
                    round_high(NF - 1)
                    if ahead:
                        act.wait_ge(y2_ready, e * NT)
                        split_high(e + 1, 1 - u, c)

            with act.Fori(0, E // 2 - 1) as ee:
                for u in range(2):
                    expert(ee * 2 + u, u, True)
            for u in range(2):
                expert(E - 2 + u, u, u == 0)
            for c in range(B):
                copy_turned(nc, act, XT, turn_ps, c, turned, copied)

        @block.gpsimd
        def _(pool):
            norm.setup(pool)
            nc.gpsimd.memset(neg_half[:], -0.5).then_inc(half_ready, 1)
            nc.gpsimd.memset(eps[:], 1e-12).then_inc(half_ready, 1)
            pool.wait_ge(half_ready, 2)
            for c in range(B):
                nc.gpsimd.tensor_copy(OUT[:, c * TPB:(c + 1) * TPB, :], X[:, c * TPB:(c + 1) * TPB, :]).then_inc(out_started, 1)
            with pool.Fori(0, E // 2) as ee:
                for u in range(2):
                    with pool.Fori(0, B) as c:
                        pool.wait_ge(tail_loaded[u], ee * 16 + 16)
                        it = (ee * 2 + u) * B + c
                        pool.wait_ge(n_ready, it * TPB)
                        for t in range(TPB):
                            nc.gpsimd.tensor_tensor(R[:, t, :], X[:, ds(c * TPB + t, 1), :].rearrange("p a d -> p (a d)"),
                                                    tail[:, u, 0, :], ALU.add).then_inc(base_ready, 1)
                        for t in range(TPB):
                            n = it * TPB + t
                            pool.wait_ge(mv_ready, n + 1)
                            nc.gpsimd.tensor_tensor(ve[:, t:t + 1], mv[:, t, 1:2], eps[:], ALU.add).then_inc(ve_ready, 1)
                            pool.wait_ge(ve_ready, n + 1)
                            nc.gpsimd.tensor_tensor(rstd[:, t:t + 1], ve[:, t:t + 1], neg_half[:], ALU.pow).then_inc(rstd_ready, 1)
            for c in range(B):
                norm.inverse_deviation(pool, c)

        @block.vector
        def _(dve):
            v = nc.vector
            dve.wait_ge(loaded, 80)
            v.tensor_scalar(half_bg[:], bg[:], 0.5, None, ALU.mult).then_inc(bias_scaled, 1)
            for k in range(KD):
                dve.wait_ge(x_high, k + 1)
                v.tensor_tensor(X_low[:, k, :], XT[:, k, :], X_high[:, k, :], ALU.subtract).then_inc(x_low, 1)

            def split_low(e, u, c):
                dve.wait_ge(w_high, (e * QUARTERS + c) * 3 + 3)
                for n in names:
                    v.scalar_tensor_tensor(low[n][:, u, ds(c * QW, QW)], W[n][:, ds(c * QW, QW)], W_SCALE, high[n][:, u, ds(c * QW, QW)],
                                           ALU.mult, ALU.subtract).then_inc(w_low, 1)

            with dve.Fori(0, QUARTERS) as c:
                split_low(0, 0, c)
            dve.wait_ge(routed, 1)
            v.tensor_tensor(logits[:], router_ps[:].rearrange("p (t e) -> p t e", e=E),
                            br[:].rearrange("p (a e) -> p a e", a=1).broadcast_to([P, NT, E]), ALU.add).then_inc(r_step, 1)
            dve.wait_ge(r_step, 1)
            v.tensor_reduce(best[:], logits[:], AX_X, ALU.max).then_inc(comb_ready, 1)
            dve.wait_ge(comb_ready, 1)
            v.tensor_tensor(logits[:], logits[:], best[:].rearrange("p (t a) -> p t a", a=1).broadcast_to([P, NT, E]), ALU.subtract).then_inc(r_step, 1)
            dve.wait_ge(exp_ready, 1)
            for t in range(NT):
                v.max(top8[:, t, :], logits[:, t, :]).then_inc(comb_ready, 1)
            dve.wait_ge(comb_ready, 1 + NT)
            for t in range(NT):
                v.max_index(index8[:, t, :], top8[:, t, :], logits[:, t, :]).then_inc(comb_ready, 1)
            v.tensor_tensor(pair_sum[:], top8[:, :, 0], top8[:, :, 1], ALU.add).then_inc(comb_ready, 1)
            dve.wait_ge(comb_ready, 2 + 2 * NT)
            v.tensor_copy(index_f[:], index8[:, :, 0:2]).then_inc(comb_ready, 1)
            v.reciprocal(pair_sum[:], pair_sum[:]).then_inc(comb_ready, 1)
            dve.wait_ge(comb_ready, 4 + 2 * NT)
            for t in range(NT):
                for q, dst in ((0, first), (1, second)):
                    v.tensor_scalar(dst[:, t, :], lanes[:], index_f[:, t, q:q + 1], top8[:, t, q:q + 1], ALU.is_equal, ALU.mult).then_inc(comb_ready, 1)
            dve.wait_ge(comb_ready, 4 + 4 * NT)
            v.tensor_tensor(first[:], first[:], second[:], ALU.add).then_inc(comb_ready, 1)
            dve.wait_ge(comb_ready, 5 + 4 * NT)
            v.tensor_tensor(comb[:], first[:], pair_sum[:].rearrange("p (t a) -> p t a", a=1).broadcast_to([P, NT, E]), ALU.mult).then_inc(comb_ready, 1)
            dve.wait_ge(comb_ready, 6 + 4 * NT)
            dve.wait_ge(out_started, B)

            def expert(e, u, ahead):
                with dve.Fori(0, B) as c:
                    it = e * B + c

                    def round_low(j):
                        n = it * NF + j
                        dve.wait_ge(h_high_ready, n + 1)
                        v.tensor_tensor(h_low[:, j, :], h[:, j % 4, :], h_high[:, j, :], ALU.subtract).then_inc(act_ready, 1)

                    for j in range(NF):
                        n = it * NF + j
                        dve.wait_ge(gelu_ready, n + 1)
                        dve.wait_ge(gate_ready, n + 1)
                        dve.wait_ge(act_ready, n - 3 if j >= 4 else it * NF)
                        v.scalar_tensor_tensor(h[:, j % 4, :], gate[:, j % 4, :], 1.0, gelu[:, j % 4, :], ALU.add, ALU.mult).then_inc(h_ready, 1)
                        if j >= 1:
                            round_low(j - 1)
                    round_low(NF - 1)

                    def finish(t):
                        n = it * TPB + t
                        dve.wait_ge(rstd_ready, n + 1)
                        v.tensor_scalar(N[:, t % 2, :], R[:, t, :], mv[:, t, 0:1], rstd[:, t:t + 1], ALU.subtract, ALU.mult).then_inc(n_ready, 1)
                        dve.wait_ge(n_ready, n + 1)
                        v.tensor_tensor(N[:, t % 2, :], N[:, t % 2, :], tail[:, u, 1, :], ALU.mult).then_inc(g_ready, 1)
                        dve.wait_ge(g_ready, n + 1)
                        v.tensor_tensor(N[:, t % 2, :], N[:, t % 2, :], tail[:, u, 2, :], ALU.add).then_inc(b_ready, 1)
                        dve.wait_ge(b_ready, n + 1)
                        o = OUT[:, ds(c * TPB + t, 1), :].rearrange("p a d -> p (a d)")
                        w = comb[:, ds(c * TPB + t, 1), ds(e, 1)].rearrange("p a b -> p (a b)")
                        v.scalar_tensor_tensor(o, N[:, t % 2, :], w, o, ALU.mult, ALU.add).then_inc(mixed, 1)

                    if ahead:
                        split_low(e + 1, 1 - u, c)
                    for t0 in range(0, TPB, 2):
                        pair = (t0, t0 + 1)
                        for t in pair:
                            n = it * TPB + t
                            dve.wait_ge(base_ready, n + 1)
                            dve.wait_ge(y2_ready, n + 1)
                            v.scalar_tensor_tensor(R[:, t, :], y2_ps[t % 2][:], 0.5 / W_SCALE, R[:, t, :], ALU.mult, ALU.add).then_inc(r_ready, 1)
                        for t in pair:
                            n = it * TPB + t
                            dve.wait_ge(r_ready, n + 1)
                            v.bn_stats(stats[:, t, :], R[:, t, :]).then_inc(stats_ready, 1)
                            dve.wait_ge(stats_ready, n + 1)
                            v.memset(fence[:], 0.0)
                            v.bn_aggr(mv[:, t, :], stats[:, t, :]).then_inc(mv_ready, 1)
                        for t in pair:
                            finish(t)

            with dve.Fori(0, E // 2 - 1) as ee:
                for u in range(2):
                    expert(ee * 2 + u, u, True)
            for u in range(2):
                expert(E - 2 + u, u, u == 0)
            dve.wait_ge(mixed, E * NT)
            norm.finish(dve, mixed, (E - 1) * NT, out=X)


PARTS = 3
KEY_RUNS = ((0, 3), (0, 2), (0, 1))
QUERY_RUNS = ((0, 3), (1, 3), (2, 3))
STACK = 6 * DH
NEG = 2.0 ** 100
UNITS = B * H
VW = DH + 1
STRIP = 32
STRIPS = P // STRIP
PROBS = 8
SPLIT_SLOTS = 4


class Heads:

    def __init__(self, ctx, nc, name, n_keys, extra, extra_rows, causal, qd, kd, V, ATT, ident16, tri, strip_sum, slots, lag, order,
                 copy_after, score_banks, max_banks):
        self.nc, self.n_keys, self.causal = nc, n_keys, causal
        self.qd, self.kd, self.V, self.ATT, self.tri = qd, kd, V, ATT, tri
        self.extra_rows = extra_rows
        self.slots, self.lag, self.copy_after = slots, lag, copy_after
        self.ident_bf, self.ident_half = ident16
        self.strip_sum_dram = strip_sum
        self.R = STACK + extra
        self.loads = len(KEY_RUNS) + len(QUERY_RUNS) + (0 if causal else 1)
        self.tiles = [(kt, min(P, n_keys - kt * P)) for kt in range((n_keys + P - 1) // P)]
        self.NG = len(self.tiles)
        self.quads = [self.tiles[g:g + STRIPS] for g in range(0, self.NG, STRIPS)]
        n_chunks = (n_keys + S - 1) // S
        w = -(-n_keys // n_chunks)
        self.chunks = [(qt, c, min(w, n_keys - c)) for qt in range(TPB) for c in range(0, n_keys, w)]
        self.per_q = n_chunks
        counts = {"scores": 0, "max": 0, "values": 0}
        self.order = []
        for kind in order.split():
            self.order.append((kind, counts.get(kind, 0)))
            if kind in counts:
                counts[kind] += 1
        assert counts == {"scores": self.NG, "max": len(self.chunks), "values": len(self.quads) - 1}
        assert slots % 2 == 0
        sb = lambda n, s, dt=F32: ctx.enter_context(nc.sbuf_tensor(f"{name}_{n}", s, dt))
        ps = lambda n, s, dt=F32: ctx.enter_context(nc.psum_tensor(f"{name}_{n}", s, dt))
        sem = lambda n: ctx.enter_context(nc.semaphore(f"{name}_{n}"))
        self.KS = sb("KS", [self.R + 2, slots, n_keys], BF16)
        self.QS = sb("QS", [self.R + 2, slots, S], BF16)
        self.VS = sb("VS", [P, 2, len(self.tiles), STRIP])
        self.strip_sum = sb("strip_sum", [P, VW])
        self.probs = sb("probs", [P, PROBS, S])
        self.maxima = sb("maxima", [P, TPB, n_chunks])
        self.neg = sb("neg", [P, TPB])
        self.neg_parts = sb("neg_parts", [P, 2, TPB], BF16)
        self.neg_rows = sb("neg_rows", [2 * TPB, 2, P], BF16)
        self.av = sb("av", [P, S])
        self.inv = sb("inv", [P, TPB])
        self.score_ps = [ps(f"score{i}", [P, S]) for i in range(score_banks)]
        self.max_ps = [ps(f"max{i}", [P, S]) for i in range(max_banks)]
        self.av_ps = ps("av_ps", [P, S])
        small_ps = ps("small", [P, S])
        self.token_ps = small_ps[:, 0:TPB * VW]
        self.row_ps = small_ps[0:2 * TPB, P:P + P // 2].bitcast(BF16)
        self.loaded = [sem(f"loaded{i}") for i in range(slots)]
        self.rows_loaded = [sem(f"rows_loaded{i}") for i in range(slots)]
        self.sum_loaded, self.extra_ready = sem("sum_loaded"), sem("extra_ready")
        self.chunk_ready, self.chunk_read = sem("chunk_ready"), sem("chunk_read")
        self.neg_f, self.neg_a, self.neg_ready = sem("neg_f"), sem("neg_a"), sem("neg_ready")
        self.rows_turned, self.rows_copied = sem("rows_turned"), sem("rows_copied")
        self.scores_ready, self.probs_ready, self.probs_used = sem("scores_ready"), sem("probs_ready"), sem("probs_used")
        self.padded, self.values_ready = sem("padded"), sem("values_ready")
        self.av_copied, self.token_ready = sem("av_copied"), sem("token_ready")
        self.inv_ready, self.unit_read = sem("inv_ready"), sem("unit_read")

    def walk(self, eng, step, unroll=None):
        n = unroll or self.slots
        for u in range(n):
            step(u, u, 0)
        with eng.Fori(1, UNITS // n - 1) as i:
            for u in range(n):
                step(i * n + u, u, i)
        for u in range(n):
            step(UNITS - n + u, u, UNITS // n - 1)

    def ahead(self, s, n):
        return not isinstance(s, int) or s + n < UNITS

    def at(self, s, n):
        return not isinstance(s, int) or s >= n

    def place(self, u, k, per_unit, places):
        total = self.slots * per_unit
        even = total % places == 0
        at = lambda n: (n % total if even else n % per_unit) % places
        n = u * per_unit + k + total
        back = next(d for d in range(1, total) if at(n - d) == at(n))
        return at(n), back

    def load(self, sp, unit, slot):
        for dst, src, runs in ((self.KS, self.kd, KEY_RUNS), (self.QS, self.qd, QUERY_RUNS)):
            start, per = 0, src.shape[0] // PARTS
            for p0, p1 in runs:
                rows = (p1 - p0) * DH
                sp.dma_start(dst[start:start + rows, slot, :], src[p0 * per:p1 * per, ds(unit, 1)].rearrange("g u d s -> g (u d) s")).then_inc(self.loaded[slot], 16)
                start += rows
        if not self.causal:
            sp.dma_start(self.KS[STACK:STACK + 1, slot, :], self.extra_rows[ds(unit, 1)]).then_inc(self.loaded[slot], 16)

    def load_rows(self, sp, unit, slot):
        sp.wait_ge(self.rows_copied, unit + 1)
        sp.dma_start(self.QS[self.R:self.R + 2, slot, :].rearrange("a (t q) -> a t q", q=P),
                     self.neg_rows[:, slot % 2, :]).then_inc(self.rows_loaded[slot], 16)

    def sync(self, sp):
        sp.dma_start(self.strip_sum[:], self.strip_sum_dram).then_inc(self.sum_loaded, 16)
        if self.causal:
            for dst, src, rows in ((self.QS, self.extra_rows[0], self.R), (self.KS, self.extra_rows[1], self.R + 2)):
                sp.dma_start(dst[STACK:rows], src.rearrange("u r s -> r u s")).then_inc(self.extra_ready, 16)
        else:
            sp.wait_ge(self.extra_ready, 2)
        for u in range(self.slots):
            self.load(sp, u, u)
        for u in range(self.lag - 1):
            self.load_rows(sp, u, u)

        def step(s, u, i):
            if self.ahead(s, self.lag - 1):
                self.load_rows(sp, s + self.lag - 1, (u + self.lag - 1) % self.slots)
            if self.ahead(s, self.slots):
                sp.wait_ge(self.scores_ready, (s + 1) * self.NG)
                self.load(sp, s + self.slots, u)

        self.walk(sp, step)

    def max_chunk(self, pe, unit, slot, m):
        nc = self.nc
        qt, c, w = self.chunks[m]
        n = unit * len(self.chunks) + m
        bank, back = self.place(slot, m, len(self.chunks), len(self.max_ps))
        if not isinstance(unit, int) or n >= back:
            pe.wait_ge(self.chunk_read, n - back + 1)
        out = self.max_ps[bank]
        last = nc.tensor.matmul(out[:, 0:w], self.QS[0:self.R, slot, qt * P:(qt + 1) * P], self.KS[0:self.R, slot, c:c + w],
                                start=True, stop=True)
        if self.causal:
            last = nc.tensor.matmul(out[:, qt * P:(qt + 1) * P], self.ident_half[:], self.tri[:, 0, :], start=False, stop=True,
                                    skip_group_check=True)
        last.then_inc(self.chunk_ready, 1)

    def turn_rows(self, pe, unit):
        pe.wait_ge(self.neg_ready, unit + 1)
        if self.at(unit, 1):
            pe.wait_ge(self.rows_copied, unit)
        if self.at(unit, self.lag + 1):
            pe.wait_ge(self.unit_read, unit - self.lag)
        self.nc.tensor.transpose(self.row_ps, self.neg_parts[:].rearrange("p a t -> p (a t)"), self.ident_bf[:]).then_inc(self.rows_turned, 1)

    def scores(self, pe, s, u, g):
        nc = self.nc
        n = s * self.NG + g
        bank, back = self.place(u, g, self.NG, len(self.score_ps))
        if not isinstance(s, int) or n >= back:
            pe.wait_ge(self.probs_ready, n - back + 1)
        out = self.score_ps[bank]
        kt, r = self.tiles[g]
        last = nc.tensor.matmul(out[0:r, :], self.KS[:, u, kt * P:kt * P + r], self.QS[:, u, :], start=True, stop=True)
        if self.causal:
            last = nc.tensor.matmul(out[:, kt * P:(kt + 1) * P], self.ident_half[:], self.tri[:, 1, :], start=False, stop=True,
                                    skip_group_check=True)
        last.then_inc(self.scores_ready, 1)

    def values(self, pe, s, u, quad):
        nc = self.nc
        tiles = self.quads[quad]
        if quad == 0:
            pe.wait_ge(self.values_ready, s + 1)
            if self.at(s, 1):
                pe.wait_ge(self.av_copied, s)
        pe.wait_ge(self.probs_ready, s * self.NG + tiles[-1][0] + 1)
        final = quad == len(self.quads) - 1
        if len(tiles) == STRIPS:
            parts = [(j, t, 0, S) for j, t in enumerate(tiles)]
        else:
            parts = [(j, t, j * P, P) for t in tiles for j in range(STRIPS)]
        for j, (kt, r), q0, w in parts:
            buf = self.place(u, kt, self.NG, PROBS)[0]
            last = nc.tensor.matmul(self.av_ps[j * STRIP:(j + 1) * STRIP, q0:q0 + w], self.VS[0:r, u % 2, kt, :],
                                    self.probs[0:r, buf, q0:q0 + w], start=(quad == 0), stop=final,
                                    tile_position=(0, j * STRIP), skip_group_check=True)
        last.then_inc(self.probs_used, len(tiles))

    def token_major(self, pe, unit):
        nc = self.nc
        pe.wait_ge(self.av_copied, unit + 1)
        if self.at(unit, 1):
            pe.wait_ge(self.unit_read, unit)
        turned = unit + 1 + self.lag
        pe.wait_ge(self.rows_copied, min(turned, UNITS) if isinstance(unit, int) else turned)
        for qt in range(TPB):
            last = nc.tensor.matmul(self.token_ps[:, qt * VW:(qt + 1) * VW], self.av[:, qt * P:(qt + 1) * P], self.strip_sum[:],
                                    start=True, stop=True)
        last.then_inc(self.token_ready, 1)

    def tensor(self, pe):
        pe.wait_ge(self.extra_ready, 32 if self.causal else 2)
        for unit in range(self.lag):
            pe.wait_ge(self.loaded[unit], 16 * self.loads)
            for m in range(len(self.chunks)):
                self.max_chunk(pe, unit, unit, m)
            if unit >= 1:
                self.turn_rows(pe, unit - 1)
        pe.wait_ge(self.sum_loaded, 16)

        def step(s, u, i):
            pe.wait_ge(self.rows_loaded[u], i * 16 + 16)
            ahead = u + self.lag
            if self.ahead(s, self.lag):
                pe.wait_ge(self.loaded[ahead % self.slots], (i + ahead // self.slots + 1) * 16 * self.loads)
            for kind, k in self.order:
                if kind == "scores":
                    self.scores(pe, s, u, k)
                elif kind == "max" and self.ahead(s, self.lag):
                    self.max_chunk(pe, s + self.lag, ahead % self.slots, k)
                elif kind == "turn" and self.ahead(s, self.lag - 1):
                    self.turn_rows(pe, s + self.lag - 1)
                elif kind == "values":
                    self.values(pe, s, u, k)
                elif kind == "last" and self.at(s, 1):
                    self.values(pe, s - 1, (u - 1) % self.slots, len(self.quads) - 1)
                elif kind == "token" and self.at(s, 1):
                    self.token_major(pe, s - 1)

        self.walk(pe, step)
        self.values(pe, UNITS - 1, self.slots - 1, len(self.quads) - 1)
        self.token_major(pe, UNITS - 1)

    def copy_sums(self, act, unit):
        act.wait_ge(self.probs_used, (unit + 1) * self.NG)
        if self.at(unit, 1):
            act.wait_ge(self.token_ready, unit)
        self.nc.scalar.activation(self.av[:], self.av_ps[:], ACT.Copy).then_inc(self.av_copied, 1)

    def scalar(self, act):
        nc, NG = self.nc, self.NG

        def step(s, u, i):
            for g, (_, r) in enumerate(self.tiles):
                n = s * NG + g
                bank, _ = self.place(u, g, NG, len(self.score_ps))
                buf, back = self.place(u, g, NG, PROBS)
                act.wait_ge(self.scores_ready, n + 1)
                if not isinstance(s, int) or n >= back:
                    act.wait_ge(self.probs_used, n - back + 1)
                nc.scalar.activation(self.probs[0:r, buf, :], self.score_ps[bank][0:r, :], ACT.Exp).then_inc(self.probs_ready, 1)
                if g == self.copy_after and self.at(s, 1):
                    self.copy_sums(act, s - 1)

        self.walk(act, step)
        self.copy_sums(act, UNITS - 1)

    def pool(self, pool):
        nc = self.nc
        nc.gpsimd.memset(self.VS[:], 0.0).then_inc(self.padded, 1)
        pool.wait_ge(self.padded, 1)

        def step(s, u, i):
            if self.at(s, 2):
                pool.wait_ge(self.probs_used, (s - 1) * self.NG)
            nc.gpsimd.tensor_copy(self.VS[:, u % 2, :, 0:VW], self.V[:, :, ds(s * VW, VW)]).then_inc(self.values_ready, 1)

        self.walk(pool, step, 2)

    def maximum(self, dve, unit, slot, m):
        qt, c, w = self.chunks[m]
        dve.wait_ge(self.chunk_ready, unit * len(self.chunks) + m + 1)
        self.nc.vector.tensor_reduce(self.maxima[:, qt, m % self.per_q:m % self.per_q + 1], self.max_ps[self.place(slot, m, len(self.chunks), len(self.max_ps))[0]][:, 0:w], AX_X,
                                     ALU.max).then_inc(self.chunk_read, 1)

    def negate(self, dve, unit):
        v = self.nc.vector
        dve.wait_ge(self.chunk_read, (unit + 1) * len(self.chunks))
        v.tensor_reduce(self.neg[:], self.maxima[:], AX_X, ALU.max, negate=True).then_inc(self.neg_f, 1)
        dve.wait_ge(self.neg_f, unit + 1)
        if self.at(unit, 1):
            dve.wait_ge(self.rows_turned, unit)
        v.tensor_copy(self.neg_parts[:, 0, :], self.neg[:]).then_inc(self.neg_a, 1)
        dve.wait_ge(self.neg_a, unit + 1)
        v.tensor_tensor(self.neg_parts[:, 1, :], self.neg[:], self.neg_parts[:, 0, :], ALU.subtract).then_inc(self.neg_ready, 1)

    def copy_rows(self, dve, unit, slot, round_):
        if self.at(unit, 2):
            dve.wait_ge(self.rows_loaded[(slot - 2) % self.slots], round_ * 16 + 16)
        dve.wait_ge(self.rows_turned, unit + 1)
        self.nc.vector.tensor_copy(self.neg_rows[:, slot % 2, :], self.row_ps).then_inc(self.rows_copied, 1)

    def divide(self, dve, unit):
        v = self.nc.vector
        dve.wait_ge(self.token_ready, unit + 1)
        token = self.token_ps.rearrange("p (t v) -> p t v", v=VW)
        v.reciprocal(self.inv[:], token[:, :, DH]).then_inc(self.inv_ready, 1)
        dve.wait_ge(self.inv_ready, unit + 1)
        v.tensor_tensor(self.ATT[:, :, ds(unit * DH, DH)], token[:, :, 0:DH],
                        self.inv[:].rearrange("p (t a) -> p t a", a=1).broadcast_to([P, TPB, DH]), ALU.mult).then_inc(self.unit_read, 1)

    def vector(self, dve):
        if not self.causal:
            self.nc.vector.memset(self.KS[STACK:self.R + 2], 1.0).then_inc(self.extra_ready, 1)
            self.nc.vector.memset(self.QS[STACK:self.R], 1.0).then_inc(self.extra_ready, 1)
        for unit in range(self.lag):
            for m in range(len(self.chunks)):
                self.maximum(dve, unit, unit, m)
            if unit >= 1:
                self.copy_rows(dve, unit - 1, unit - 1, 0)
            self.negate(dve, unit)

        def step(s, u, i):
            for kind, k in self.order:
                if kind == "max" and self.ahead(s, self.lag):
                    self.maximum(dve, s + self.lag, (u + self.lag) % self.slots, k)
                elif kind == "turn" and self.ahead(s, self.lag - 1):
                    ahead = u + self.lag - 1
                    self.copy_rows(dve, s + self.lag - 1, ahead % self.slots, i + (ahead - 2) // self.slots)
                elif kind == "token" and self.at(s, 1):
                    self.divide(dve, s - 1)
            if self.ahead(s, self.lag):
                self.negate(dve, s + self.lag)

        self.walk(dve, step)
        self.divide(dve, UNITS - 1)


class Split:

    def __init__(self, ctx, nc, name):
        self.nc = nc
        sb = lambda n, s, dt: ctx.enter_context(nc.sbuf_tensor(f"{name}_{n}", s, dt))
        sems = lambda n: [ctx.enter_context(nc.semaphore(f"{name}_{n}{i}")) for i in range(SPLIT_SLOTS)]
        self.t = sb("t", [P, SPLIT_SLOTS, S], F32)
        self.parts = sb("parts", [P, SPLIT_SLOTS, PARTS, S], BF16)
        self.t_ready, self.a_ready, self.r_ready, self.b_ready, self.c_ready, self.stored = (
            sems(n) for n in ("t_ready", "a_ready", "r_ready", "b_ready", "c_ready", "stored"))

    def before_t(self, dve, slot, turn):
        dve.wait_ge(self.c_ready[slot], turn)

    def part(self, slot, k, query, w):
        return self.parts[:, slot, PARTS - 1 - k if query else k, 0:w]

    def scalar(self, act, items):
        nc = self.nc
        for slot, turn, query, w in items:
            act.wait_ge(self.stored[slot], turn * 16)
            act.wait_ge(self.t_ready[slot], turn + 1)
            nc.scalar.copy(self.part(slot, 0, query, w), self.t[:, slot, 0:w]).then_inc(self.a_ready[slot], 1)
        for slot, turn, query, w in items:
            act.wait_ge(self.r_ready[slot], turn + 1)
            nc.scalar.copy(self.part(slot, 1, query, w), self.t[:, slot, 0:w]).then_inc(self.b_ready[slot], 1)

    def pool(self, pool, items):
        nc = self.nc
        for slot, turn, query, w in items:
            t = self.t[:, slot, 0:w]
            pool.wait_ge(self.a_ready[slot], turn + 1)
            nc.gpsimd.tensor_tensor(t, t, self.part(slot, 0, query, w), ALU.subtract).then_inc(self.r_ready[slot], 1)
        for slot, turn, query, w in items:
            pool.wait_ge(self.b_ready[slot], turn + 1)
            nc.gpsimd.tensor_tensor(self.part(slot, 2, query, w), self.t[:, slot, 0:w], self.part(slot, 1, query, w),
                                    ALU.subtract).then_inc(self.c_ready[slot], 1)

    def sync(self, sp, slot, turn, w, dst, block, unit0, units, c0):
        sp.wait_ge(self.c_ready[slot], turn + 1)
        per = dst.shape[0] // PARTS
        sp.dma_start(dst[block::per, ds(unit0, units), :, c0:c0 + w].rearrange("g u d s -> (u d) g s"),
                     self.parts[:, slot, :, 0:w]).then_inc(self.stored[slot], 16)


def project_out(nc, ctx, name, X, XT, ATT, ident, WoT, bo):
    sem = lambda n: ctx.enter_context(nc.semaphore(f"{name}_{n}"))
    ps = [ctx.enter_context(nc.psum_tensor(f"{name}_out{i}", [P, S], F32)) for i in range(8)]
    turn_ps, out_ps, back_ps = ps[0:2], ps[2:6], ps[6:8]
    norm = Norm(ctx, nc, f"{name}_norm", X, LN_EPS)
    loaded, turned, copied = sem("loaded"), sem("turned"), sem("copied")
    out_ready, base_ready, sum_ready, turned2, copied2 = sem("out_ready"), sem("base_ready"), sem("sum_ready"), sem("turned2"), sem("copied2")
    WoT_sb = ctx.enter_context(nc.sbuf_tensor(f"{name}_WoT", [P, KD, D], F32))
    bo_sb = ctx.enter_context(nc.sbuf_tensor(f"{name}_bo", [P, D], F32)) if bo is not None else None
    need = 16 if bo is None else 32
    with nc.Block() as block:
        @block.sync
        def _(sp):
            sp.dma_start(WoT_sb[:], WoT.rearrange("(k p) d -> p k d", p=P)).then_inc(loaded, 16)
            if bo is not None:
                sp.dma_start(bo_sb[:], bo.partition_broadcast(P)).then_inc(loaded, 16)

        @block.tensor
        def _(pe):
            def attended(c):
                if c >= 1:
                    pe.wait_ge(copied, KD * c)
                for h in range(KD):
                    for t in range(TPB):
                        last = nc.tensor.transpose(turn_ps[h][:, t * P:(t + 1) * P], ATT[:, t, c * D + h * P:c * D + (h + 1) * P], ident[:])
                    last.then_inc(turned, 1)

            pe.wait_ge(loaded, need)
            for c in range(B + 1):
                if c < B:
                    attended(c)
                if c == 0:
                    continue
                pe.wait_ge(copied, KD * c)
                for t in range((c - 1) * TPB, c * TPB):
                    if t >= TPB:
                        pe.wait_ge(sum_ready, t - TPB + 1)
                    for k in range(KD):
                        last = nc.tensor.matmul(out_ps[t % TPB][:, 0:D], XT[:, k, t * P:(t + 1) * P], WoT_sb[:, k, :],
                                                start=(k == 0), stop=(k == KD - 1))
                    last.then_inc(out_ready, 1)
            for c in range(B):
                turn_group(nc, pe, X, ident[:], back_ps, c, norm.normed, copied2, turned2)

        @block.scalar
        def _(act):
            for c in range(B):
                copy_turned(nc, act, XT, turn_ps, c, turned, copied)
            act.wait_ge(out_ready, NT)
            for c in range(B):
                copy_turned(nc, act, XT, back_ps, c, turned2, copied2)

        @block.gpsimd
        def _(pool):
            norm.setup(pool)
            for c in range(B):
                norm.inverse_deviation(pool, c)

        @block.vector
        def _(dve):
            if bo is not None:
                dve.wait_ge(loaded, need)
                for t in range(NT):
                    nc.vector.tensor_tensor(X[:, t, :], X[:, t, :], bo_sb[:], ALU.add).then_inc(base_ready, 1)
                dve.wait_ge(base_ready, NT)
            for c in range(B):
                for t in range(c * TPB, (c + 1) * TPB):
                    dve.wait_ge(out_ready, t + 1)
                    nc.vector.tensor_tensor(X[:, t, :], out_ps[t % TPB][:, 0:D], X[:, t, :], ALU.add).then_inc(sum_ready, 1)
                norm.statistics(dve, c, sum_ready)
            for c in range(B):
                norm.normalize(dve, c)


def narrow_identities(nc, ctx, name):
    return [ctx.enter_context(nc.sbuf_tensor(f"{name}_ident{i}", [P, P], dt)) for i, dt in enumerate((BF16, F16))]


def run_heads(nc, heads):
    with nc.Block() as block:
        @block.sync
        def _(sp):
            heads.sync(sp)

        @block.tensor
        def _(pe):
            heads.tensor(pe)

        @block.scalar
        def _(act):
            heads.scalar(act)

        @block.gpsimd
        def _(pool):
            heads.pool(pool)

        @block.vector
        def _(dve):
            heads.vector(dve)


SELF_SLOTS = 8
CAUSAL = 2 * (TPB - 1)


def phase_self(nc, ctx, dram, X, XT, ident):
    qd, kd = (nc.dram_tensor(f"D_{n}", (PARTS, UNITS, DH, S), BF16, kind="Internal").ap() for n in ("qd", "kd"))
    q_extra = nc.dram_tensor("D_q_extra", (SELF_SLOTS, CAUSAL, S), BF16, kind="Internal").ap()
    k_extra = nc.dram_tensor("D_k_extra", (SELF_SLOTS, CAUSAL + 2, S), BF16, kind="Internal").ap()
    V = ctx.enter_context(nc.sbuf_tensor("D_V", [P, TPB, UNITS * VW], F32))
    ATT = ctx.enter_context(nc.sbuf_tensor("D_ATT", [P, TPB, UNITS * DH], F32))
    idents = narrow_identities(nc, ctx, "D")
    tri = ctx.enter_context(nc.sbuf_tensor("D_tri", [P, 2, P], F16))
    with ExitStack() as own:
        sb = lambda n, s, dt=F32: own.enter_context(nc.sbuf_tensor(f"D_{n}", s, dt))
        sem = lambda n: ctx.enter_context(nc.semaphore(f"D_{n}"))
        w = sb("w", [P, KD, 3 * D])
        tri_f = sb("tri_f", [P, 2, P])
        rows_f = sb("rows_f", [SELF_SLOTS, 2 * CAUSAL + 2, S])
        rows_b = sb("rows_b", [SELF_SLOTS, 2 * CAUSAL + 2, S], BF16)
        banks = [own.enter_context(nc.psum_tensor(f"D_bank{i}", [P, S], F32)) for i in range(SPLIT_SLOTS)]
        v_ps = [own.enter_context(nc.psum_tensor(f"D_v{i}", [P, D], F32)) for i in range(2)]
        split = Split(own, nc, "D_split")
        loaded, rows_ready, rows_stored, ones_ready = sem("loaded"), sem("rows_ready"), sem("rows_stored"), sem("ones_ready")
        cast_ready = sem("cast_ready")
        product = [sem(f"product{i}") for i in range(SPLIT_SLOTS)]
        v_product, v_copied = sem("v_product"), sem("v_copied")
        items = [(which, hf) for hf in range(KD) for which in range(2)]
        pairs = lambda b: [[(n, b, items[n][0] == 0, S) for n in (m, m + 1)] for m in (0, 2)]

        with nc.Block() as block:
            @block.sync
            def _(sp):
                sp.dma_start(w[:], dram["wqkvT"].rearrange("(k p) e -> p k e", p=P)).then_inc(loaded, 16)
                sp.dma_start(tri_f[:], dram["causal_tri"]).then_inc(loaded, 16)
                sp.dma_start(rows_f[:], dram["causal_rows"]).then_inc(loaded, 16)
                with sp.Fori(0, B) as b:
                    for n, (which, hf) in enumerate(items):
                        split.sync(sp, n, b, S, (qd, kd)[which], 0, b * H + hf * (H // KD), H // KD, 0)
                sp.wait_ge(rows_ready, 1)
                sp.dma_start(q_extra, rows_b[:, 0:CAUSAL, :]).then_inc(rows_stored, 16)
                sp.dma_start(k_extra, rows_b[:, CAUSAL:, :]).then_inc(rows_stored, 16)
                sp.wait_ge(rows_stored, 32)
                for i in range(SPLIT_SLOTS):
                    sp.wait_ge(split.stored[i], B * 16)

            @block.tensor
            def _(pe):
                mm = nc.tensor.matmul
                pe.wait_ge(loaded, 48)
                with pe.Fori(0, B) as b:
                    for n, (which, hf) in enumerate(items):
                        pe.wait_ge(split.t_ready[n], b)
                        for k in range(KD):
                            last = mm(banks[n][:], w[:, k, which * D + hf * P:which * D + (hf + 1) * P], XT[:, k, ds(b * S, S)],
                                      start=(k == 0), stop=(k == KD - 1))
                        last.then_inc(product[n], 1)
                for t in range(NT):
                    if t >= 2:
                        pe.wait_ge(v_copied, t - 1)
                    for k in range(KD):
                        last = mm(v_ps[t % 2][:], XT[:, k, t * P:(t + 1) * P], w[:, k, 2 * D:3 * D], start=(k == 0), stop=(k == KD - 1))
                    last.then_inc(v_product, 1)

            @block.scalar
            def _(act):
                with act.Fori(0, B) as b:
                    for pair in pairs(b):
                        split.scalar(act, pair)

            @block.gpsimd
            def _(pool):
                nc.gpsimd.memset(V[:], 1.0).then_inc(ones_ready, 1)
                with pool.Fori(0, B) as b:
                    for pair in pairs(b):
                        split.pool(pool, pair)

            @block.vector
            def _(dve):
                v = nc.vector
                dve.wait_ge(loaded, 48)
                v.tensor_copy(idents[0][:], ident[:]).then_inc(cast_ready, 1)
                v.tensor_copy(idents[1][:], ident[:]).then_inc(cast_ready, 1)
                v.tensor_copy(tri[:], tri_f[:]).then_inc(cast_ready, 1)
                v.tensor_copy(rows_b[:], rows_f[:]).then_inc(rows_ready, 1)
                with dve.Fori(0, B) as b:
                    for n, (which, hf) in enumerate(items):
                        split.before_t(dve, n, b)
                        dve.wait_ge(product[n], b + 1)
                        v.tensor_scalar(split.t[:, n, :], banks[n][:], 0.25 if which == 0 else 1.0, None, ALU.mult).then_inc(split.t_ready[n], 1)
                dve.wait_ge(ones_ready, 1)
                for t in range(NT):
                    b, kt = divmod(t, TPB)
                    dve.wait_ge(v_product, t + 1)
                    v.tensor_copy(V[:, kt, b * H * VW:(b + 1) * H * VW].rearrange("p (h v) -> p h v", v=VW)[:, :, 0:DH],
                                  v_ps[t % 2][:].rearrange("p (h d) -> p h d", d=DH)).then_inc(v_copied, 1)

    with ExitStack() as own:
        run_heads(nc, Heads(own, nc, "Dh", S, CAUSAL, (q_extra, k_extra), True, qd, kd, V, ATT, idents, tri, dram["strip_sum"], SELF_SLOTS, 3,
                            "scores max scores last max turn max scores scores max token", 1, 4, 2))
    with ExitStack() as own:
        project_out(nc, own, "Do", X, XT, ATT, ident, dram["self_WoT"], None)


def phase_cross1(nc, ctx, dram, X, XT, ident):
    KC = 4
    kw = -(-S2 // KC)
    chunks = [(c * kw, min(kw, S2 - c * kw)) for c in range(KC)]
    qd = nc.dram_tensor("E_qd", (2 * PARTS, UNITS, DH // 2, S), BF16, kind="Internal").ap()
    kd = nc.dram_tensor("E_kd", (2 * PARTS, UNITS, DH // 2, S2), BF16, kind="Internal").ap()
    mask_rows = nc.dram_tensor("E_mask_rows", (UNITS, S2), BF16, kind="Internal").ap()
    V = ctx.enter_context(nc.sbuf_tensor("E_V", [P, NK2, UNITS * VW], F32))
    idents = narrow_identities(nc, ctx, "E")
    with ExitStack() as own:
        sb = lambda n, s, dt=F32: own.enter_context(nc.sbuf_tensor(f"E_{n}", s, dt))
        sem = lambda n: own.enter_context(nc.semaphore(f"E_{n}"))
        wq, wk, wv = (sb(n, [P, KD, D]) for n in ("wq", "wk", "wv"))
        bq, bk = (sb(n, [P, 2]) for n in ("bq", "bk"))
        bv = sb("bv", [P, D])
        rotary = sb("rotary", [P, 4, S2])
        mask = sb("mask", [P, S2], I32)
        keep = sb("keep", [P, 2, S2], BF16)
        ctxT = sb("ctxT", [P, 2, KD, S2])
        mask_row = sb("mask_row", [H, 2, S2], BF16)
        other = sb("other", [P, 2, S])
        pair_ps = [[own.enter_context(nc.psum_tensor(f"E_pair{i}{j}", [P, S], F32)) for j in range(2)] for i in range(2)]
        v_ps = [own.enter_context(nc.psum_tensor(f"E_v{i}", [P, D], F32)) for i in range(4)]
        split = Split(own, nc, "E_split")
        loaded, mask_loaded = sem("loaded"), sem("mask_loaded")
        ctx_loaded = [sem(f"ctx_loaded{u}") for u in range(2)]
        row_ready, row_stored = sem("row_ready"), sem("row_stored")
        v_ones, cast_ready = sem("v_ones"), sem("cast_ready")
        keep_ready = sem("keep_ready")
        product, rotated, summed = ([sem(f"{n}{i}") for i in range(2)] for n in ("product", "rotated", "summed"))
        v_product, v_copied, keys_done = sem("v_product"), sem("v_copied"), sem("keys_done")
        v_tiles = [range(0)] + [range(c * NK2 // KC, (c + 1) * NK2 // KC) for c in range(KC - 1)]
        v_tiles[-1] = range(v_tiles[-1].start, NK2)

        def pairs(eng, query, key, batch=None):
            with eng.Fori(0, B // 2) as bb:
                for u in range(2):
                    query(bb * 2 + u, u, bb)
            with eng.Fori(0, B // 2) as bb:
                for u in range(2):
                    b = bb * 2 + u
                    if batch:
                        batch(b, u, bb)
                    for c in range(KC):
                        key(b, u, c % 2, b * (KC // 2) + (B // 2 + c // 2), c)

        both = lambda pair, turn, query, w: [(2 * pair + m, turn, query, w) for m in range(2)]

        with nc.Block() as block:
            @block.sync
            def _(sp):
                for t, n in ((wq, "wqT"), (wk, "wkT"), (wv, "wvT")):
                    sp.dma_start(t[:], dram[n].rearrange("(k p) e -> p k e", p=P)).then_inc(loaded, 16)
                for t, n in ((bq, "bq"), (bk, "bk"), (rotary, "rotary")):
                    sp.dma_start(t[:], dram[n]).then_inc(loaded, 16)
                sp.dma_start(bv[:], dram["bv"].partition_broadcast(P)).then_inc(loaded, 16)

                def load_context(b, u):
                    sp.dma_start(ctxT[:, u], dram["ctxT"][ds(b, 1)].rearrange("b (k p) s -> p (b k) s", p=P)).then_inc(ctx_loaded[u], 16)

                def load_mask(b):
                    sp.dma_start(mask[:], dram["mask"][ds(b, 1)].rearrange("b r s -> (b r) s")).then_inc(mask_loaded, 16)

                for u in range(2):
                    load_context(u, u)
                load_mask(0)

                def query(b, u, turn):
                    for m in range(2):
                        split.sync(sp, 2 * u + m, turn, S, qd, m, b * H, H, 0)

                def key(b, u, slot, turn, c):
                    c0, w = chunks[c]
                    for m in range(2):
                        split.sync(sp, 2 * slot + m, turn, w, kd, m, b * H, H, c0)

                with sp.Fori(0, B // 2) as bb:
                    for u in range(2):
                        query(bb * 2 + u, u, bb)
                for b in range(B):
                    sp.wait_ge(row_ready, b + 1)
                    sp.dma_start(mask_rows[b * H:(b + 1) * H], mask_row[:, b % 2]).then_inc(row_stored, 16)
                    if b + 1 < B:
                        load_mask(b + 1)
                    for c in range(KC):
                        key(b, b % 2, c % 2, b * (KC // 2) + (B // 2 + c // 2), c)
                    if b + 2 < B:
                        sp.wait_ge(keys_done, b + 1)
                        load_context(b + 2, b % 2)
                sp.wait_ge(row_stored, 16 * B)
                for i in range(SPLIT_SLOTS):
                    sp.wait_ge(split.stored[i], (B // 2 + B * KC // 2) * 16)

            @block.tensor
            def _(pe):
                mm = nc.tensor.matmul

                def project(slot, turn, weights, rhs, w):
                    pe.wait_ge(rotated[slot], turn)
                    for m in range(2):
                        for k in range(KD):
                            last = mm(pair_ps[slot][m][:, 0:w], weights[:, k, m * P:(m + 1) * P], rhs(k), start=(k == 0), stop=(k == KD - 1))
                    last.then_inc(product[slot], 1)

                def query(b, u, turn):
                    project(u, turn, wq, lambda k: XT[:, k, ds(b * S, S)], S)

                def batch(b, u, bb):
                    pe.wait_ge(ctx_loaded[u], bb * 16 + 16)

                def key(b, u, slot, turn, c):
                    c0, w = chunks[c]
                    project(slot, turn, wk, lambda k: ctxT[:, u, k, c0:c0 + w], w)
                    for kt in v_tiles[c]:
                        r = key_rows(kt)
                        bank = kt % 4
                        pe.wait_ge(v_copied, b * NK2 + (kt - 3 if kt >= 4 else 0))
                        for k in range(KD):
                            last = mm(v_ps[bank][0:r, :], ctxT[:, u, k, kt * P:kt * P + r], wv[:, k, :], start=(k == 0), stop=(k == KD - 1))
                        last.then_inc(v_product, 1)
                    if c == KC - 1:
                        pe.wait_ge(v_copied, (b + 1) * NK2)
                        pe.sem_inc(keys_done, 1)

                pe.wait_ge(loaded, 7 * 16)
                pairs(pe, query, key, batch)

            @block.scalar
            def _(act):
                pairs(act, lambda b, u, turn: split.scalar(act, both(u, turn, True, S)),
                      lambda b, u, slot, turn, c: split.scalar(act, both(slot, turn, False, chunks[c][1])))

            @block.gpsimd
            def _(pool):
                nc.gpsimd.memset(V[:], 1.0).then_inc(v_ones, 1)
                pairs(pool, lambda b, u, turn: split.pool(pool, both(u, turn, True, S)),
                      lambda b, u, slot, turn, c: split.pool(pool, both(slot, turn, False, chunks[c][1])))

            @block.vector
            def _(dve):
                v = nc.vector
                dve.wait_ge(loaded, 7 * 16)
                v.tensor_copy(idents[0][:], ident[:]).then_inc(cast_ready, 1)
                v.tensor_copy(idents[1][:], ident[:]).then_inc(cast_ready, 1)

                def rotate(slot, turn, bias, c0, w, finish):
                    for m in range(2):
                        split.before_t(dve, 2 * slot + m, turn)
                    dve.wait_ge(product[slot], turn + 1)
                    for m in range(2):
                        v.scalar_tensor_tensor(split.t[:, 2 * slot + m, 0:w], pair_ps[slot][m][:, 0:w], bias[:, m:m + 1],
                                               rotary[:, 2 * m, c0:c0 + w], ALU.add, ALU.mult)
                        last = v.scalar_tensor_tensor(other[:, m, 0:w], pair_ps[slot][1 - m][:, 0:w], bias[:, 1 - m:2 - m],
                                                      rotary[:, 2 * m + 1, c0:c0 + w], ALU.add, ALU.mult)
                    last.then_inc(rotated[slot], 1)
                    dve.wait_ge(rotated[slot], turn + 1)
                    both_t = split.t[:, 2 * slot:2 * slot + 2, 0:w]
                    v.tensor_tensor(both_t, both_t, other[:, :, 0:w], ALU.add).then_inc(summed[slot], 1)
                    dve.wait_ge(summed[slot], turn + 1)
                    for m in range(2):
                        finish(split.t[:, 2 * slot + m, 0:w]).then_inc(split.t_ready[2 * slot + m], 1)

                def query(b, u, turn):
                    rotate(u, turn, bq, 0, S, lambda t: v.tensor_scalar(t, t, 0.25, None, ALU.mult))

                def mask_of(b, u):
                    dve.wait_ge(mask_loaded, b * 16 + 16)
                    v.tensor_scalar(keep[:, u], mask[:], 0.0, None, ALU.not_equal).then_inc(keep_ready, 1)
                    dve.wait_ge(keep_ready, b + 1)
                    v.tensor_scalar(mask_row[:, u], keep[0:H, u], 1.0, -NEG, ALU.subtract, ALU.mult).then_inc(row_ready, 1)

                def key(b, u, slot, turn, c):
                    c0, w = chunks[c]
                    rotate(slot, turn, bk, c0, w, lambda t: v.tensor_tensor(t, t, keep[:, u, c0:c0 + w], ALU.mult))
                    for kt in v_tiles[c]:
                        r = key_rows(kt)
                        dve.wait_ge(v_product, b * NK2 + kt + 1)
                        v.tensor_tensor(V[0:r, kt, ds(b * H * VW, H * VW)].rearrange("p (h v) -> p h v", v=VW)[:, :, 0:DH],
                                        v_ps[kt % 4][0:r, :].rearrange("p (h d) -> p h d", d=DH),
                                        bv[0:r, :].rearrange("p (h d) -> p h d", d=DH), ALU.add).then_inc(v_copied, 1)

                mask_of(0, 0)
                dve.wait_ge(v_ones, 1)
                with dve.Fori(0, B // 2) as bb:
                    for u in range(2):
                        query(bb * 2 + u, u, bb)
                for b in range(B):
                    for c in range(KC):
                        key(b, b % 2, c % 2, b * (KC // 2) + (B // 2 + c // 2), c)
                        if c == 1 and b + 1 < B:
                            if b >= 1:
                                dve.wait_ge(row_stored, b * 16)
                            mask_of(b + 1, (b + 1) % 2)

    ATT = ctx.enter_context(nc.sbuf_tensor("E_ATT", [P, TPB, UNITS * DH], F32))
    with ExitStack() as own:
        run_heads(nc, Heads(own, nc, "Eh", S2, 1, mask_rows, False, qd, kd, V, ATT, idents, None, dram["strip_sum"], 4, 2,
                            "scores scores last max scores max scores max turn scores max scores max scores max "
                            "values max scores max token max scores max scores max values max scores max scores max scores max max values", 3, 3, 3))
    with ExitStack() as own:
        project_out(nc, own, "Eo", X, XT, ATT, ident, dram["cross_WoT"], dram["bo"])


def phase_ffn(nc, ctx, dram, X, XT, ident, out):
    sb = lambda n, s, dt=F32: ctx.enter_context(nc.sbuf_tensor(f"F_{n}", s, dt))
    ps = lambda n, s: ctx.enter_context(nc.psum_tensor(f"F_{n}", s, F32))
    sem = lambda n: ctx.enter_context(nc.semaphore(f"F_{n}"))

    q1, s1, w1 = sb("q1", [P, KD, F], I32), sb("s1", [P, KD, F]), sb("w1", [P, KD, F])
    q2, s2, w2 = sb("q2", [P, NF, D], I32), sb("s2", [P, NF, D]), sb("w2", [P, NF, D])
    b1, b2 = sb("b1", [P, NF]), sb("b2", [P, D])
    gamma, beta = sb("gamma", [P, KD]), sb("beta", [P, KD])
    XN = sb("XN", [P, NT, D])
    HT = sb("HT", [P, KD, T])
    sig = sb("sig", [P, 2, S])
    act_T = sb("act_T", [P, NF, S])
    turn_ps = [ps(f"turn{h}", [P, S]) for h in range(KD)]
    y1_ps = [ps(f"y1_{i}", [P, S]) for i in range(2)]
    y2_ps = [ps(f"y2_{i}", [P, D]) for i in range(2)]

    norm_in = Norm(ctx, nc, "F_in", X, 1e-5)
    norm_out = Norm(ctx, nc, "F_out", X, LN_EPS)
    loaded1, loaded2, loaded_small = sem("loaded1"), sem("loaded2"), sem("loaded_small")
    w_ready = sem("w_ready")
    turned, copied = sem("turned"), sem("copied")
    y1_ready, sig_ready, act_ready = sem("y1_ready"), sem("sig_ready"), sem("act_ready")
    y2_ready, sum_ready, xb_ready = sem("y2_ready"), sem("sum_ready"), sem("xb_ready")
    half_b2 = sem("half_b2")
    stored = sem("stored")

    with nc.Block() as block:
        @block.sync
        def _(sp):
            sp.dma_start(gamma[:], dram["L1_ffn_ln_gamma"]).then_inc(loaded_small, 16)
            sp.dma_start(beta[:], dram["L1_ffn_ln_beta"]).then_inc(loaded_small, 16)
            sp.dma_start(b1[:], dram["L1_ffn_fc1_bias"]).then_inc(loaded_small, 16)
            sp.dma_start(b2[:], dram["L1_ffn_fc2_bias"].partition_broadcast(P)).then_inc(loaded_small, 16)
            sp.dma_start(q1[:], dram["L1_ffn_fc1_q"].rearrange("(k p) f -> p k f", p=P)).then_inc(loaded1, 16)
            sp.dma_start(s1[:], dram["L1_ffn_fc1_scales"].partition_broadcast(P)).then_inc(loaded1, 16)
            sp.dma_start(q2[:], dram["L1_ffn_fc2_q"].rearrange("(k p) f -> p k f", p=P)).then_inc(loaded2, 16)
            sp.dma_start(s2[:], dram["L1_ffn_fc2_scales"].partition_broadcast(P)).then_inc(loaded2, 16)
            for c in range(B):
                sp.wait_ge(norm_out.normed, (c + 1) * TPB)
                sp.dma_start(out[c * S:(c + 1) * S, :].rearrange("(t p) d -> p t d", p=P),
                             X[:, c * TPB:(c + 1) * TPB, :]).then_inc(stored, 16)
            sp.wait_ge(stored, 16 * B)

        @block.gpsimd
        def _(pool):
            norm_in.setup(pool)
            norm_out.setup(pool)
            for c in range(B):
                norm_in.inverse_deviation(pool, c)
            for c in range(B):
                norm_out.inverse_deviation(pool, c)

        @block.scalar
        def _(act):
            act.wait_ge(loaded_small, 64)
            for c in range(B):
                for h in range(KD):
                    act.wait_ge(turned, KD * c + h + 1)
                    nc.scalar.activation(HT[:, h, c * S:(c + 1) * S], turn_ps[h][:], ACT.Identity,
                                         bias=beta[:, h:h + 1], scale=gamma[:, h:h + 1]).then_inc(copied, 1)
            with act.Fori(0, B) as c:
                for j in range(NF):
                    n = c * NF + j
                    act.wait_ge(y1_ready, n + 1)
                    if j >= 2:
                        act.wait_ge(act_ready, n - 1)
                    nc.scalar.activation(sig[:, j % 2, :], y1_ps[j % 2][:], ACT.Sigmoid,
                                         bias=b1[:, j:j + 1]).then_inc(sig_ready, 1)

        @block.vector
        def _(dve):
            for c in range(B):
                for t in range(c * TPB, (c + 1) * TPB):
                    nc.vector.bn_stats(norm_in.stats_buf[:, t, :], X[:, t, :]).then_inc(norm_in.stats_ready, 1)
                for t in range(c * TPB, (c + 1) * TPB):
                    dve.wait_ge(norm_in.stats_ready, t + 1)
                    nc.vector.bn_aggr(norm_in.mv[:, t, :], norm_in.stats_buf[:, t, :]).then_inc(norm_in.mv_ready, 1)
            for c in range(B):
                norm_in.normalize(dve, c, XN)
            dve.wait_ge(loaded1, 32)
            nc.vector.scalar_tensor_tensor(w1[:].rearrange("p k f -> p (k f)"), q1[:].rearrange("p k f -> p (k f)"), -128.0, s1[:].rearrange("p k f -> p (k f)"), ALU.add, ALU.mult).then_inc(w_ready, 1)
            dve.wait_ge(loaded2, 32)
            nc.vector.scalar_tensor_tensor(w2[:].rearrange("p k f -> p (k f)"), q2[:].rearrange("p k f -> p (k f)"), -128.0, s2[:].rearrange("p k f -> p (k f)"), ALU.add, ALU.mult).then_inc(w_ready, 1)
            dve.wait_ge(loaded_small, 64)
            nc.vector.tensor_scalar(b2[:], b2[:], 0.5, None, ALU.mult).then_inc(half_b2, 1)
            dve.wait_ge(half_b2, 1)
            for t in range(NT):
                nc.vector.scalar_tensor_tensor(X[:, t, :], X[:, t, :], 2.0, b2[:], ALU.mult, ALU.add).then_inc(xb_ready, 1)
            dve.wait_ge(xb_ready, NT)
            with dve.Fori(0, B) as c:
                for j in range(NF):
                    n = c * NF + j
                    dve.wait_ge(sig_ready, n + 1)
                    nc.vector.scalar_tensor_tensor(act_T[:, j, :], y1_ps[j % 2][:], b1[:, j:j + 1], sig[:, j % 2, :],
                                                   ALU.add, ALU.mult).then_inc(act_ready, 1)
                for t in range(TPB):
                    n = c * TPB + t
                    dve.wait_ge(y2_ready, n + 1)
                    x = X[:, ds(n, 1), :].rearrange("p a d -> p (a d)")
                    nc.vector.scalar_tensor_tensor(x, y2_ps[t % 2][:], 0.5, x, ALU.mult, ALU.add).then_inc(sum_ready, 1)
            norm_out.finish(dve, sum_ready)

        @block.tensor
        def _(pe):
            for c in range(B):
                turn_group(nc, pe, XN, ident[:], turn_ps, c, norm_in.normed, copied, turned)
            pe.wait_ge(copied, KD * B)
            pe.wait_ge(w_ready, 1)
            with pe.Fori(0, B) as c:
                for j in range(NF):
                    n = c * NF + j
                    if j >= 2:
                        pe.wait_ge(act_ready, n - 1)
                    for k in range(KD):
                        last = nc.tensor.matmul(y1_ps[j % 2][:], w1[:, k, j * P:(j + 1) * P], HT[:, k, ds(c * S, S)],
                                                start=(k == 0), stop=(k == KD - 1))
                    last.then_inc(y1_ready, 1)
                pe.wait_ge(act_ready, (c + 1) * NF)
                pe.wait_ge(w_ready, 2)
                for t in range(TPB):
                    n = c * TPB + t
                    if t >= 2:
                        pe.wait_ge(sum_ready, n - 1)
                    for j in range(NF):
                        last = nc.tensor.matmul(y2_ps[t % 2][:], act_T[:, j, t * P:(t + 1) * P], w2[:, j, :],
                                                start=(j == 0), stop=(j == NF - 1))
                    last.then_inc(y2_ready, 1)
                pe.wait_ge(sum_ready, (c + 1) * TPB)


def lay_out(a, columns):
    x = a["x"].reshape(T, D)
    i, j = np.meshgrid(np.arange(P), np.arange(P))
    quadrant = [((i >> m + 1) == (j >> m + 1)) & ((i >> m) % 2 == 1) & ((j >> m) % 2 == 0) for m in range(LEVELS)]
    ttt_masks = np.stack([q.astype(np.float32) for q in quadrant] + [quadrant[0].T.astype(np.float32),
                         np.where(j <= i, -ETA, 0.0).astype(np.float32)], axis=1)
    causal_tri = np.where(np.stack([i > j, j > i], axis=1), -10000.0, 0.0).astype(np.float32)
    block = np.arange(S) // P
    q_rows = [(block == t) * 1.0 for t in range(TPB - 1) for _ in range(2)]
    k_rows = [(block > t) * v for t in range(TPB - 1) for v in (-9984.0, -16.0)] + [np.ones(S)] * 2
    causal_rows = np.tile(np.array(q_rows + k_rows, np.float32), (SELF_SLOTS, 1, 1))
    pairs = np.concatenate([np.arange(0, D, 2), np.arange(1, D, 2)])
    inv_freq = (1.0 / 10000.0 ** (np.arange(0, DH, 2, dtype=np.float32) / np.float32(DH))).astype(np.float32)
    angle = (np.arange(S2, dtype=np.float32)[None, :] * np.concatenate([inv_freq, inv_freq])[:, None]).astype(np.float64)
    even, odd = np.tile(angle[0::2], (H, 1)), np.tile(angle[1::2], (H, 1))
    rotary = np.stack([np.cos(even), -np.sin(even), np.cos(odd), np.sin(odd)], axis=1).astype(np.float32)
    laid = {
        "ttt_masks": ttt_masks,
        "L0_xattn_W1": a["L0_xattn_W1"], "xW2T": a["L0_xattn_W2"].T,
        "L0_xattn_b1": columns(a["L0_xattn_b1"]), "L0_xattn_b2": columns(a["L0_xattn_b2"]),
        "ctx": a["ctx_1024"], "ctxT": a["ctx_1024"].transpose(0, 2, 1), "fside": a["fside_1xSxS2_0"][0],
        "L0_ffn_Wr": a["L0_ffn_Wr"].reshape(KD, P, E).transpose(1, 0, 2), "L0_ffn_br": np.tile(a["L0_ffn_br"], (P, 1)),
        "lanes": np.tile(np.arange(E, dtype=np.float32), (P, 1)),
        "L0_ffn_bi": a["L0_ffn_bi"].reshape(E, NF, P).transpose(2, 0, 1),
        "L0_ffn_bg": a["L0_ffn_bg"].reshape(E, NF, P).transpose(2, 0, 1),
        "L0_ffn_Wi": a["L0_ffn_Wi"], "L0_ffn_Wg": a["L0_ffn_Wg"], "L0_ffn_Wo": a["L0_ffn_Wo"],
        "expert_tail": np.tile(np.stack([a["L0_ffn_bo"], a["L0_ffn_gamma"], a["L0_ffn_beta"]], axis=1), (P, 1, 1, 1)),
        "wqkvT": a["L1_attn_w_qkv"].T, "self_WoT": a["L1_attn_w_out"].T,
        "causal_tri": causal_tri, "causal_rows": causal_rows,
        "wqT": a["L1_xattn_Wq"].T[:, pairs], "wkT": a["L1_xattn_Wk"].T[:, pairs], "wvT": a["L1_xattn_Wv"].T,
        "bq": columns(a["L1_xattn_bq"][pairs]), "bk": columns(a["L1_xattn_bk"][pairs]),
        "bv": a["L1_xattn_bv"], "bo": a["L1_xattn_bo"], "cross_WoT": a["L1_xattn_Wo"].T, "rotary": rotary,
        "mask": np.repeat(a["mask_BxS2_if1"][:, None, :], P, axis=1),
        "thKT": a["L0_attn_theta_K"].T, "thQT": a["L0_attn_theta_Q"].T, "thVT": a["L0_attn_theta_V"].T,
        "L0_attn_theta_K": a["L0_attn_theta_K"], "L0_attn_theta_Q": a["L0_attn_theta_Q"],
        "W0T": a["L0_attn_W0"].T, "L0_attn_b0": a["L0_attn_b0"],
        "strip_sum": np.tile(np.eye(STRIP, VW, dtype=np.float32), (STRIPS, 1)),
        "identity": np.eye(P, dtype=np.float32),
        "x": x,
        "xT": x.T,
        "L1_ffn_ln_gamma": columns(a["L1_ffn_ln_gamma"]),
        "L1_ffn_ln_beta": columns(a["L1_ffn_ln_beta"]),
        "L1_ffn_fc1_q": a["L1_ffn_fc1_q"],
        "L1_ffn_fc1_scales": a["L1_ffn_fc1_scales"],
        "L1_ffn_fc1_bias": columns(a["L1_ffn_fc1_bias"]),
        "L1_ffn_fc2_q": a["L1_ffn_fc2_q"],
        "L1_ffn_fc2_scales": a["L1_ffn_fc2_scales"],
        "L1_ffn_fc2_bias": a["L1_ffn_fc2_bias"],
    }
    return laid


def renew_semaphores(nc):
    released = nc.released_uncleared_semaphores
    nc.all_engine_barrier(sems_to_clear=range(min(released), max(released) + 1))


def build_program(nc, dram, out):
    with ExitStack() as ctx:
        X = ctx.enter_context(nc.sbuf_tensor("X", [P, NT, D], F32))
        XT = ctx.enter_context(nc.sbuf_tensor("XT", [P, KD, T], F32))
        ident = ctx.enter_context(nc.sbuf_tensor("ident", [P, P], F32))
        for phase in (phase_ttt, phase_cross0, phase_moe, phase_self, phase_cross1):
            with ExitStack() as own:
                phase(nc, own, dram, X, XT, ident)
            renew_semaphores(nc)
        with ExitStack() as own:
            phase_ffn(nc, own, dram, X, XT, ident, out)


def kernel(**inputs):
    import concourse.bacc as bacc
    from concourse.bass_utils import run_bass_kernel_spmd

    a = {k: np.asarray(v) for k, v in inputs.items()}
    columns = lambda v: np.ascontiguousarray(v.reshape(-1, P).T)
    laid = lay_out(a, columns)
    nc = bacc.Bacc("TRN2", target_bir_lowering=False, num_devices=1)
    arrays, dram = {}, {}
    for name, v in laid.items():
        v = np.ascontiguousarray(v)
        arrays[f"in_{name}_dram"] = v
        dram[name] = nc.dram_tensor(f"in_{name}_dram", v.shape, mybir.dt.from_np(v.dtype), kind="ExternalInput").ap()
    out = nc.dram_tensor("out_0_dram", (T, D), F32, kind="ExternalOutput").ap()
    build_program(nc, dram, out)
    r = run_bass_kernel_spmd(nc, [arrays], core_ids=[0])
    return r.results[0]["out_0_dram"].reshape(B, S, D)
```
